# Optimizing a Trainium2 kernel written in Bass

```python
import numpy as np
import jax
import jax.numpy as jnp

def _softmax(x, axis=-1):
    return jax.nn.softmax(x, axis=axis)

def _gelu(x):
    return jax.nn.gelu(x, approximate=True)

def _silu(x):
    return jax.nn.silu(x)

def _sigmoid(x):
    return jax.nn.sigmoid(x)

def _layernorm(x, axis=-1, eps=1e-05):
    m = jnp.mean(x, axis=axis, keepdims=True)
    v = jnp.var(x, axis=axis, keepdims=True)
    return (x - m) / jnp.sqrt(v + eps)

def _scatter_add(tgt, idx, src, axis=0):
    return tgt.at[idx].add(src)

def _segment_sum(src, seg, n):
    return jax.ops.segment_sum(src, seg, n)
kernel_name = 'mk_seq_preln_d1_jaxref_r4_f330dc'

def setup_inputs(seed: int=0):
    np.random.seed(seed)
    _w = jnp.asarray

    def _L0_attn_setup():
        import math
        import jax, jax.numpy as jnp
        import numpy as np
        DIM = 256
        HID = 512
        QK = 128
        G = 64
        B, N = (4, 1024)
        NUM_BUCKETS = 32
        MAX_DIST = 128

        def _rel_pos_bias(rel_emb, g, scale):
            pos = jnp.arange(g)
            rel = pos[None, :] - pos[:, None]
            n = -rel
            nb = NUM_BUCKETS // 2
            ret = (n < 0).astype(jnp.int32) * nb
            n = jnp.abs(n)
            max_exact = nb // 2
            is_small = n < max_exact
            val_large = max_exact + (jnp.log(jnp.maximum(n, 1).astype(jnp.float32) / max_exact) / math.log(MAX_DIST / max_exact) * (nb - max_exact)).astype(jnp.int32)
            val_large = jnp.minimum(val_large, nb - 1)
            bucket = ret + jnp.where(is_small, n, val_large)
            return rel_emb[bucket, 0] * scale

        def _layernorm(x, g, b, eps=1e-05):
            mu = jnp.mean(x, axis=-1, keepdims=True)
            var = jnp.mean((x - mu) ** 2, axis=-1, keepdims=True)
            return (x - mu) * jax.lax.rsqrt(var + eps) * g + b
        key = jax.random.key(seed)
        ks = jax.random.split(key, 8)
        return {'x': jax.random.normal(ks[0], (B, N, DIM), dtype=jnp.float32), 'ln_g': jnp.ones((DIM,), jnp.float32), 'ln_b': jnp.zeros((DIM,), jnp.float32), 'W_h': jax.random.normal(ks[1], (DIM, 2 * HID), jnp.float32) * 0.02, 'b_h': jnp.zeros((2 * HID,), jnp.float32), 'W_qk': jax.random.normal(ks[2], (DIM, QK), jnp.float32) * 0.02, 'b_qk': jnp.zeros((QK,), jnp.float32), 'os_gamma': jax.random.normal(ks[3], (4, QK), jnp.float32) * 0.02, 'os_beta': jnp.zeros((4, QK), jnp.float32), 'rel_emb': jax.random.normal(ks[4], (NUM_BUCKETS, 1), jnp.float32) * 0.02, 'W_out': jax.random.normal(ks[5], (HID, DIM), jnp.float32) * 0.02, 'b_out': jnp.zeros((DIM,), jnp.float32)}
    _L0_attn_in = _L0_attn_setup()

    def _L0_ffn_setup():
        import jax, jax.numpy as jnp
        import numpy as np
        H = 256
        I = 1024
        E = 8
        K = 2
        B, S = (2, 512)

        def _moe_linear(x, router_w, expert_w):
            n_exp = router_w.shape[0]
            logits = x @ router_w.T
            vals, idx = jax.lax.top_k(logits, K)
            probs = jax.nn.softmax(vals, axis=-1)
            onehot = jax.nn.one_hot(idx, n_exp, dtype=x.dtype)
            combine = jnp.einsum('tk,tke->te', probs, onehot)
            out = jnp.zeros((x.shape[0], expert_w.shape[1]), x.dtype)
            for e in range(n_exp):
                out = out + combine[:, e:e + 1] * (x @ expert_w[e].T)
            return out
        key = jax.random.key(seed)
        ks = jax.random.split(key, 7)
        init = lambda k, shape, fan_in: jax.random.normal(k, shape, jnp.float32) / np.float32(np.sqrt(fan_in))
        return {'x': jax.random.normal(ks[0], (B, S, H), jnp.float32), 'router_gate': init(ks[1], (E, H), H), 'w_gate': init(ks[2], (E, I, H), H), 'router_up': init(ks[3], (E, H), H), 'w_up': init(ks[4], (E, I, H), H), 'router_down': init(ks[5], (E, I), I), 'w_down': init(ks[6], (E, H, I), I)}
    _L0_ffn_in = _L0_ffn_setup()
    _d = {'L0_attn_x': _L0_attn_in['x'], 'L0_attn_ln_g': _L0_attn_in['ln_g'], 'L0_attn_ln_b': _L0_attn_in['ln_b'], 'L0_attn_W_h': _L0_attn_in['W_h'], 'L0_attn_b_h': _L0_attn_in['b_h'], 'L0_attn_W_qk': _L0_attn_in['W_qk'], 'L0_attn_b_qk': _L0_attn_in['b_qk'], 'L0_attn_os_gamma': _L0_attn_in['os_gamma'], 'L0_attn_os_beta': _L0_attn_in['os_beta'], 'L0_attn_rel_emb': _L0_attn_in['rel_emb'], 'L0_attn_W_out': _L0_attn_in['W_out'], 'L0_attn_b_out': _L0_attn_in['b_out'], 'L0_ffn_router_gate': _L0_ffn_in['router_gate'], 'L0_ffn_w_gate': _L0_ffn_in['w_gate'], 'L0_ffn_router_up': _L0_ffn_in['router_up'], 'L0_ffn_w_up': _L0_ffn_in['w_up'], 'L0_ffn_router_down': _L0_ffn_in['router_down'], 'L0_ffn_w_down': _L0_ffn_in['w_down']}
    _x0 = _d['L0_attn_x']
    _d['L0_attn_x'] = jax.random.normal(jax.random.fold_in(jax.random.key(seed), 1), (1, 4096, 256), dtype=_x0.dtype)
    del _x0
    return _d

def reference(L0_attn_x, L0_attn_ln_g, L0_attn_ln_b, L0_attn_W_h, L0_attn_b_h, L0_attn_W_qk, L0_attn_b_qk, L0_attn_os_gamma, L0_attn_os_beta, L0_attn_rel_emb, L0_attn_W_out, L0_attn_b_out, L0_ffn_router_gate, L0_ffn_w_gate, L0_ffn_router_up, L0_ffn_w_up, L0_ffn_router_down, L0_ffn_w_down):

    def _L0_attn_ref(x, ln_g, ln_b, W_h, b_h, W_qk, b_qk, os_gamma, os_beta, rel_emb, W_out, b_out):
        import math
        import jax, jax.numpy as jnp
        import numpy as np
        DIM = 256
        HID = 512
        QK = 128
        G = 64
        B, N = (4, 1024)
        NUM_BUCKETS = 32
        MAX_DIST = 128

        def _rel_pos_bias(rel_emb, g, scale):
            pos = jnp.arange(g)
            rel = pos[None, :] - pos[:, None]
            n = -rel
            nb = NUM_BUCKETS // 2
            ret = (n < 0).astype(jnp.int32) * nb
            n = jnp.abs(n)
            max_exact = nb // 2
            is_small = n < max_exact
            val_large = max_exact + (jnp.log(jnp.maximum(n, 1).astype(jnp.float32) / max_exact) / math.log(MAX_DIST / max_exact) * (nb - max_exact)).astype(jnp.int32)
            val_large = jnp.minimum(val_large, nb - 1)
            bucket = ret + jnp.where(is_small, n, val_large)
            return rel_emb[bucket, 0] * scale

        def _layernorm(x, g, b, eps=1e-05):
            mu = jnp.mean(x, axis=-1, keepdims=True)
            var = jnp.mean((x - mu) ** 2, axis=-1, keepdims=True)
            return (x - mu) * jax.lax.rsqrt(var + eps) * g + b
        b, n = (x.shape[0], x.shape[1])
        ng = n // G
        normed = _layernorm(x, ln_g, ln_b)
        hid = jax.nn.silu(normed @ W_h + b_h)
        v, gate = (hid[..., :HID], hid[..., HID:])
        qk = jax.nn.silu(normed @ W_qk + b_qk)
        heads = qk[..., None, :] * os_gamma + os_beta
        quad_q, lin_q, quad_k, lin_k = [heads[..., h, :] for h in range(4)]

        def grp(t):
            return t.reshape(b, ng, G, t.shape[-1])
        quad_q, quad_k, lin_q, lin_k, vg = map(grp, (quad_q, quad_k, lin_q, lin_k, v))
        sim = jnp.einsum('bgid,bgjd->bgij', quad_q, quad_k) / G
        sim = sim + _rel_pos_bias(rel_emb, G, QK ** 0.5)
        attn = jax.nn.relu(sim) ** 2
        quad_out = jnp.einsum('bgij,bgje->bgie', attn, vg)
        lin_kv = jnp.einsum('bgnd,bgne->bde', lin_k, vg) / n
        lin_out = jnp.einsum('bde,bgnd->bgne', lin_kv, lin_q)
        out = (quad_out + lin_out).reshape(b, n, HID)
        out = gate * out
        return out @ W_out + b_out + x

    def _L0_ffn_ref(x, router_gate, w_gate, router_up, w_up, router_down, w_down):
        import jax, jax.numpy as jnp
        import numpy as np
        H = 256
        I = 1024
        E = 8
        K = 2
        B, S = (2, 512)

        def _moe_linear(x, router_w, expert_w):
            n_exp = router_w.shape[0]
            logits = x @ router_w.T
            vals, idx = jax.lax.top_k(logits, K)
            probs = jax.nn.softmax(vals, axis=-1)
            onehot = jax.nn.one_hot(idx, n_exp, dtype=x.dtype)
            combine = jnp.einsum('tk,tke->te', probs, onehot)
            out = jnp.zeros((x.shape[0], expert_w.shape[1]), x.dtype)
            for e in range(n_exp):
                out = out + combine[:, e:e + 1] * (x @ expert_w[e].T)
            return out
        b, s, h = x.shape
        xt = x.reshape(b * s, h)
        g = _moe_linear(xt, router_gate, w_gate)
        u = _moe_linear(xt, router_up, w_up)
        inter = jax.nn.silu(g) * u
        d = _moe_linear(inter, router_down, w_down)
        return d.reshape(b, s, h)
    x = L0_attn_x
    x = x + _L0_attn_ref(_layernorm(x, axis=-1), L0_attn_ln_g, L0_attn_ln_b, L0_attn_W_h, L0_attn_b_h, L0_attn_W_qk, L0_attn_b_qk, L0_attn_os_gamma, L0_attn_os_beta, L0_attn_rel_emb, L0_attn_W_out, L0_attn_b_out)
    x = x + _L0_ffn_ref(_layernorm(x, axis=-1), L0_ffn_router_gate, L0_ffn_w_gate, L0_ffn_router_up, L0_ffn_w_up, L0_ffn_router_down, L0_ffn_w_down)
    return x

_drawn_inputs = setup_inputs


def setup_inputs(seed=0):
    import zlib

    import numpy as np

    out = dict(_drawn_inputs(seed))
    spreads = {'L0_attn_ln_g': (1.0, 0.6),
     'L0_attn_ln_b': (0.0, 0.8),
     'L0_attn_b_h': (0.0, 0.8),
     'L0_attn_b_qk': (0.0, 0.8),
     'L0_attn_os_beta': (0.0, 0.8),
     'L0_attn_b_out': (0.0, 0.8)}
    factors = {'L0_attn_W_h': 7.134,
     'L0_attn_W_qk': 8.0,
     'L0_attn_os_gamma': 8.0,
     'L0_attn_rel_emb': 5.486,
     'L0_attn_W_out': 6.309,
     'L0_ffn_router_gate': 8.0,
     'L0_ffn_w_gate': 8.0,
     'L0_ffn_router_up': 8.0,
     'L0_ffn_w_up': 8.0,
     'L0_ffn_router_down': 8.0,
     'L0_ffn_w_down': 8.0}
    for name, (base, spread) in spreads.items():
        noise = np.random.default_rng([zlib.crc32(name.encode()), seed]).standard_normal(out[name].shape)
        drawn = base * np.exp(spread * noise) if base else spread * noise
        out[name] = jnp.asarray(drawn.astype(out[name].dtype))
    for name, factor in factors.items():
        out[name] = (out[name] * factor).astype(out[name].dtype)
    return out
```

```python
from contextlib import ExitStack

import numpy as np

import concourse.bass as bass
from concourse import mybir

F32 = mybir.dt.float32
I32 = mybir.dt.int32
U32 = mybir.dt.uint32
ALU = mybir.AluOpType
ACT = mybir.ActivationFunctionType
AX = mybir.AxisListType
ds = bass.ds

P = 128
TOK = 4096
D = 256
HID = 512
G = 64
E = 8
INNER = 1024
T = TOK // P
KD = D // P
KI = INNER // P
KH = HID // P
SUB = 4
M = T // SUB
MT = SUB * P
NT = 2 * T + E
EPS = 1e-5
BUCKETS = 32
SIM_SCALE = 1.0 / G
BIAS_SCALE = float(P) ** 0.5
OFF_GROUP = -1.0e30


class Steps:

    def __init__(self):
        self.base, self.n = 0, 0

    def next(self):
        self.n += 1
        return self.base + self.n

    def enter(self, turn, per):
        self.outer, self.per = self.base + self.n, per
        self.base, self.n = turn * per + self.outer, 0

    def leave(self, turns):
        assert self.n == self.per, (self.n, self.per)
        self.base, self.n = self.outer + turns * self.per, 0


class Signal:

    def __init__(self, ctx, nc, name, credits=0):
        self.sem, self.credits = ctx.enter_context(nc.semaphore(name)), credits

    def after(self, n):
        return n + (1 + self.credits)

    def room(self, n):
        return n + 1

    def landed(self, turn, each=16):
        return turn * each + (each + self.credits)

    def sent(self, turn):
        return turn * 16 + 16


def block_kernel(nc, x_in, ln_g, ln_b, w_h, bh_value, bh_gate, w_qk, b_qk, os_gamma, os_beta, rel_emb, w_out,
                 b_out, r_gate, w_gate, r_up, w_up, r_down, w_down, bucket_in, out):
    with ExitStack() as ctx:
        def sb(name, shape, dt=F32):
            return ctx.enter_context(nc.sbuf_tensor(name, shape, dt))

        def sig(name, credits=0):
            return Signal(ctx, nc, name, credits)

        def dram(name, shape):
            return nc.dram_tensor(name, shape, F32, kind="Internal").ap()

        ROUTES = ("gate", "up", "down")

        gate_d = dram("gate_d", [M * P, KH * MT])
        v_d = dram("v_d", [M * P, SUB * HID])
        x2_d = dram("x2_d", [TOK, D])
        inter_d = dram("inter_d", [TOK, INNER])
        sorted_d = {"gate": dram("gate_sorted", [NT * P, INNER]), "up": dram("up_sorted", [NT * P, INNER]),
                    "down": dram("down_sorted", [NT * P, D])}

        bank = [ctx.enter_context(nc.psum_tensor(f"bank{i}", [P, 512], F32)) for i in range(8)]

        x_sb = sb("x_sb", [P, T, D])
        ident = sb("ident", [P, P])
        before = sb("before", [P, P])
        ones = sb("ones", [P, P])
        zeros = sb("zeros", [P, P])
        iota = sb("iota", [P, P])
        iota_i = sb("iota_i", [P, P], I32)
        token_i = sb("token_i", [P, T], I32)
        token_f = sb("token_f", [P, T])
        mean, var, rstd, rstd12 = (sb(n, [P, T]) for n in ("mean", "var", "rstd", "rstd12"))
        root_in, root, corr = (sb(n, [P, T]) for n in ("root_in", "root", "corr"))
        stats = sb("stats", [P, SUB, 6])
        mv = sb("mv", [P, SUB, 2])
        g_col, b_col = sb("g_col", [P, KD]), sb("b_col", [P, KD])
        bqk_col, bgate_col = sb("bqk_col", [P, 1]), sb("bgate_col", [P, KH])
        gamma_col, beta_col = sb("gamma_col", [P, 4]), sb("beta_col", [P, 4])
        rt_sb = sb("rt_sb", [P, KD, 2 * E])
        rd_sb = sb("rd_sb", [P, KI, E])
        top_v = sb("top_v", [P, 3, 2, T])
        top_i = sb("top_i", [P, 3, 2, T])
        comb = {r: sb(f"comb_{r}", [P, 2, T]) for r in ROUTES}
        pos = {r: sb(f"pos_{r}", [P, 2, T], I32) for r in ROUTES}
        ids = {r: sb(f"ids_{r}", [P, NT], I32) for r in ROUTES}
        expert_of = {r: sb(f"expert_{r}", [1, NT], I32) for r in ROUTES}
        lg = sb("lg", [P, SUB, 2, E])
        mx = sb("mx", [P, SUB, 2, 8])
        mi = sb("mi", [P, SUB, 2, 8], U32)
        idx_s = [sb(f"idx_s{b}", [P, 4], I32) for b in range(4)]
        oh = sb("oh", [P, 2, E, T])
        occ, keep, tot, incl, rank, full = (sb(n, [P, E, T]) for n in ("occ", "keep", "tot", "incl", "rank", "full"))
        tiles_e, end_e, base_e, ones_e, load_e = (sb(n, [P, E]) for n in ("tiles_e", "end_e", "base_e", "ones_e",
                                                                        "load_e"))
        pos_f, pa_f, pb_f = (sb(n, [P, 2, T]) for n in ("pos_f", "pa_f", "pb_f"))
        pa_i, pb_i = sb("pa_i", [P, 2, T], I32), sb("pb_i", [P, 2, T], I32)
        ends = sb("ends", [1, NT, E])
        ex_f = sb("ex_f", [1, NT])
        row_oh = [sb(f"row_oh{b}", [P, 2, P]) for b in range(2)]
        tile_id = [sb(f"tile_id{b}", [P, 2, NT]) for b in range(2)]

        WORDS = 32800
        arena = sb("arena", [P, WORDS])
        used = [0]

        def cut(*shape):
            n = int(np.prod(shape))
            a = arena[:, used[0]:used[0] + n]
            used[0] += n
            assert used[0] <= WORDS, used[0]
            if len(shape) == 1:
                return a
            names = "abc"[:len(shape)]
            return a.rearrange(f"p ({' '.join(names)}) -> p {' '.join(names)}", **dict(zip(names, shape)))

        wh_sb = cut(KD, 2 * HID)
        wqk_sb = cut(KD, P)
        wo_sb = cut(KH, D)
        bv_row = cut(HID)
        bo_row = cut(D)
        emb_row = cut(BUCKETS)
        buckets = cut(G)
        bias_oh = cut(G, BUCKETS)
        bias_t = cut(P)
        attn_t = cut(T, P)
        linq_t = cut(TOK)
        v_st = [cut(SUB, HID) for _ in range(2)]
        assert used[0] >= E * KD * INNER
        xh = cut(SUB, D)
        xn_s = cut(SUB, D)
        nt_s = [cut(KD, MT) for _ in range(2)]
        qk_t, quad_q, quad_k, lin_k = (cut(MT) for _ in range(4))
        link_n = cut(SUB, P)
        v_tmp = cut(2, HID)
        gate_st = [cut(KH, MT) for _ in range(2)]
        lin_kv = cut(HID)
        sim_s = cut(SUB, P)
        proj_s = cut(SUB, D)
        gated = [nt_s[c // 2][:, c % 2, :] for c in range(KH)]
        x2h = [xh, xn_s]

        used[0] = 0
        w_sb = cut(E * KD * INNER)
        rows = [cut(INNER) for _ in range(4)]
        rows_t = [cut(INNER) for _ in range(2)]
        y_s = [cut(INNER) for _ in range(2)]
        used[0] = E * KD * INNER
        in4 = [[cut(INNER) for _ in range(4)] for _ in range(2)]
        inter_t, part, upart = cut(INNER), cut(INNER), cut(INNER)
        in2 = [[in4[b][k][:, 0:D] for k in range(2)] for b in range(2)]
        out_s = [in4[b][2][:, 0:D] for b in range(2)]

        dve_step, pool_step = sig("vector_step"), sig("pool_step")
        x_loaded = [sig(f"x_loaded{c}") for c in range(4)]
        consts_loaded, consts_made = sig("consts_loaded"), sig("consts_made")
        root_asked, root_made = sig("root_asked"), sig("root_made")
        exp_asked, exp_made = sig("exp_asked"), sig("exp_made")
        xh_ready, xt_mm, nt_ready = sig("xh_ready"), sig("xt_mm"), sig("nt_ready", 1)
        qk_mm, qkt_ready = sig("qk_mm"), sig("qkt_ready")
        quad_ready, link_ready, linq_ready = sig("quad_ready", 1), sig("link_ready", 1), sig("linq_ready")
        gate_mm, gate_ready = sig("gate_mm"), sig("gate_ready", 2)
        v_mm, v_biased, v_ready = sig("v_mm", 8), sig("v_biased", 2), sig("v_ready", 2)
        sim_mm, sim_read = sig("sim_mm", 1), sig("sim_read", 1)
        linkt_mm, linkn_ready = sig("linkt_mm", 1), sig("linkn_ready")
        kv_mm, kv_used = sig("kv_mm", 2), sig("kv_used", 1)
        gate_stored, v_stored = ([sig(f"{n}_stored{b}", 16) for b in range(2)] for n in ("gate", "v"))
        kv_final = sig("kv_final")
        gate_back, v_back = ([sig(f"{n}_back{b}") for b in range(2)] for n in ("gate", "v"))
        mix_mm, gated_ready = sig("mix_mm", 8), sig("gated_ready", 8)
        proj_mm, proj_used = sig("proj_mm", 2), sig("proj_used", 2)
        xn_ready, x1_ready = sig("xn_ready"), sig("x1_ready", 1)
        x2_ready, x2t_mm, x2t_ready = sig("x2_ready"), sig("x2t_mm", 2), sig("x2t_ready", 1)
        x2_stored = [sig(f"x2_stored{b}", 16) for b in range(2)]
        logit_mm, lg_ready = sig("logit_mm", 1), sig("lg_ready", 1)
        occ_ready, rank_mm = sig("occ_ready"), sig("rank_mm")
        onehot_ready, table_mm, routed = sig("onehot_ready"), sig("table_mm", 2), sig("routed")

        class Phase:

            def __init__(self, r):
                self.w_loaded = sig(f"w_loaded_{r}")
                self.idx_ready = sig(f"idx_ready_{r}")
                self.gathered = [sig(f"gathered_{r}{b}") for b in range(4)]
                self.xt_mm = sig(f"xt_mm_{r}", 4)
                self.xt_ready = sig(f"xt_ready_{r}", 2)
                self.y_mm = sig(f"y_mm_{r}", 2)
                self.y0_ready = sig(f"y0_ready_{r}", 2)
                self.y1_ready = sig(f"y1_ready_{r}", 2)
                self.y_stored = [sig(f"y_stored_{r}{b}", 16) for b in range(2)]

        phase = {r: Phase(r) for r in ROUTES}
        c_idx, c_got = sig("c_idx"), [sig(f"c_got{b}") for b in range(2)]
        c_y0, c_z0, c_g, c_h, c_done = sig("c_y0"), sig("c_z0"), sig("c_g"), sig("c_h"), sig("c_done", 1)
        c_t_mm, c_t_ready, c_log_mm, c_lg = sig("c_t_mm", 2), sig("c_t_ready", 1), sig("c_log_mm", 1), sig("c_lg", 1)
        c_stored = [sig(f"c_stored{b}", 16) for b in range(2)]
        o_idx, o_got = sig("o_idx"), [sig(f"o_got{b}") for b in range(2)]
        o_y0, o_sum, o_ready = sig("o_y0"), sig("o_sum", 2), sig("o_ready", 1)
        o_stored = [sig(f"o_stored{b}", 16) for b in range(2)]

        def give(eng, *signals):
            for s in signals:
                eng.sem_inc(s.sem, s.credits)

        waited = {}

        def alone(eng):
            if eng not in waited:
                waited[eng] = sig(f"waited{len(waited)}")
            eng.sem_inc(waited[eng].sem, 1)

        CONSTS = 16

        block = ctx.enter_context(nc.Block())

        @block.sync
        def _(sp):
            give(sp, *gate_stored, *v_stored, *x2_stored, *c_stored, *o_stored,
                 *(s for r in ROUTES for s in phase[r].y_stored))
            x_v = x_in.rearrange("(t p) d -> p t d", p=P)
            for c in range(4):
                sp.dma_start(x_sb[:, c * 8:(c + 1) * 8, :], x_v[:, c * 8:(c + 1) * 8, :])\
                    .then_inc(x_loaded[c].sem, 16)

            def flat(a):
                return a.rearrange("p a b -> p (a b)")

            with sp.Fori(0, M // 2) as it:
                for b in range(2):
                    m = it * 2 + b
                    sp.wait_ge(gate_ready.sem, gate_ready.after(m * KH + KH - 1))
                    sp.dma_start(gate_d[ds(m * P, P), :], flat(gate_st[b])).then_inc(gate_stored[b].sem, 16)
                    sp.wait_ge(v_ready.sem, v_ready.after(m * SUB + SUB - 1))
                    sp.dma_start(v_d[ds(m * P, P), :], flat(v_st[b])).then_inc(v_stored[b].sem, 16)
            for b in range(2):
                sp.wait_ge(gate_stored[b].sem, gate_stored[b].landed(M // 2 - 1))
                sp.wait_ge(v_stored[b].sem, v_stored[b].landed(M // 2 - 1))
            sp.wait_ge(kv_mm.sem, kv_mm.after(M - 1))
            with sp.Fori(0, M // 2) as it:
                for b in range(2):
                    m = it * 2 + b
                    sp.wait_ge(gated_ready.sem, gated_ready.room(m * KH + KH - 1))
                    sp.dma_start(flat(gate_st[b]), gate_d[ds(m * P, P), :]).then_inc(gate_back[b].sem, 16)
                    sp.wait_ge(mix_mm.sem, mix_mm.room(m * KH + KH - 1))
                    sp.dma_start(flat(v_st[b]), v_d[ds(m * P, P), :]).then_inc(v_back[b].sem, 16)
            sp.wait_ge(proj_mm.sem, proj_mm.after(2 * M - 1))
            sp.wait_ge(proj_used.sem, proj_used.after(2 * M - 1))
            sp.dma_start(w_sb, w_gate).then_inc(phase["gate"].w_loaded.sem, 16)
            x2_v = x2_d.rearrange("(m s p) d -> m p s d", p=P, s=SUB)
            with sp.Fori(0, M // 2) as it:
                for b in range(2):
                    m = it * 2 + b
                    sp.wait_ge(x2_ready.sem, x2_ready.after(m))
                    sp.dma_start(x2_v[ds(m, 1)].rearrange("m p s d -> (m p) s d"), x2h[b])\
                        .then_inc(x2_stored[b].sem, 16)

            def store_sorted(r, width):
                n = phase[r]
                with sp.Fori(0, NT // 2) as it:
                    for b in range(2):
                        i = it * 2 + b
                        sp.wait_ge(n.y0_ready.sem, n.y0_ready.after(i))
                        if width > 512:
                            sp.wait_ge(n.y1_ready.sem, n.y1_ready.after(i))
                        sp.dma_start(sorted_d[r][ds(i * P, P), :], y_s[b][:, 0:width]).then_inc(n.y_stored[b].sem, 16)

            store_sorted("gate", INNER)
            sp.wait_ge(phase["gate"].y_mm.sem, phase["gate"].y_mm.after(NT - 1))
            sp.dma_start(w_sb, w_up).then_inc(phase["up"].w_loaded.sem, 16)
            store_sorted("up", INNER)
            sp.wait_ge(phase["up"].y_mm.sem, phase["up"].y_mm.after(NT - 1))
            sp.dma_start(w_sb, w_down).then_inc(phase["down"].w_loaded.sem, 16)
            with sp.Fori(0, T // 2) as it:
                for b in range(2):
                    t = it * 2 + b
                    sp.wait_ge(c_done.sem, c_done.after(t))
                    sp.dma_start(inter_d[ds(t * P, P), :], in4[b][1]).then_inc(c_stored[b].sem, 16)
            store_sorted("down", D)
            with sp.Fori(0, T // 2) as it:
                for b in range(2):
                    t = it * 2 + b
                    sp.wait_ge(o_ready.sem, o_ready.after(t))
                    sp.dma_start(out[ds(t * P, P), :], out_s[b]).then_inc(o_stored[b].sem, 16)
            for b in range(2):
                sp.wait_ge(o_stored[b].sem, o_stored[b].landed(T // 2 - 1))
            for s, n in ((x2_stored, M), (c_stored, T), *((phase[r].y_stored, NT) for r in ROUTES)):
                for b in range(2):
                    sp.wait_ge(s[b].sem, s[b].landed(n // 2 - 1))

        @block.gpsimd
        def _(pool):
            give(pool, link_ready, x1_ready)
            step = Steps()

            def load(dst, src):
                pool.dma_start(dst, src).then_inc(consts_loaded.sem, 16)

            load(wh_sb, w_h.rearrange("(k p) n -> p k n", p=P))
            load(wqk_sb, w_qk.rearrange("(k p) n -> p k n", p=P))
            load(wo_sb, w_out.rearrange("(k p) n -> p k n", p=P))
            load(g_col[:, :], ln_g)
            load(b_col[:, :], ln_b)
            load(bqk_col[:, :], b_qk)
            load(bgate_col[:, :], bh_gate)
            load(bv_row, bh_value.partition_broadcast(P))
            load(bo_row, b_out.partition_broadcast(P))
            load(emb_row, rel_emb.partition_broadcast(P))
            load(gamma_col[:, :], os_gamma)
            load(beta_col[:, :], os_beta)
            load(buckets, bucket_in)
            load(rt_sb[:, :, 0:E], r_gate.rearrange("(k p) n -> p k n", p=P))
            load(rt_sb[:, :, E:2 * E], r_up.rearrange("(k p) n -> p k n", p=P))
            load(rd_sb[:, :, :], r_down.rearrange("(k p) n -> p k n", p=P))
            pool.memset(ident[:, :], 0.0).then_inc(pool_step.sem, 1)
            pool.wait_ge(pool_step.sem, step.next())
            pool.memset(before[:, :], 1.0).then_inc(pool_step.sem, 1)
            pool.wait_ge(pool_step.sem, step.next())
            pool.memset(ones[:, :], 1.0).then_inc(pool_step.sem, 1)
            pool.wait_ge(pool_step.sem, step.next())
            pool.memset(zeros[:, :], 0.0).then_inc(pool_step.sem, 1)
            pool.wait_ge(pool_step.sem, step.next())
            pool.iota(iota_i[:, :], pattern=[[1, P]], base=0, channel_multiplier=0).then_inc(pool_step.sem, 1)
            pool.wait_ge(pool_step.sem, step.next())
            pool.iota(token_i[:, :], pattern=[[P, T]], base=0, channel_multiplier=1).then_inc(pool_step.sem, 1)
            pool.wait_ge(pool_step.sem, step.next())
            pool.affine_select(out=ident[:, :], in_=ident[:, :], compare_op=ALU.not_equal, fill=1.0,
                               base=0, pattern=[[-1, P]], channel_multiplier=1).then_inc(pool_step.sem, 1)
            pool.wait_ge(pool_step.sem, step.next())
            pool.affine_select(out=before[:, :], in_=before[:, :], compare_op=ALU.is_gt, fill=0.0,
                               base=0, pattern=[[1, P]], channel_multiplier=-1).then_inc(pool_step.sem, 1)
            pool.wait_ge(pool_step.sem, step.next())
            pool.tensor_copy(iota[:, :], iota_i[:, :]).then_inc(pool_step.sem, 1)
            pool.wait_ge(pool_step.sem, step.next())
            pool.tensor_copy(token_f[:, :], token_i[:, :]).then_inc(pool_step.sem, 1)
            pool.wait_ge(pool_step.sem, step.next())
            pool.sem_inc(consts_made.sem, 1)
            pool.wait_ge(consts_loaded.sem, 16 * CONSTS)
            with pool.Fori(0, M) as m:
                pool.wait_ge(qkt_ready.sem, qkt_ready.after(m))
                pool.wait_ge(linkt_mm.sem, linkt_mm.room(m))
                alone(pool)
                pool.tensor_scalar(lin_k, qk_t, gamma_col[:, 3:4], beta_col[:, 3:4], ALU.mult,
                                   ALU.add).then_inc(link_ready.sem, 1)
            with pool.Fori(0, M) as m:
                step.enter(m, 1)
                pool.wait_ge(xn_ready.sem, xn_ready.after(m))
                alone(pool)
                x_m = x_sb[:, ds(m * SUB, SUB), :]
                pool.tensor_tensor(xn_s, xn_s, x_m, ALU.add).then_inc(pool_step.sem, 1)
                pool.wait_ge(pool_step.sem, step.next())
                pool.wait_ge(proj_used.sem, proj_used.after(m * 2 + 1))
                alone(pool)
                pool.tensor_tensor(x_m, xn_s, proj_s, ALU.add).then_inc(x1_ready.sem, 1)
            step.leave(M)

            def indexed(b, k):
                return bass.IndirectOffsetOnAxis(ap=idx_s[b][:, k:k + 1].bitcast(U32), axis=0)

            def gather_tiles(r, source, width):
                n = phase[r]
                with pool.Fori(0, NT // 4) as it:
                    for b in range(4):
                        i = it * 4 + b
                        pool.wait_ge(n.xt_mm.sem, n.xt_mm.room(i))
                        pool.tensor_copy(idx_s[b][:, 0:1], ids[r][:, ds(i, 1)]).then_inc(n.idx_ready.sem, 1)
                        pool.wait_ge(n.idx_ready.sem, n.idx_ready.after(i))
                        alone(pool)
                        pool.indirect_dma_start(rows[b][:, 0:width], None, source[:, :], indexed(b, 0))\
                            .then_inc(n.gathered[b].sem, 16)

            for b in range(2):
                pool.wait_ge(x2_stored[b].sem, x2_stored[b].landed(M // 2 - 1))
            pool.wait_ge(routed.sem, routed.after(0))
            gather_tiles("gate", x2_d, D)
            pool.wait_ge(routed.sem, routed.after(1))
            pool.wait_ge(phase["gate"].xt_mm.sem, phase["gate"].xt_mm.after(NT - 1))
            gather_tiles("up", x2_d, D)
            for r in ("gate", "up"):
                for b in range(2):
                    pool.wait_ge(phase[r].y_stored[b].sem, phase[r].y_stored[b].landed(NT // 2 - 1))
            with pool.Fori(0, T // 2) as it:
                for b in range(2):
                    t = it * 2 + b
                    pool.wait_ge(c_t_mm.sem, c_t_mm.room(t))
                    pool.wait_ge(c_stored[b].sem, c_stored[b].sent(it))
                    for k in range(4):
                        ins = pool.tensor_copy(idx_s[b][:, k:k + 1], pos[ROUTES[k // 2]][:, k % 2, ds(t, 1)])
                    ins.then_inc(c_idx.sem, 1)
                    pool.wait_ge(c_idx.sem, c_idx.after(t))
                    alone(pool)
                    for k in range(4):
                        pool.indirect_dma_start(in4[b][k], None, sorted_d[ROUTES[k // 2]][:, :],
                                                indexed(b, k)).then_inc(c_got[b].sem, 16)
            pool.wait_ge(routed.sem, routed.after(2))
            for b in range(2):
                pool.wait_ge(c_stored[b].sem, c_stored[b].landed(T // 2 - 1))
            gather_tiles("down", inter_d, INNER)
            for b in range(2):
                pool.wait_ge(phase["down"].y_stored[b].sem, phase["down"].y_stored[b].landed(NT // 2 - 1))
            with pool.Fori(0, T // 2) as it:
                for b in range(2):
                    t = it * 2 + b
                    pool.wait_ge(o_sum.sem, o_sum.room(t))
                    for k in range(2):
                        ins = pool.tensor_copy(idx_s[b][:, k:k + 1], pos["down"][:, k, ds(t, 1)])
                    ins.then_inc(o_idx.sem, 1)
                    pool.wait_ge(o_idx.sem, o_idx.after(t))
                    alone(pool)
                    for k in range(2):
                        pool.indirect_dma_start(in2[b][k], None, sorted_d["down"][:, :],
                                                indexed(b, k)).then_inc(o_got[b].sem, 16)

        @block.scalar
        def _(act):
            give(act, nt_ready, gate_ready, v_ready, x2t_ready, c_t_ready,
                 *(s for r in ROUTES for s in (phase[r].xt_ready, phase[r].y0_ready)))
            roots = [0]

            def square_root():
                act.wait_ge(root_asked.sem, root_asked.after(roots[0]))
                act.activation(root[:, :], root_in[:, :], ACT.Sqrt).then_inc(root_made.sem, 1)
                roots[0] += 1

            def exponential(n):
                act.wait_ge(exp_asked.sem, exp_asked.after(n))
                c = comb[ROUTES[n]]
                act.activation(c[:, 1, :], c[:, 0, :], ACT.Exp).then_inc(exp_made.sem, 1)

            square_root()
            square_root()
            act.wait_ge(consts_loaded.sem, 16 * CONSTS)
            with act.Fori(0, M // 2) as it:
                for b in range(2):
                    m = it * 2 + b
                    act.wait_ge(xt_mm.sem, xt_mm.after(m))
                    act.wait_ge(v_mm.sem, v_mm.room(m * SUB + SUB - 1))
                    for k in range(KD):
                        ins = act.activation(nt_s[b][:, k, :], bank[k][:, :], ACT.Identity, bias=b_col[:, k:k + 1],
                                             scale=g_col[:, k:k + 1])
                    ins.then_inc(nt_ready.sem, 1)
                    act.wait_ge(qk_mm.sem, qk_mm.after(m))
                    act.wait_ge(quad_ready.sem, quad_ready.room(m))
                    act.wait_ge(link_ready.sem, link_ready.room(m))
                    act.activation(qk_t, bank[2][:, :], ACT.Silu, bias=bqk_col[:, :]).then_inc(qkt_ready.sem, 1)
                    act.wait_ge(qkt_ready.sem, qkt_ready.after(m))
                    act.activation(linq_t[:, ds(m * MT, MT)], qk_t, ACT.Identity, bias=beta_col[:, 1:2],
                                   scale=gamma_col[:, 1:2]).then_inc(linq_ready.sem, 1)
                    act.wait_ge(gate_stored[b].sem, gate_stored[b].sent(it))
                    for c in range(KH):
                        act.wait_ge(gate_mm.sem, gate_mm.after(m * KH + c))
                        act.activation(gate_st[b][:, c, :], bank[3 + c % 2][:, :], ACT.Silu,
                                       bias=bgate_col[:, c:c + 1]).then_inc(gate_ready.sem, 1)
                    act.wait_ge(v_stored[b].sem, v_stored[b].sent(it))
                    act.wait_ge(kv_mm.sem, kv_mm.room(m))
                    for s in range(SUB):
                        act.wait_ge(v_biased.sem, v_biased.after(m * SUB + s))
                        act.activation(v_st[b][:, s, :], v_tmp[:, s % 2, :], ACT.Silu).then_inc(v_ready.sem, 1)
            square_root()
            with act.Fori(0, M) as m:
                act.wait_ge(x2t_mm.sem, x2t_mm.after(m))
                act.wait_ge(logit_mm.sem, logit_mm.room(m))
                for k in range(KD):
                    ins = act.activation(nt_s[0][:, k, :], bank[k][:, :], ACT.Copy)
                ins.then_inc(x2t_ready.sem, 1)
            exponential(0)
            exponential(1)

            def expert_copies(r, kc, width):
                n = phase[r]

                def transposed(i, b):
                    act.wait_ge(n.xt_mm.sem, n.xt_mm.after(i))
                    act.wait_ge(n.y_mm.sem, n.y_mm.room(i))
                    w = min(kc, 4) * P
                    for h in range(-(-kc // 4)):
                        ins = act.activation(rows_t[b % 2][:, h * 512:h * 512 + w],
                                             bank[2 * (b % 2) + h][:, 0:w], ACT.Copy)
                    ins.then_inc(n.xt_ready.sem, 1)

                def product(i, b, it):
                    act.wait_ge(n.y_mm.sem, n.y_mm.after(i))
                    act.wait_ge(n.y_stored[b % 2].sem, n.y_stored[b % 2].sent(it * 2 + b // 2))
                    w = min(width, 512)
                    act.activation(y_s[b % 2][:, 0:w], bank[4 + 2 * (b % 2)][:, 0:w],
                                   ACT.Copy).then_inc(n.y0_ready.sem, 1)

                transposed(0, 0)
                with act.Fori(0, NT // 4 - 1) as it:
                    for b in range(4):
                        transposed(it * 4 + b + 1, b + 1)
                        product(it * 4 + b, b, it)
                for b in range(4):
                    if b < 3:
                        transposed(NT - 4 + b + 1, b + 1)
                    product(NT - 4 + b, b, NT // 4 - 1)

            expert_copies("gate", KD, INNER)
            for b in range(2):
                act.wait_ge(phase["gate"].y_stored[b].sem, phase["gate"].y_stored[b].landed(NT // 2 - 1))
            expert_copies("up", KD, INNER)

            def inner(t, b, it, copy_before):
                act.wait_ge(c_got[b].sem, c_got[b].landed(it, 64))
                act.wait_ge(c_done.sem, c_done.room(t))
                act.activation(part, in4[b][0], ACT.Copy, scale=comb["gate"][:, 0, ds(t, 1)]).then_inc(c_y0.sem, 1)
                act.activation(upart, in4[b][2], ACT.Copy, scale=comb["up"][:, 0, ds(t, 1)]).then_inc(c_z0.sem, 1)
                if copy_before:
                    inner_transposed(t - 1)
                act.wait_ge(c_g.sem, c_g.after(t))
                act.activation(in4[b][0], part, ACT.Silu).then_inc(c_h.sem, 1)

            def inner_transposed(t):
                act.wait_ge(c_t_mm.sem, c_t_mm.after(t))
                act.wait_ge(c_log_mm.sem, c_log_mm.room(t))
                for h in range(2):
                    ins = act.activation(inter_t[:, h * 512:(h + 1) * 512], bank[h][:, :], ACT.Copy)
                ins.then_inc(c_t_ready.sem, 1)

            inner(0, 0, 0, False)
            with act.Fori(0, T // 2 - 1) as it:
                inner(it * 2 + 1, 1, it, True)
                inner(it * 2 + 2, 0, it + 1, True)
            inner(T - 1, 1, T // 2 - 1, True)
            inner_transposed(T - 1)
            exponential(2)
            expert_copies("down", KI, D)
            with act.Fori(0, T // 2) as it:
                for b in range(2):
                    t = it * 2 + b
                    act.wait_ge(o_got[b].sem, o_got[b].landed(it, 32))
                    act.wait_ge(o_ready.sem, o_ready.room(t))
                    act.activation(part[:, 0:D], in2[b][0], ACT.Copy,
                                   scale=comb["down"][:, 0, ds(t, 1)]).then_inc(o_y0.sem, 1)

        @block.tensor
        def _(pe):
            give(pe, v_mm, sim_mm, linkt_mm, kv_mm, mix_mm, proj_mm, x2t_mm, logit_mm, table_mm, c_t_mm, c_log_mm,
                 *(s for r in ROUTES for s in (phase[r].xt_mm, phase[r].y_mm)))
            pe.wait_ge(consts_made.sem, consts_made.after(0))
            pe.wait_ge(consts_loaded.sem, 16 * CONSTS)

            def turn_rows(src):
                for k in range(KD):
                    for s in range(SUB):
                        ins = pe.transpose(bank[k][:, s * P:(s + 1) * P], src[:, s, k * P:(k + 1) * P], ident[:, :])
                return ins

            def transposes(m):
                pe.wait_ge(xh_ready.sem, xh_ready.after(m))
                pe.wait_ge(nt_ready.sem, nt_ready.room(m))
                turn_rows(xh).then_inc(xt_mm.sem, 1)

            def projections(m, b):
                pe.wait_ge(nt_ready.sem, nt_ready.after(m))
                pe.wait_ge(sim_read.sem, sim_read.room(m))
                for k in range(KD):
                    ins = pe.matmul(bank[2][:, :], wqk_sb[:, k, :], nt_s[b][:, k, :], start=(k == 0),
                                    stop=(k == KD - 1))
                ins.then_inc(qk_mm.sem, 1)
                for c in range(KH):
                    pe.wait_ge(gate_ready.sem, gate_ready.room(m * KH + c))
                    for k in range(KD):
                        ins = pe.matmul(bank[3 + c % 2][:, :], wh_sb[:, k, HID + c * P:HID + (c + 1) * P],
                                        nt_s[b][:, k, :], start=(k == 0), stop=(k == KD - 1))
                    ins.then_inc(gate_mm.sem, 1)
                for s in range(SUB):
                    pe.wait_ge(v_biased.sem, v_biased.room(m * SUB + s))
                    for k in range(KD):
                        ins = pe.matmul(bank[5 + s % 2][:, :], nt_s[b][:, k, s * P:(s + 1) * P], wh_sb[:, k, 0:HID],
                                        start=(k == 0), stop=(k == KD - 1))
                    ins.then_inc(v_mm.sem, 1)

            def groups(m, b):
                pe.wait_ge(quad_ready.sem, quad_ready.after(m))
                pe.wait_ge(qkt_ready.sem, qkt_ready.after(m))
                for s in range(SUB):
                    c = slice(s * P, (s + 1) * P)
                    ins = pe.matmul(bank[2][:, c], quad_k[:, c], quad_q[:, c], start=True, stop=True)
                ins.then_inc(sim_mm.sem, 1)
                pe.wait_ge(link_ready.sem, link_ready.after(m))
                pe.wait_ge(kv_used.sem, kv_used.room(m))
                for s in range(SUB):
                    c = slice(s * P, (s + 1) * P)
                    ins = pe.transpose(bank[7][:, c], lin_k[:, c], ident[:, :])
                ins.then_inc(linkt_mm.sem, 1)
                pe.wait_ge(linkn_ready.sem, linkn_ready.after(m))
                pe.wait_ge(v_ready.sem, v_ready.after(m * SUB + SUB - 1))
                for s in range(SUB):
                    ins = pe.matmul(bank[7][:, :], link_n[:, s, :], v_st[b][:, s, :], start=(s == 0),
                                    stop=(s == SUB - 1))
                ins.then_inc(kv_mm.sem, 1)

            transposes(0)
            with pe.Fori(0, M // 2 - 1) as it:
                for b in range(2):
                    m = it * 2 + b
                    projections(m, b)
                    transposes(m + 1)
                    groups(m, b)
            for b in range(2):
                m = M - 2 + b
                projections(m, b)
                if b == 0:
                    transposes(m + 1)
                groups(m, b)

            pe.wait_ge(kv_final.sem, kv_final.after(0))
            pe.wait_ge(linq_ready.sem, linq_ready.after(M - 1))
            with pe.Fori(0, M // 2) as it:
                for b in range(2):
                    m = it * 2 + b
                    pe.wait_ge(v_back[b].sem, v_back[b].landed(it))
                    for c in range(KH):
                        pe.wait_ge(gated_ready.sem, gated_ready.after(m * KH + c - KH))
                        pe.matmul(bank[c][:, :], lin_kv[:, c * P:(c + 1) * P], linq_t[:, ds(m * MT, MT)],
                                  start=True, stop=False, skip_group_check=True)
                        for s in range(SUB):
                            ins = pe.matmul(bank[c][:, s * P:(s + 1) * P], v_st[b][:, s, c * P:(c + 1) * P],
                                            attn_t[:, ds(m * SUB + s, 1), :].rearrange("p a b -> p (a b)"),
                                            start=False, stop=(s == SUB - 1), skip_group_check=True)
                        ins.then_inc(mix_mm.sem, 1)
                    pe.wait_ge(gated_ready.sem, gated_ready.after(m * KH + KH - 1))
                    for h in range(2):
                        pe.wait_ge(proj_used.sem, proj_used.room(m * 2 + h))
                        for s in (2 * h, 2 * h + 1):
                            for c in range(KH):
                                ins = pe.matmul(bank[4 + h][:, (s % 2) * D:(s % 2 + 1) * D],
                                                gated[c][:, s * P:(s + 1) * P], wo_sb[:, c, :], start=(c == 0),
                                                stop=(c == KH - 1))
                        ins.then_inc(proj_mm.sem, 1)

            with pe.Fori(0, M // 2) as it:
                for b in range(2):
                    m = it * 2 + b
                    pe.wait_ge(x2_ready.sem, x2_ready.after(m))
                    pe.wait_ge(x2t_ready.sem, x2t_ready.room(m))
                    turn_rows(x2h[b]).then_inc(x2t_mm.sem, 1)
                    pe.wait_ge(x2t_ready.sem, x2t_ready.after(m))
                    pe.wait_ge(lg_ready.sem, lg_ready.room(m))
                    for s in range(SUB):
                        for k in range(KD):
                            ins = pe.matmul(bank[2][:, s * 2 * E:(s + 1) * 2 * E], nt_s[0][:, k, s * P:(s + 1) * P],
                                            rt_sb[:, k, :], start=(k == 0), stop=(k == KD - 1))
                    ins.then_inc(logit_mm.sem, 1)

            def routing(n):
                pe.wait_ge(occ_ready.sem, occ_ready.after(n))
                flat = occ[:, :, :].rearrange("p e t -> p (e t)")
                pe.matmul(bank[0][:, 0:E * T], before[:, :], flat, start=True, stop=True)
                pe.matmul(bank[1][:, 0:E * T], ones[:, :], flat, start=True, stop=True).then_inc(rank_mm.sem, 1)
                pe.matmul(bank[2][:, 0:NT], zeros[:, :], zeros[:, 0:NT], start=True, stop=False,
                          skip_group_check=True)
                with pe.Fori(0, T // 2) as it:
                    for b in range(2):
                        pe.wait_ge(onehot_ready.sem, onehot_ready.after(it * 2 + (b + n * T)))
                        for k in range(2):
                            ins = pe.matmul(bank[2][:, 0:NT], row_oh[b][:, k, :], tile_id[b][:, k, :], start=False,
                                            stop=False, skip_group_check=True)
                        ins.then_inc(table_mm.sem, 1)

            routing(0)
            routing(1)

            def experts(r, kc, width):
                n = phase[r]

                def transposed(i, b, it):
                    pe.wait_ge(n.gathered[b % 4].sem, n.gathered[b % 4].landed(it))
                    pe.wait_ge(n.xt_ready.sem, n.xt_ready.room(i))
                    for k in range(kc):
                        ins = pe.transpose(bank[2 * (b % 2) + k // 4][:, (k % 4) * P:(k % 4 + 1) * P],
                                           rows[b % 4][:, k * P:(k + 1) * P], ident[:, :])
                    ins.then_inc(n.xt_mm.sem, 1)

                def product(i, b):
                    e = pe.value_load(expert_of[r][0:1, ds(i, 1)], min_val=0, max_val=E - 1)
                    pe.wait_ge(n.xt_ready.sem, n.xt_ready.after(i))
                    pe.wait_ge(n.y0_ready.sem, n.y0_ready.room(i))
                    if width > 512:
                        pe.wait_ge(n.y1_ready.sem, n.y1_ready.room(i))
                    w = min(width, 512)
                    for h in range(width // w):
                        for k in range(kc):
                            ins = pe.matmul(bank[4 + 2 * (b % 2) + h][:, 0:w], rows_t[b % 2][:, k * P:(k + 1) * P],
                                            w_sb[:, ds(e * (kc * width) + (k * width + h * w), w)],
                                            start=(k == 0), stop=(k == kc - 1))
                    ins.then_inc(n.y_mm.sem, 1)

                pe.wait_ge(routed.sem, routed.after(2 if r == "down" else 1))
                pe.wait_ge(n.w_loaded.sem, n.w_loaded.landed(0))
                transposed(0, 0, 0)
                with pe.Fori(0, NT // 4 - 1) as it:
                    for b in range(4):
                        transposed(it * 4 + b + 1, b + 1, it + (b + 1) // 4)
                        product(it * 4 + b, b)
                for b in range(4):
                    if b < 3:
                        transposed(NT - 4 + b + 1, b + 1, NT // 4 - 1)
                    product(NT - 4 + b, b)

            experts("gate", KD, INNER)
            pe.wait_ge(phase["gate"].y0_ready.sem, phase["gate"].y0_ready.after(NT - 1))
            pe.wait_ge(phase["gate"].y1_ready.sem, phase["gate"].y1_ready.after(NT - 1))
            experts("up", KD, INNER)
            with pe.Fori(0, T // 2) as it:
                for b in range(2):
                    t = it * 2 + b
                    pe.wait_ge(c_done.sem, c_done.after(t))
                    pe.wait_ge(c_t_ready.sem, c_t_ready.room(t))
                    for k in range(KI):
                        ins = pe.transpose(bank[k // 4][:, (k % 4) * P:(k % 4 + 1) * P],
                                           in4[b][1][:, k * P:(k + 1) * P], ident[:, :])
                    ins.then_inc(c_t_mm.sem, 1)
                    pe.wait_ge(c_t_ready.sem, c_t_ready.after(t))
                    pe.wait_ge(c_lg.sem, c_lg.room(t))
                    for k in range(KI):
                        ins = pe.matmul(bank[2][:, 0:E], inter_t[:, k * P:(k + 1) * P], rd_sb[:, k, :],
                                        start=(k == 0), stop=(k == KI - 1))
                    ins.then_inc(c_log_mm.sem, 1)
            routing(2)
            experts("down", KI, D)

        @block.vector
        def _(dve):
            give(dve, quad_ready, v_biased, sim_read, kv_used, gated_ready, proj_used, lg_ready, c_done, c_lg, o_sum,
                 o_ready, *(phase[r].y1_ready for r in ROUTES))
            step = Steps()
            roots = [0]

            def inverse_root(dst, src):
                dve.tensor_scalar(root_in[:, :], src[:, :], EPS, None, ALU.add).then_inc(root_asked.sem, 1)
                dve.wait_ge(root_asked.sem, root_asked.after(roots[0]))
                dve.wait_ge(root_made.sem, root_made.after(roots[0]))
                roots[0] += 1
                dve.reciprocal(dst[:, :], root[:, :]).then_inc(dve_step.sem, 1)
                dve.wait_ge(dve_step.sem, step.next())
                dve.tensor_tensor(corr[:, :], root_in[:, :], dst[:, :], ALU.mult).then_inc(dve_step.sem, 1)
                dve.wait_ge(dve_step.sem, step.next())
                dve.tensor_tensor(corr[:, :], corr[:, :], dst[:, :], ALU.mult).then_inc(dve_step.sem, 1)
                dve.wait_ge(dve_step.sem, step.next())
                dve.tensor_scalar(corr[:, :], corr[:, :], -0.5, 1.5, ALU.mult, ALU.add).then_inc(dve_step.sem, 1)
                dve.wait_ge(dve_step.sem, step.next())
                dve.tensor_tensor(dst[:, :], dst[:, :], corr[:, :], ALU.mult).then_inc(dve_step.sem, 1)
                dve.wait_ge(dve_step.sem, step.next())

            def tile_of(t):
                return x_sb[:, ds(t, 1), :].rearrange("p a d -> p (a d)")

            def macro_stats(m):
                alone(dve)
                for s in range(SUB):
                    ins = dve.bn_stats(stats[:, s, :], tile_of(m * SUB + s))
                ins.then_inc(dve_step.sem, 1)
                dve.wait_ge(dve_step.sem, step.next())
                alone(dve)
                for s in range(SUB):
                    ins = dve.bn_aggr(mv[:, s, :], stats[:, s, :])
                ins.then_inc(dve_step.sem, 1)
                dve.wait_ge(dve_step.sem, step.next())
                alone(dve)
                dve.tensor_copy(mean[:, ds(m * SUB, SUB)], mv[:, :, 0])
                dve.tensor_copy(var[:, ds(m * SUB, SUB)], mv[:, :, 1]).then_inc(dve_step.sem, 1)
                dve.wait_ge(dve_step.sem, step.next())

            def centred(dst, m, scale):
                for s in range(SUB):
                    t = m * SUB + s
                    ins = dve.tensor_scalar(dst[:, s, :], tile_of(t), mean[:, ds(t, 1)], scale[:, ds(t, 1)],
                                            ALU.subtract, ALU.mult)
                return ins

            for c in range(4):
                dve.wait_ge(x_loaded[c].sem, x_loaded[c].landed(0))
                with dve.Fori(0, 2) as g:
                    step.enter(g, 3)
                    macro_stats(g + 2 * c)
                step.leave(2)
            inverse_root(rstd, var)
            dve.tensor_tensor(corr[:, :], rstd[:, :], rstd[:, :], ALU.mult).then_inc(dve_step.sem, 1)
            dve.wait_ge(dve_step.sem, step.next())
            dve.tensor_tensor(var[:, :], var[:, :], corr[:, :], ALU.mult).then_inc(dve_step.sem, 1)
            dve.wait_ge(dve_step.sem, step.next())
            inverse_root(rstd12, var)
            dve.tensor_tensor(rstd12[:, :], rstd12[:, :], rstd[:, :], ALU.mult).then_inc(dve_step.sem, 1)
            dve.wait_ge(dve_step.sem, step.next())
            centred(xh, 0, rstd12).then_inc(xh_ready.sem, 1)

            dve.wait_ge(consts_loaded.sem, 16 * CONSTS)
            dve.wait_ge(consts_made.sem, consts_made.after(0))
            dve.tensor_tensor(bias_oh, buckets.unsqueeze(2).to_broadcast([P, G, BUCKETS]),
                              iota[:, 0:BUCKETS].unsqueeze(1).to_broadcast([P, G, BUCKETS]),
                              ALU.is_equal).then_inc(dve_step.sem, 1)
            dve.wait_ge(dve_step.sem, step.next())
            dve.tensor_tensor(bias_oh, bias_oh, emb_row.unsqueeze(1).to_broadcast([P, G, BUCKETS]),
                              ALU.mult).then_inc(dve_step.sem, 1)
            dve.wait_ge(dve_step.sem, step.next())
            dve.tensor_reduce(sim_s[:, 0, 0:G], bias_oh, AX.X, ALU.add).then_inc(dve_step.sem, 1)
            dve.wait_ge(dve_step.sem, step.next())
            dve.memset(bias_t, OFF_GROUP).then_inc(dve_step.sem, 1)
            dve.wait_ge(dve_step.sem, step.next())
            dve.memset(lin_kv, 0.0).then_inc(dve_step.sem, 1)
            dve.wait_ge(dve_step.sem, step.next())
            for h in range(2):
                block_h = slice(h * G, (h + 1) * G)
                dve.tensor_scalar(bias_t[block_h, block_h], sim_s[block_h, 0, 0:G], BIAS_SCALE, None,
                                  ALU.mult).then_inc(dve_step.sem, 1)
                dve.wait_ge(dve_step.sem, step.next())

            def first_pass(m, last):
                if not last:
                    dve.wait_ge(xt_mm.sem, xt_mm.after(m))
                    centred(xh, m + 1, rstd12).then_inc(xh_ready.sem, 1)
                dve.wait_ge(qkt_ready.sem, qkt_ready.after(m))
                dve.wait_ge(sim_mm.sem, sim_mm.room(m))
                dve.tensor_scalar(quad_q, qk_t, gamma_col[:, 0:1], beta_col[:, 0:1], ALU.mult, ALU.add)
                dve.tensor_scalar(quad_k, qk_t, gamma_col[:, 2:3], beta_col[:, 2:3], ALU.mult,
                                  ALU.add).then_inc(quad_ready.sem, 1)
                for s in range(SUB):
                    dve.wait_ge(v_mm.sem, v_mm.after(m * SUB + s))
                    dve.wait_ge(v_ready.sem, v_ready.room(m * SUB + s))
                    dve.tensor_tensor(v_tmp[:, s % 2, :], bank[5 + s % 2][:, :], bv_row, ALU.add)\
                        .then_inc(v_biased.sem, 1)
                dve.wait_ge(sim_mm.sem, sim_mm.after(m))
                dve.scalar_tensor_tensor(
                    out=sim_s, in0=bank[2][:, :].rearrange("p (s q) -> p s q", s=SUB), scalar=SIM_SCALE,
                    in1=bias_t.unsqueeze(1).to_broadcast([P, SUB, P]), op0=ALU.mult, op1=ALU.add)\
                    .then_inc(sim_read.sem, 1)
                dve.wait_ge(sim_read.sem, sim_read.after(m))
                dve.scalar_tensor_tensor(out=attn_t[:, ds(m * SUB, SUB), :], in0=sim_s, scalar=0.0, in1=sim_s,
                                         op0=ALU.max, op1=ALU.mult)
                dve.wait_ge(linkt_mm.sem, linkt_mm.after(m))
                dve.wait_ge(kv_mm.sem, kv_mm.after(m - 1))
                dve.tensor_copy(link_n.rearrange("p s q -> p (s q)"), bank[7][:, :]).then_inc(linkn_ready.sem, 1)
                dve.wait_ge(kv_mm.sem, kv_mm.after(m))
                dve.tensor_tensor(lin_kv, lin_kv, bank[7][:, :], ALU.add).then_inc(kv_used.sem, 1)

            with dve.Fori(0, M - 1) as m:
                first_pass(m, False)
            first_pass(M - 1, True)
            dve.wait_ge(kv_used.sem, kv_used.after(M - 1))
            dve.tensor_scalar(lin_kv, lin_kv, 1.0 / TOK, None, ALU.mult).then_inc(kv_final.sem, 1)

            def second_pass(m, b, it, stats_before):
                dve.wait_ge(x1_ready.sem, x1_ready.room(m))
                centred(xn_s, m, rstd).then_inc(xn_ready.sem, 1)
                dve.wait_ge(gate_back[b].sem, gate_back[b].landed(it))
                dve.wait_ge(proj_mm.sem, proj_mm.after(m * 2 - 1))
                for c in range(KH):
                    dve.wait_ge(mix_mm.sem, mix_mm.after(m * KH + c))
                    dve.tensor_tensor(gated[c], bank[c][:, :], gate_st[b][:, c, :], ALU.mult)\
                        .then_inc(gated_ready.sem, 1)
                if stats_before:
                    dve.wait_ge(x1_ready.sem, x1_ready.after(m - 1))
                    macro_stats(m - 1)
                for h in range(2):
                    dve.wait_ge(proj_mm.sem, proj_mm.after(m * 2 + h))
                    dve.tensor_tensor(proj_s[:, 2 * h:2 * h + 2, :],
                                      bank[4 + h][:, :].rearrange("p (s d) -> p s d", s=2),
                                      bo_row.unsqueeze(1).to_broadcast([P, 2, D]), ALU.add)\
                        .then_inc(proj_used.sem, 1)

            second_pass(0, 0, 0, False)
            with dve.Fori(0, M // 2 - 1) as it:
                step.enter(it, 6)
                second_pass(it * 2 + 1, 1, it, True)
                second_pass(it * 2 + 2, 0, it + 1, True)
            step.leave(M // 2 - 1)
            second_pass(M - 1, 1, M // 2 - 1, True)
            dve.wait_ge(x1_ready.sem, x1_ready.after(M - 1))
            macro_stats(M - 1)
            inverse_root(rstd, var)

            def pick_two(subs, routes, put):
                pairs = [(s, j) for s in range(subs) for j in range(routes)]
                for s, j in pairs:
                    ins = dve.max(mx[:, s, j, :], lg[:, s, j, :])
                ins.then_inc(dve_step.sem, 1)
                dve.wait_ge(dve_step.sem, step.next())
                alone(dve)
                for s, j in pairs:
                    ins = dve.max_index(mi[:, s, j, :], mx[:, s, j, :], lg[:, s, j, :])
                ins.then_inc(dve_step.sem, 1)
                dve.wait_ge(dve_step.sem, step.next())
                alone(dve)
                for table, got in ((top_v, mx), (top_i, mi)):
                    for j in range(routes):
                        ins = put(table, got, j)
                ins.then_inc(dve_step.sem, 1)
                dve.wait_ge(dve_step.sem, step.next())

            with dve.Fori(0, M // 2) as it:
                step.enter(it, 8)
                for b in range(2):
                    m = it * 2 + b
                    dve.wait_ge(x2t_mm.sem, x2t_mm.room(m))
                    dve.wait_ge(x2_stored[b].sem, x2_stored[b].sent(it))
                    centred(x2h[b], m, rstd).then_inc(x2_ready.sem, 1)
                    dve.wait_ge(logit_mm.sem, logit_mm.after(m))
                    ins = dve.tensor_copy(lg[:, :, :, :].rearrange("p s j e -> p (s j e)"),
                                          bank[2][:, 0:SUB * 2 * E])
                    ins.then_inc(dve_step.sem, 1)
                    dve.wait_ge(dve_step.sem, step.next())
                    dve.sem_inc(lg_ready.sem, 1)
                    pick_two(SUB, 2, lambda table, got, j: dve.tensor_copy(
                        table[:, j, :, ds(m * SUB, SUB)].rearrange("p k s -> p s k"), got[:, :, j, 0:2]))
            step.leave(M // 2)

            def routing(n):
                r = ROUTES[n]
                c = comb[r]
                dve.tensor_tensor(c[:, 0, :], top_v[:, n, 1, :], top_v[:, n, 0, :], ALU.subtract)\
                    .then_inc(exp_asked.sem, 1)
                for k in range(2):
                    ins = dve.tensor_tensor(oh[:, k, :, :], iota[:, 0:E].unsqueeze(2).to_broadcast([P, E, T]),
                                            top_i[:, n, k, :].unsqueeze(1).to_broadcast([P, E, T]), ALU.is_equal)
                ins.then_inc(dve_step.sem, 1)
                dve.wait_ge(dve_step.sem, step.next())
                dve.tensor_tensor(occ[:, :, :], oh[:, 0, :, :], oh[:, 1, :, :], ALU.add).then_inc(occ_ready.sem, 1)
                dve.wait_ge(exp_made.sem, exp_made.after(n))
                dve.tensor_scalar(c[:, 0, :], c[:, 1, :], 1.0, None, ALU.add).then_inc(dve_step.sem, 1)
                dve.wait_ge(dve_step.sem, step.next())
                dve.reciprocal(c[:, 0, :], c[:, 0, :]).then_inc(dve_step.sem, 1)
                dve.wait_ge(dve_step.sem, step.next())
                dve.tensor_tensor(c[:, 1, :], c[:, 1, :], c[:, 0, :], ALU.mult).then_inc(dve_step.sem, 1)
                dve.wait_ge(dve_step.sem, step.next())
                dve.wait_ge(rank_mm.sem, rank_mm.after(n))

                def flat(a):
                    return a[:, :, :].rearrange("p e t -> p (e t)")

                dve.tensor_copy(flat(tot), bank[1][:, 0:E * T]).then_inc(dve_step.sem, 1)
                dve.wait_ge(dve_step.sem, step.next())
                dve.tensor_tensor_scan(flat(incl), flat(keep), flat(tot), 0.0, ALU.mult, ALU.add)\
                    .then_inc(dve_step.sem, 1)
                dve.wait_ge(dve_step.sem, step.next())
                dve.tensor_tensor(flat(rank), flat(incl), flat(tot), ALU.subtract).then_inc(dve_step.sem, 1)
                dve.wait_ge(dve_step.sem, step.next())
                dve.tensor_tensor(flat(rank), flat(rank), bank[0][:, 0:E * T], ALU.add).then_inc(dve_step.sem, 1)
                dve.wait_ge(dve_step.sem, step.next())
                dve.tensor_scalar(load_e[:, :], incl[:, :, T - 1], 1.0 / P, None, ALU.mult).then_inc(dve_step.sem, 1)
                dve.wait_ge(dve_step.sem, step.next())
                dve.tensor_tensor(full[:, :, :], load_e[:, :].unsqueeze(2).to_broadcast([P, E, T]),
                                  iota[:, 0:T].unsqueeze(1).to_broadcast([P, E, T]), ALU.is_gt)\
                                      .then_inc(dve_step.sem, 1)
                dve.wait_ge(dve_step.sem, step.next())
                dve.tensor_reduce(tiles_e[:, :], full[:, :, :], AX.X, ALU.add).then_inc(dve_step.sem, 1)
                dve.wait_ge(dve_step.sem, step.next())
                dve.tensor_tensor_scan(end_e[:, :], ones_e[:, :], tiles_e[:, :], 0.0, ALU.mult, ALU.add)\
                    .then_inc(dve_step.sem, 1)
                dve.wait_ge(dve_step.sem, step.next())
                dve.tensor_tensor(base_e[:, :], end_e[:, :], tiles_e[:, :], ALU.subtract).then_inc(dve_step.sem, 1)
                dve.wait_ge(dve_step.sem, step.next())
                dve.tensor_scalar(base_e[:, :], base_e[:, :], float(P), None, ALU.mult).then_inc(dve_step.sem, 1)
                dve.wait_ge(dve_step.sem, step.next())
                dve.tensor_tensor(rank[:, :, :], rank[:, :, :],
                                  base_e[:, :].unsqueeze(2).to_broadcast([P, E, T]), ALU.add)\
                                      .then_inc(dve_step.sem, 1)
                dve.wait_ge(dve_step.sem, step.next())
                for k in range(2):
                    dve.tensor_tensor(full[:, :, :], oh[:, k, :, :], rank[:, :, :], ALU.mult)\
                        .then_inc(dve_step.sem, 1)
                    dve.wait_ge(dve_step.sem, step.next())
                    dve.tensor_reduce(pos_f[:, k, :], full[:, :, :].rearrange("p e t -> p t e"), AX.X,
                                      ALU.add).then_inc(dve_step.sem, 1)
                    dve.wait_ge(dve_step.sem, step.next())
                dve.tensor_copy(pos[r][:, :, :], pos_f[:, :, :]).then_inc(dve_step.sem, 1)
                dve.wait_ge(dve_step.sem, step.next())
                dve.tensor_scalar(pa_i[:, :, :], pos[r][:, :, :], 7, None, ALU.logical_shift_right)
                dve.tensor_scalar(pb_i[:, :, :], pos[r][:, :, :], P - 1, None, ALU.bitwise_and)\
                    .then_inc(dve_step.sem, 1)
                dve.wait_ge(dve_step.sem, step.next())
                dve.tensor_copy(pa_f[:, :, :], pa_i[:, :, :])
                dve.tensor_copy(pb_f[:, :, :], pb_i[:, :, :]).then_inc(dve_step.sem, 1)
                dve.wait_ge(dve_step.sem, step.next())
                dve.tensor_tensor(ends[:, :, :], end_e[0:1, :].unsqueeze(1).to_broadcast([1, NT, E]),
                                  iota[0:1, 0:NT].unsqueeze(2).to_broadcast([1, NT, E]), ALU.is_le)\
                                      .then_inc(dve_step.sem, 1)
                dve.wait_ge(dve_step.sem, step.next())
                dve.tensor_reduce(ex_f[:, :], ends[:, :, :], AX.X, ALU.add).then_inc(dve_step.sem, 1)
                dve.wait_ge(dve_step.sem, step.next())
                dve.tensor_scalar(ex_f[:, :], ex_f[:, :], float(E - 1), None, ALU.min).then_inc(dve_step.sem, 1)
                dve.wait_ge(dve_step.sem, step.next())
                dve.tensor_copy(expert_of[r][:, :], ex_f[:, :]).then_inc(dve_step.sem, 1)
                dve.wait_ge(dve_step.sem, step.next())
                with dve.Fori(0, T // 2) as it:
                    for b in range(2):
                        t = it * 2 + b
                        dve.wait_ge(table_mm.sem, table_mm.room(t + n * T))
                        for k in range(2):
                            dve.tensor_scalar(row_oh[b][:, k, :], iota[:, :], pb_f[:, k, ds(t, 1)], None,
                                              ALU.is_equal)
                            ins = dve.tensor_scalar(tile_id[b][:, k, :], iota[:, 0:NT], pa_f[:, k, ds(t, 1)],
                                                    token_f[:, ds(t, 1)], ALU.is_equal, ALU.mult)
                        ins.then_inc(onehot_ready.sem, 1)
                dve.wait_ge(table_mm.sem, table_mm.after(T - 1 + n * T))
                dve.tensor_copy(ids[r][:, :], bank[2][:, 0:NT]).then_inc(routed.sem, 1)

            dve.memset(ones_e[:, :], 1.0)
            dve.memset(keep[:, :, :], 1.0).then_inc(dve_step.sem, 1)
            dve.wait_ge(dve_step.sem, step.next())
            dve.memset(keep[:, :, 0:1], 0.0).then_inc(dve_step.sem, 1)
            dve.wait_ge(dve_step.sem, step.next())
            routing(0)
            dve.wait_ge(routed.sem, routed.after(0))
            routing(1)

            def expert_copies(r):
                n = phase[r]
                with dve.Fori(0, NT // 2) as it:
                    for b in range(2):
                        i = it * 2 + b
                        dve.wait_ge(n.y_mm.sem, n.y_mm.after(i))
                        dve.wait_ge(n.y_stored[b].sem, n.y_stored[b].sent(it))
                        dve.tensor_copy(y_s[b][:, 512:1024], bank[5 + 2 * b][:, :]).then_inc(n.y1_ready.sem, 1)

            expert_copies("gate")
            for b in range(2):
                dve.wait_ge(phase["gate"].y_stored[b].sem, phase["gate"].y_stored[b].landed(NT // 2 - 1))
            expert_copies("up")

            def inner(t, b, logits_before):
                dve.wait_ge(c_y0.sem, c_y0.after(t))
                dve.scalar_tensor_tensor(out=part, in0=in4[b][1], scalar=comb["gate"][:, 1, ds(t, 1)], in1=part,
                                         op0=ALU.mult, op1=ALU.add).then_inc(c_g.sem, 1)
                dve.wait_ge(c_z0.sem, c_z0.after(t))
                dve.scalar_tensor_tensor(out=upart, in0=in4[b][3], scalar=comb["up"][:, 1, ds(t, 1)],
                                         in1=upart, op0=ALU.mult, op1=ALU.add).then_inc(dve_step.sem, 1)
                dve.wait_ge(dve_step.sem, step.next())
                if logits_before:
                    inner_top(t - 1)
                dve.wait_ge(c_h.sem, c_h.after(t))
                dve.tensor_tensor(in4[b][1], in4[b][0], upart, ALU.mult).then_inc(c_done.sem, 1)

            def inner_top(t):
                dve.wait_ge(c_log_mm.sem, c_log_mm.after(t))
                dve.tensor_copy(lg[:, 0, 0, :], bank[2][:, 0:E]).then_inc(dve_step.sem, 1)
                dve.wait_ge(dve_step.sem, step.next())
                dve.sem_inc(c_lg.sem, 1)
                pick_two(1, 1, lambda table, got, j: dve.tensor_copy(table[:, 2, :, ds(t, 1)],
                                                                    got[:, 0, 0, 0:2].unsqueeze(2)))

            inner(0, 0, False)
            with dve.Fori(0, T // 2 - 1) as it:
                step.enter(it, 10)
                inner(it * 2 + 1, 1, True)
                inner(it * 2 + 2, 0, True)
            step.leave(T // 2 - 1)
            inner(T - 1, 1, True)
            inner_top(T - 1)
            routing(2)
            with dve.Fori(0, T // 2) as it:
                for b in range(2):
                    t = it * 2 + b
                    dve.wait_ge(o_y0.sem, o_y0.after(t))
                    dve.scalar_tensor_tensor(out=part[:, 0:D], in0=in2[b][1], scalar=comb["down"][:, 1, ds(t, 1)],
                                             in1=part[:, 0:D], op0=ALU.mult, op1=ALU.add).then_inc(o_sum.sem, 1)
                    dve.wait_ge(o_sum.sem, o_sum.after(t))
                    dve.wait_ge(o_stored[b].sem, o_stored[b].sent(it))
                    dve.tensor_tensor(out_s[b], part[:, 0:D], tile_of(t), ALU.add).then_inc(o_ready.sem, 1)


def buckets_of_pairs():
    n = np.arange(G)[None, :] - np.arange(G)[:, None]
    half = BUCKETS // 2
    exact = half // 2
    size = np.abs(n)
    ratio = np.log(np.maximum(size, 1).astype(np.float32) / np.float32(exact)) / np.float32(np.log(128 / exact))
    large = np.minimum(exact + (ratio * np.float32(half - exact)).astype(np.int32), half - 1)
    bucket = np.where(n < 0, half, 0) + np.where(size < exact, size, large)
    return np.concatenate([bucket, bucket]).astype(np.float32)


def kernel(**inputs):
    import concourse.bacc as bacc
    from concourse.bass_utils import run_bass_kernel_spmd

    a = {k: np.asarray(v) for k, v in inputs.items()}
    c = np.ascontiguousarray

    def columns(v, k):
        return c(v.reshape(k, P).T)

    def experts_in(w, kc):
        n_out = w.shape[1]
        return c(w.transpose(2, 0, 1).reshape(kc, P, E, n_out).transpose(1, 2, 0, 3).reshape(P, -1))

    arrays = {
        "x": a["L0_attn_x"].reshape(TOK, D), "ln_g": columns(a["L0_attn_ln_g"], KD),
        "ln_b": columns(a["L0_attn_ln_b"], KD), "w_h": a["L0_attn_W_h"], "bh_value": a["L0_attn_b_h"][:HID],
        "bh_gate": columns(a["L0_attn_b_h"][HID:], KH), "w_qk": a["L0_attn_W_qk"],
        "b_qk": columns(a["L0_attn_b_qk"], 1), "os_gamma": a["L0_attn_os_gamma"].T,
        "os_beta": a["L0_attn_os_beta"].T, "rel_emb": a["L0_attn_rel_emb"].reshape(-1), "w_out": a["L0_attn_W_out"],
        "b_out": a["L0_attn_b_out"], "r_gate": a["L0_ffn_router_gate"].T,
        "w_gate": experts_in(a["L0_ffn_w_gate"], KD), "r_up": a["L0_ffn_router_up"].T,
        "w_up": experts_in(a["L0_ffn_w_up"], KD), "r_down": a["L0_ffn_router_down"].T,
        "w_down": experts_in(a["L0_ffn_w_down"], KI), "buckets": buckets_of_pairs(),
    }
    arrays = {f"in_{k}": c(v) for k, v in arrays.items()}
    nc = bacc.Bacc("TRN2", target_bir_lowering=False, num_devices=1)
    args = [nc.dram_tensor(k, v.shape, mybir.dt.from_np(v.dtype), kind="ExternalInput").ap()
            for k, v in arrays.items()]
    out = nc.dram_tensor("out", (TOK, D), F32, kind="ExternalOutput").ap()
    block_kernel(nc, *args, out)
    r = run_bass_kernel_spmd(nc, [arrays], core_ids=[0])
    return r.results[0]["out"].reshape(1, TOK, D)
```

```python
from contextlib import ExitStack

import numpy as np

import concourse.bass as bass
from concourse import mybir

F32 = mybir.dt.float32
BF16 = mybir.dt.bfloat16
I32 = mybir.dt.int32
U32 = mybir.dt.uint32
ALU = mybir.AluOpType
ACT = mybir.ActivationFunctionType
AX = mybir.AxisListType
ds = bass.ds

P = 128
TOK = 4096
D = 256
HID = 512
G = 64
E = 8
INNER = 1024
T = TOK // P
KD = D // P
KI = INNER // P
SLAB = D * INNER // P
KH = HID // P
SUB = 4
M = T // SUB
MT = SUB * P
H = T // 2
B = 4
EPS = 1e-5
BUCKETS = 32
SIM_SCALE = 1.0 / G
BIAS_SCALE = float(P) ** 0.5
OFF_GROUP = -1.0e30


class Route:

    def __init__(self, n, matrix, column, first, tiles, batches_before):
        self.n, self.matrix, self.column, self.first, self.tiles = n, matrix, column, first, tiles
        self.nt = 2 * tiles + E
        self.batches_before = batches_before


class Group:

    def __init__(self, n, *routes):
        self.n, self.routes, self.matrix, self.column = n, routes, routes[0].matrix, routes[0].column
        self.tiles, self.nt, self.count = routes[0].tiles, routes[0].nt, len(routes)
        self.at = slice(routes[0].first, routes[0].first + self.count * self.tiles)
        self.words = self.count * E * self.tiles
        for k, r in enumerate(routes):
            r.group, r.tiles_before = self, k * self.nt


GATE = Route(0, "gate", 0, 0, T, 0)
UP = [Route(1 + h, "up", 1, h * H, H, (T + h * H) // B) for h in range(2)]
DOWN = [Route(3 + h, "down", 2, h * H, H, (2 * T + h * H) // B) for h in range(2)]
ROUTES = (GATE, *UP, *DOWN)
GROUPS = (Group(0, GATE), Group(1, *UP), Group(2, DOWN[0]), Group(3, DOWN[1]))
BODY = 10


class Steps:

    def __init__(self):
        self.base, self.n = 0, 0

    def next(self):
        self.n += 1
        return self.base + self.n

    def enter(self, turn, per):
        self.outer, self.per = self.base + self.n, per
        self.base, self.n = turn * per + self.outer, 0

    def leave(self, turns):
        assert self.n == self.per, (self.n, self.per)
        self.base, self.n = self.outer + turns * self.per, 0


class Signal:

    def __init__(self, ctx, nc, name, credits=0):
        self.sem, self.credits = ctx.enter_context(nc.semaphore(name)), credits

    def after(self, n):
        return n + (1 + self.credits)

    def room(self, n):
        return n + 1

    def landed(self, turn, each=16):
        return turn * each + (each + self.credits)

    def sent(self, turn):
        return turn * 16 + 16


def block_kernel(nc, x_in, ln_g, ln_b, w_h, bh_value, bh_gate, w_qk, b_qk, os_gamma, os_beta, rel_emb, w_out,
                 b_out, r_gate, w_gate, r_up, w_up, r_down, w_down, bucket_in, out):
    with ExitStack() as ctx:
        def sb(name, shape, dt=F32):
            return ctx.enter_context(nc.sbuf_tensor(name, shape, dt))

        def sig(name, credits=0):
            return Signal(ctx, nc, name, credits)

        def dram(name, shape):
            return nc.dram_tensor(name, shape, F32, kind="Internal").ap()

        gate_d = dram("gate_d", [M * P, KH * MT])
        v_d = dram("v_d", [M * P, SUB * HID])
        x2_d = dram("x2_d", [TOK, D])
        inter_d = [dram(f"inter_d{h}", [H * P, INNER]) for h in range(2)]
        sorted_d = {r: dram(f"sorted{r.n}", [r.nt * P, D if r.matrix == "down" else INNER]) for r in ROUTES}

        bank = [ctx.enter_context(nc.psum_tensor(f"bank{i}", [P, 512], F32)) for i in range(8)]

        x_sb = sb("x_sb", [P, T, D])
        ident = sb("ident", [P, P])
        before = sb("before", [P, P])
        ones = sb("ones", [P, P])
        zeros = sb("zeros", [P, P])
        iota = sb("iota", [P, P])
        iota_i = sb("iota_i", [P, P], I32)
        iota_h = sb("iota_h", [P, P], BF16)
        part_i, part = sb("part_i", [P, 1], I32), sb("part", [P, 1])
        start_i = sb("start_i", [P, T, 2], I32)
        start_h = sb("start_h", [P, T, 2], BF16)
        mean, var, rstd, rstd12 = (sb(n, [P, T]) for n in ("mean", "var", "rstd", "rstd12"))
        root_in, root, corr = (sb(n, [P, T]) for n in ("root_in", "root", "corr"))
        stats = sb("stats", [P, T // 4, 6])
        mv = sb("mv", [P, T // 4, 2])
        root4_in, root4, rstd4, corr4 = (sb(n, [P, SUB]) for n in ("root4_in", "root4", "rstd4", "corr4"))
        g_col, b_col = sb("g_col", [P, KD]), sb("b_col", [P, KD])
        bqk_col, bgate_col = sb("bqk_col", [P, 1]), sb("bgate_col", [P, KH])
        gamma_col, beta_col = sb("gamma_col", [P, 4]), sb("beta_col", [P, 4])
        rt_sb = sb("rt_sb", [P, KD, 2 * E])
        rd_sb = sb("rd_sb", [P, KI, E])
        top_v = sb("top_v", [P, 3, 2, T])
        top_i = sb("top_i", [P, 3, 2, T])
        comb = {m: sb(f"comb_{m}", [P, 2, T]) for m in ("gate", "up", "down")}
        pos = {m: sb(f"pos_{m}", [P, T, 2], I32) for m in ("gate", "up", "down")}
        id_f = sb("id_f", [P, GATE.nt])
        ids = {r: sb(f"ids{r.n}", [P, r.nt], I32) for r in ROUTES}
        expert_of = {g: sb(f"expert_of{g.n}", [1, g.count * g.nt], I32) for g in GROUPS}
        run_counts = sb("run_counts", [1, E], I32)
        lg = sb("lg", [P, SUB, 2, E])
        mx = sb("mx", [P, SUB, 2, 8])
        mi = sb("mi", [P, SUB, 2, 8], U32)
        idx_s = [sb(f"idx_s{b}", [P, 1], I32) for b in range(5)]
        idx2 = [sb(f"idx2_{b}", [P, 2], I32) for b in range(4)]
        idx4 = [sb(f"idx4_{b}", [P, 4], I32) for b in range(2)]
        ET = E * T
        oh = [[sb(f"oh{n}{k}", [P, ET]) for k in range(2)] for n in range(2)]
        occ, tot, within = ([sb(f"{w}{n}", [P, ET]) for n in range(2)] for w in ("occ", "tot", "within"))
        keep, keep_half, incl, rank, full = (sb(n, [P, ET]) for n in ("keep", "keep_half", "incl", "rank", "full"))
        tiles_e, end_e, base_e, restart_e, load_e = (sb(n, [P, 2 * E]) for n in (
            "tiles_e", "end_e", "base_e", "restart_e", "load_e"))
        pos_f = sb("pos_f", [P, T, 2])
        pa_h, pb_h = sb("pa_h", [P, T, 2], BF16), sb("pb_h", [P, T, 2], BF16)
        pa_i, pb_i = sb("pa_i", [P, T, 2], I32), sb("pb_i", [P, T, 2], I32)
        ex_f = sb("ex_f", [1, 2 * UP[0].nt])

        WORDS = 36900
        arena = sb("arena", [P, WORDS])
        used = [0]

        def cut(*shape):
            n = int(np.prod(shape))
            a = arena[:, used[0]:used[0] + n]
            used[0] += n
            assert used[0] <= WORDS, used[0]
            if len(shape) == 1:
                return a
            names = "abc"[:len(shape)]
            return a.rearrange(f"p ({' '.join(names)}) -> p {' '.join(names)}", **dict(zip(names, shape)))

        wh_sb = cut(KD, 2 * HID)
        wqk_sb = cut(KD, P)
        wo_sb = cut(KH, D)
        bv_row = cut(HID)
        bo_row = cut(D)
        emb_row = cut(BUCKETS)
        buckets = cut(G)
        bias_oh = cut(G, BUCKETS)
        bias_t = cut(P)
        attn_t = cut(T, P)
        linq_t = cut(TOK)
        v_st = [cut(SUB, HID) for _ in range(2)]
        assert used[0] >= E * KD * INNER
        xh = cut(SUB, D)
        xn_s = cut(SUB, D)
        nt_s = [cut(KD, MT) for _ in range(2)]
        x2t_s = cut(KD, MT)
        qk_t, quad_q = x2t_s[:, 0, :], x2t_s[:, 1, :]
        quad_k, lin_k = (cut(MT) for _ in range(2))
        link_n = cut(SUB, P)
        v_tmp = cut(2, HID)
        gate_st = [cut(KH, MT) for _ in range(2)]
        lin_kv = cut(HID)
        sim_s = cut(SUB, P)
        proj_s = cut(SUB, D)
        gated = [nt_s[c // 2][:, c % 2, :] for c in range(KH)]
        x2h = xh

        used[0] = 0
        w_sb = cut(E * SLAB)
        ring = cut(5 * INNER)
        rows_in = [ring[:, b * D:(b + 1) * D] for b in range(5)]
        rows_down = [ring[:, b * INNER:(b + 1) * INNER] for b in range(5)]
        onehots = ring[:, 5 * D:]
        row_words, tile_words = B * P, 2 * B * GATE.nt
        row_oh = [onehots[:, b * row_words:(b + 1) * row_words].bitcast(BF16).rearrange("p (t q) -> p t q", t=2 * B)
                  for b in range(2)]
        tile_oh = [onehots[:, 2 * row_words + b * tile_words:2 * row_words + (b + 1) * tile_words].bitcast(BF16)
                   for b in range(2)]
        ends = onehots[0:1, 2 * (row_words + tile_words):]
        rows_t = [cut(INNER) for _ in range(2)]
        y_s = [cut(INNER) for _ in range(2)]
        in4 = [[cut(INNER) for _ in range(4)] for _ in range(2)]
        inter_t = cut(INNER)
        inter = [cut(INNER) for _ in range(2)]
        in2 = [[in4[b // 2][b % 2 * 2 + k][:, 0:D] for k in range(2)] for b in range(4)]
        out_s = [inter[b // 2][:, b % 2 * D:(b % 2 + 1) * D] for b in range(4)]

        dve_step, pool_step = sig("vector_step"), sig("pool_step")
        x_loaded = [sig(f"x_loaded{c}") for c in range(4)]
        consts_loaded, consts_made = sig("consts_loaded"), sig("consts_made")
        buckets_loaded, bucket_oh, emb_chosen = sig("buckets_loaded"), sig("bucket_oh"), sig("emb_chosen")
        root_asked, root_made = sig("root_asked"), sig("root_made")
        exp_asked, exp_made = sig("exp_asked"), sig("exp_made")
        xh_ready, xt_mm, nt_ready = sig("xh_ready"), sig("xt_mm"), sig("nt_ready", 1)
        qk_mm, qkt_ready = sig("qk_mm"), sig("qkt_ready")
        quad_ready, link_ready, linq_ready = sig("quad_ready", 1), sig("link_ready", 1), sig("linq_ready")
        gate_mm, gate_ready = sig("gate_mm"), sig("gate_ready", 2)
        v_mm, v_biased, v_ready = sig("v_mm", 8), sig("v_biased", 2), sig("v_ready", 2)
        sim_mm, sim_read = sig("sim_mm", 1), sig("sim_read", 1)
        linkt_mm, linkn_ready = sig("linkt_mm", 1), sig("linkn_ready")
        kv_mm, kv_used = sig("kv_mm", 2), sig("kv_used", 1)
        gate_stored, v_stored = ([sig(f"{n}_stored{b}", 16) for b in range(2)] for n in ("gate", "v"))
        kv_final = sig("kv_final")
        gate_back, v_back = ([sig(f"{n}_back{b}") for b in range(2)] for n in ("gate", "v"))
        mix_mm, gated_ready = sig("mix_mm", 8), sig("gated_ready", 8)
        proj_mm, proj_used = sig("proj_mm", 2), sig("proj_used", 2)
        xn_ready, x1_ready = sig("xn_ready"), sig("x1_ready", 1)
        root4_asked, root4_made = sig("root4_asked"), sig("root4_made")
        x2_ready, x2t_mm, x2t_ready = sig("x2_ready"), sig("x2t_mm", 1), sig("x2t_ready", 1)
        x2_stored = sig("x2_stored", 16)
        logit_mm, lg_ready = sig("logit_mm", 1), sig("lg_ready", 1)
        occ_ready, rank_mm = sig("occ_ready"), sig("rank_mm")
        onehot_ready, table_mm, routed = sig("onehot_ready"), sig("table_mm", 2), sig("routed")
        w_landed, w_ready = sig("w_landed"), sig("w_ready")

        class Phase:

            def __init__(self, r):
                self.ring = 4 if r is GATE else 5
                self.idx_ready = sig(f"idx_ready{r.n}")
                self.gathered = [sig(f"gathered{r.n}_{b}") for b in range(self.ring)]
                self.xt_mm = sig(f"xt_mm{r.n}", self.ring)
                self.xt_ready = sig(f"xt_ready{r.n}", 2)
                self.half_ready = sig(f"half_ready{r.n}", 2)
                self.y_mm = sig(f"y_mm{r.n}", 2)
                self.y0_ready = sig(f"y0_ready{r.n}", 2)
                self.y_stored = [sig(f"y_stored{r.n}_{b}", 16) for b in range(2)]

        phase = {r: Phase(r) for r in ROUTES}
        c_idx, c_got = sig("c_idx"), [sig(f"c_got{b}") for b in range(2)]
        c_y0, c_z0, c_g, c_h, c_done = sig("c_y0"), sig("c_z0"), sig("c_g"), sig("c_h"), sig("c_done", 2)
        c_u = sig("c_u")
        c_t_mm, c_t_ready, c_log_mm, c_lg = sig("c_t_mm", 2), sig("c_t_ready", 1), sig("c_log_mm", 1), sig("c_lg", 1)
        c_stored = [sig(f"c_stored{b}", 16) for b in range(2)]
        o_idx, o_got = sig("o_idx"), [sig(f"o_got{b}") for b in range(4)]
        o_y0, o_sum, o_ready = sig("o_y0"), sig("o_sum"), sig("o_ready", 4)
        o_stored = [sig(f"o_stored{b}", 16) for b in range(4)]

        def give(eng, *signals):
            for s in signals:
                eng.sem_inc(s.sem, s.credits)

        waited = {}

        def alone(eng):
            if eng not in waited:
                waited[eng] = sig(f"waited{len(waited)}")
            eng.sem_inc(waited[eng].sem, 1)

        GATHERS, FIRST_PARTS, SECOND_PARTS = (1, 3, 6, 8), (0, 2, 5, 7), (2, 4, 7, 9)
        AHEAD = 4

        CONSTS = 15

        block = ctx.enter_context(nc.Block())

        @block.sync
        def _(sp):
            give(sp, *gate_stored, *v_stored, *c_stored, *o_stored)
            x_v = x_in.rearrange("(t p) d -> p t d", p=P)
            for c in range(4):
                sp.dma_start(x_sb[:, c * 8:(c + 1) * 8, :], x_v[:, c * 8:(c + 1) * 8, :])\
                    .then_inc(x_loaded[c].sem, 16)

            def flat(a):
                return a.rearrange("p a b -> p (a b)")

            with sp.Fori(0, M // 2) as it:
                for b in range(2):
                    m = it * 2 + b
                    sp.wait_ge(gate_ready.sem, gate_ready.after(m * KH + KH - 1))
                    sp.dma_start(gate_d[ds(m * P, P), :], flat(gate_st[b])).then_inc(gate_stored[b].sem, 16)
                    sp.wait_ge(v_ready.sem, v_ready.after(m * SUB + SUB - 1))
                    sp.dma_start(v_d[ds(m * P, P), :], flat(v_st[b])).then_inc(v_stored[b].sem, 16)
            for b in range(2):
                sp.wait_ge(gate_stored[b].sem, gate_stored[b].landed(M // 2 - 1))
                sp.wait_ge(v_stored[b].sem, v_stored[b].landed(M // 2 - 1))
            sp.wait_ge(kv_mm.sem, kv_mm.after(M - 1))
            with sp.Fori(0, M // 2) as it:
                for b in range(2):
                    m = it * 2 + b
                    sp.wait_ge(gated_ready.sem, gated_ready.room(m * KH + KH - 1))
                    sp.dma_start(flat(gate_st[b]), gate_d[ds(m * P, P), :]).then_inc(gate_back[b].sem, 16)
                    sp.wait_ge(mix_mm.sem, mix_mm.room(m * KH + KH - 1))
                    sp.dma_start(flat(v_st[b]), v_d[ds(m * P, P), :]).then_inc(v_back[b].sem, 16)
            sp.wait_ge(proj_mm.sem, proj_mm.after(2 * M - 1))
            sp.wait_ge(proj_used.sem, proj_used.after(2 * M - 1))

            def load_expert(e, w):
                sp.dma_start(w_sb[:, ds(e * SLAB, SLAB)], w[:, ds(e * SLAB, SLAB)]).then_inc(w_landed.sem, 16)

            with sp.Fori(0, E) as e:
                load_expert(e, w_gate)
                sp.wait_ge(w_landed.sem, w_landed.landed(e))
                sp.sem_inc(w_ready.sem, 1)
            sp.wait_ge(routed.sem, routed.after(GATE.n))
            with sp.Fori(0, E) as e:
                products = sp.value_load(run_counts[0:1, ds(e, 1)], min_val=phase[GATE].y_mm.credits,
                                         max_val=GATE.nt + phase[GATE].y_mm.credits)
                sp.wait_ge(phase[GATE].y_mm.sem, products)
                load_expert(e, w_up)
                sp.wait_ge(w_landed.sem, w_landed.landed(e + E))
                sp.sem_inc(w_ready.sem, 1)
            for h in range(2):
                with sp.Fori(0, H // 2) as it:
                    for b in range(2):
                        t = it * 2 + b
                        sp.wait_ge(c_done.sem, c_done.after(t + h * H))
                        sp.dma_start(inter_d[h][ds(t * P, P), :], inter[b]).then_inc(c_stored[b].sem, 16)
                if h == 0:
                    sp.wait_ge(phase[UP[1]].y_mm.sem, phase[UP[1]].y_mm.after(UP[1].nt - 1))
                    with sp.Fori(0, E) as e:
                        load_expert(e, w_down)
                        sp.wait_ge(w_landed.sem, w_landed.landed(e + 2 * E))
                        sp.sem_inc(w_ready.sem, 1)
            with sp.Fori(0, T // 4) as it:
                for b in range(4):
                    t = it * 4 + b
                    sp.wait_ge(o_ready.sem, o_ready.after(t))
                    sp.dma_start(out[ds(t * P, P), :], out_s[b]).then_inc(o_stored[b].sem, 16)
            for b in range(4):
                sp.wait_ge(o_stored[b].sem, o_stored[b].landed(T // 4 - 1))
            for b in range(2):
                sp.wait_ge(c_stored[b].sem, c_stored[b].landed(T // 2 - 1))
                for r in ROUTES:
                    sp.wait_ge(phase[r].y_stored[b].sem, phase[r].y_stored[b].landed(r.nt // 2 - 1))

        @block.gpsimd
        def _(pool):
            give(pool, link_ready, x1_ready)
            step = Steps()

            pool.memset(ident[:, :], 0.0).then_inc(pool_step.sem, 1)
            pool.wait_ge(pool_step.sem, step.next())
            pool.memset(before[:, :], 1.0).then_inc(pool_step.sem, 1)
            pool.wait_ge(pool_step.sem, step.next())
            pool.memset(ones[:, :], 1.0).then_inc(pool_step.sem, 1)
            pool.wait_ge(pool_step.sem, step.next())
            pool.memset(zeros[:, :], 0.0).then_inc(pool_step.sem, 1)
            pool.wait_ge(pool_step.sem, step.next())
            pool.iota(iota_i[:, :], pattern=[[1, P]], base=0, channel_multiplier=0).then_inc(pool_step.sem, 1)
            pool.wait_ge(pool_step.sem, step.next())
            pool.iota(part_i[:, :], pattern=[[0, 1]], base=0, channel_multiplier=1).then_inc(pool_step.sem, 1)
            pool.wait_ge(pool_step.sem, step.next())
            pool.iota(start_i[:, :, :], pattern=[[P, T], [0, 2]], base=0,
                      channel_multiplier=0).then_inc(pool_step.sem, 1)
            pool.wait_ge(pool_step.sem, step.next())
            pool.affine_select(out=ident[:, :], in_=ident[:, :], compare_op=ALU.not_equal, fill=1.0,
                               base=0, pattern=[[-1, P]], channel_multiplier=1).then_inc(pool_step.sem, 1)
            pool.wait_ge(pool_step.sem, step.next())
            pool.affine_select(out=before[:, :], in_=before[:, :], compare_op=ALU.is_gt, fill=0.0,
                               base=0, pattern=[[1, P]], channel_multiplier=-1).then_inc(pool_step.sem, 1)
            pool.wait_ge(pool_step.sem, step.next())
            pool.tensor_copy(iota[:, :], iota_i[:, :]).then_inc(pool_step.sem, 1)
            pool.wait_ge(pool_step.sem, step.next())
            pool.tensor_copy(iota_h[:, :], iota_i[:, :]).then_inc(pool_step.sem, 1)
            pool.wait_ge(pool_step.sem, step.next())
            pool.tensor_copy(part[:, :], part_i[:, :]).then_inc(pool_step.sem, 1)
            pool.wait_ge(pool_step.sem, step.next())
            pool.tensor_copy(start_h[:, :, :], start_i[:, :, :]).then_inc(pool_step.sem, 1)
            pool.wait_ge(pool_step.sem, step.next())
            pool.sem_inc(consts_made.sem, 1)
            pool.wait_ge(consts_loaded.sem, 16 * CONSTS)
            pool.wait_ge(bucket_oh.sem, bucket_oh.after(0))
            pool.tensor_tensor(bias_oh, bias_oh, emb_row.unsqueeze(1).to_broadcast([P, G, BUCKETS]),
                               ALU.mult).then_inc(emb_chosen.sem, 1)
            with pool.Fori(0, M) as m:
                pool.wait_ge(qkt_ready.sem, qkt_ready.after(m))
                pool.wait_ge(linkt_mm.sem, linkt_mm.room(m))
                alone(pool)
                pool.tensor_scalar(lin_k, qk_t, gamma_col[:, 3:4], beta_col[:, 3:4], ALU.mult,
                                   ALU.add).then_inc(link_ready.sem, 1)
            with pool.Fori(0, M) as m:
                step.enter(m, 1)
                pool.wait_ge(xn_ready.sem, xn_ready.after(m))
                alone(pool)
                x_m = x_sb[:, ds(m * SUB, SUB), :]
                pool.tensor_tensor(xn_s, xn_s, x_m, ALU.add).then_inc(pool_step.sem, 1)
                pool.wait_ge(pool_step.sem, step.next())
                pool.wait_ge(proj_used.sem, proj_used.after(m * 2 + 1))
                alone(pool)
                pool.tensor_tensor(x_m, xn_s, proj_s, ALU.add).then_inc(x1_ready.sem, 1)
            step.leave(M)

            def indexed(a, k):
                return bass.IndirectOffsetOnAxis(ap=a[:, k:k + 1].bitcast(U32), axis=0)

            def gather_rows(r, i, b):
                n = phase[r]
                dst, source = (rows_down[b], inter_d[r.first // H]) if r.matrix == "down" else (rows_in[b], x2_d)
                pool.wait_ge(n.xt_mm.sem, n.xt_mm.room(i))
                pool.tensor_copy(idx_s[b][:, :], ids[r][:, ds(i, 1)]).then_inc(n.idx_ready.sem, 1)
                pool.wait_ge(n.idx_ready.sem, n.idx_ready.after(i))
                alone(pool)
                pool.indirect_dma_start(dst, None, source[:, :], indexed(idx_s[b], 0)).then_inc(n.gathered[b].sem, 16)

            def gather_products(t, b, h):
                pool.wait_ge(c_done.sem, c_done.room(t))
                pool.tensor_copy(idx4[b][:, 0:2], pos["gate"][:, ds(t, 1), :].rearrange("p a k -> p (a k)"))
                pool.tensor_copy(idx4[b][:, 2:4], pos["up"][:, ds(t, 1), :].rearrange("p a k -> p (a k)"))\
                    .then_inc(c_idx.sem, 1)
                pool.wait_ge(c_idx.sem, c_idx.after(t))
                alone(pool)
                for k in range(4):
                    pool.indirect_dma_start(in4[b][k], None, sorted_d[(GATE, UP[h])[k // 2]][:, :],
                                            indexed(idx4[b], k)).then_inc(c_got[b].sem, 16)

            def gather_outputs(r, t, b):
                pool.wait_ge(o_ready.sem, o_ready.room(t))
                pool.tensor_copy(idx2[b][:, :], pos["down"][:, ds(t, 1), :].rearrange("p a k -> p (a k)"))\
                    .then_inc(o_idx.sem, 1)
                pool.wait_ge(o_idx.sem, o_idx.after(t))
                alone(pool)
                for k in range(2):
                    pool.indirect_dma_start(in2[b][k], None, sorted_d[r][:, :], indexed(idx2[b], k))\
                        .then_inc(o_got[b].sem, 16)

            def products_stored(r):
                for b in range(2):
                    pool.wait_ge(phase[r].y_stored[b].sem, phase[r].y_stored[b].landed(r.nt // 2 - 1))

            pool.wait_ge(x2_stored.sem, x2_stored.landed(M - 1))
            pool.wait_ge(routed.sem, routed.after(GATE.n))
            with pool.Fori(0, GATE.nt // 4) as it:
                for b in range(4):
                    gather_rows(GATE, it * 4 + b, b)

            def gather_sorted(r, beside=None):
                def body(it, last):
                    for j in range(BODY):
                        if not last or j < BODY - AHEAD:
                            gather_rows(r, it * BODY + (j + AHEAD), (j + AHEAD) % 5)
                        if j in GATHERS and beside is not None:
                            beside(it, GATHERS.index(j), last)

                with pool.Fori(0, r.nt // BODY - 1) as it:
                    body(it, False)
                body(r.nt // BODY - 1, True)

            def first_rows(r, before):
                pool.wait_ge(routed.sem, routed.after(r.n))
                pool.wait_ge(phase[before].xt_mm.sem, phase[before].xt_mm.after(before.nt - 1))
                for i in range(AHEAD):
                    gather_rows(r, i, i)

            def products_beside(h):
                def gather(it, k, last):
                    if not last or k < 2:
                        gather_products(it * 4 + (h * H + 2 + k), k % 2, h)
                return gather

            first_rows(UP[0], GATE)
            gather_sorted(UP[0])
            first_rows(UP[1], UP[0])
            products_stored(GATE)
            products_stored(UP[0])
            for b in range(2):
                gather_products(b, b, 0)
            gather_sorted(UP[1], products_beside(0))
            products_stored(UP[1])
            for b in range(2):
                gather_products(H + b, b, 1)
            for b in range(2):
                pool.wait_ge(c_stored[b].sem, c_stored[b].landed(H // 2 - 1))
            first_rows(DOWN[0], UP[1])
            gather_sorted(DOWN[0], products_beside(1))
            for b in range(2):
                pool.wait_ge(c_stored[b].sem, c_stored[b].landed(T // 2 - 1))
            first_rows(DOWN[1], DOWN[0])
            products_stored(DOWN[0])
            gather_sorted(DOWN[1], lambda it, k, last: gather_outputs(DOWN[0], it * 4 + k, k))
            products_stored(DOWN[1])
            with pool.Fori(0, H // 4) as it:
                for b in range(4):
                    gather_outputs(DOWN[1], it * 4 + (H + b), b)

        @block.scalar
        def _(act):
            give(act, nt_ready, gate_ready, v_ready, x2t_ready, x2_stored, c_t_ready,
                 *(s for r in ROUTES for s in (phase[r].xt_ready, phase[r].y0_ready, *phase[r].y_stored)))

            def load(dst, src):
                act.dma_start(dst, src).then_inc(consts_loaded.sem, 16)

            act.dma_start(buckets, bucket_in).then_inc(buckets_loaded.sem, 16)
            load(wh_sb, w_h.rearrange("(k p) n -> p k n", p=P))
            load(wqk_sb, w_qk.rearrange("(k p) n -> p k n", p=P))
            load(wo_sb, w_out.rearrange("(k p) n -> p k n", p=P))
            load(g_col[:, :], ln_g)
            load(b_col[:, :], ln_b)
            load(bqk_col[:, :], b_qk)
            load(bgate_col[:, :], bh_gate)
            load(bv_row, bh_value.partition_broadcast(P))
            load(bo_row, b_out.partition_broadcast(P))
            load(emb_row, rel_emb.partition_broadcast(P))
            load(gamma_col[:, :], os_gamma)
            load(beta_col[:, :], os_beta)
            load(rt_sb[:, :, 0:E], r_gate.rearrange("(k p) n -> p k n", p=P))
            load(rt_sb[:, :, E:2 * E], r_up.rearrange("(k p) n -> p k n", p=P))
            load(rd_sb[:, :, :], r_down.rearrange("(k p) n -> p k n", p=P))
            roots = [0]

            def square_root():
                act.wait_ge(root_asked.sem, root_asked.after(roots[0]))
                act.activation(root[:, :], root_in[:, :], ACT.Sqrt).then_inc(root_made.sem, 1)
                roots[0] += 1

            def exponential(n):
                act.wait_ge(exp_asked.sem, exp_asked.after(n))
                c, at = comb[GROUPS[n].matrix], GROUPS[n].at
                act.activation(c[:, 1, at], c[:, 0, at], ACT.Exp).then_inc(exp_made.sem, 1)

            square_root()
            square_root()
            act.wait_ge(consts_loaded.sem, 16 * CONSTS)
            with act.Fori(0, M // 2) as it:
                for b in range(2):
                    m = it * 2 + b
                    act.wait_ge(xt_mm.sem, xt_mm.after(m))
                    act.wait_ge(v_mm.sem, v_mm.room(m * SUB + SUB - 1))
                    for k in range(KD):
                        ins = act.activation(nt_s[b][:, k, :], bank[k][:, :], ACT.Identity, bias=b_col[:, k:k + 1],
                                             scale=g_col[:, k:k + 1])
                    ins.then_inc(nt_ready.sem, 1)
                    act.wait_ge(qk_mm.sem, qk_mm.after(m))
                    act.wait_ge(quad_ready.sem, quad_ready.room(m))
                    act.wait_ge(link_ready.sem, link_ready.room(m))
                    act.activation(qk_t, bank[2][:, :], ACT.Silu, bias=bqk_col[:, :]).then_inc(qkt_ready.sem, 1)
                    act.wait_ge(qkt_ready.sem, qkt_ready.after(m))
                    act.activation(linq_t[:, ds(m * MT, MT)], qk_t, ACT.Identity, bias=beta_col[:, 1:2],
                                   scale=gamma_col[:, 1:2]).then_inc(linq_ready.sem, 1)
                    act.wait_ge(gate_stored[b].sem, gate_stored[b].sent(it))
                    for c in range(KH):
                        act.wait_ge(gate_mm.sem, gate_mm.after(m * KH + c))
                        act.activation(gate_st[b][:, c, :], bank[3 + c % 2][:, :], ACT.Silu,
                                       bias=bgate_col[:, c:c + 1]).then_inc(gate_ready.sem, 1)
                    act.wait_ge(v_stored[b].sem, v_stored[b].sent(it))
                    act.wait_ge(kv_mm.sem, kv_mm.room(m))
                    for s in range(SUB):
                        act.wait_ge(v_biased.sem, v_biased.after(m * SUB + s))
                        act.activation(v_st[b][:, s, :], v_tmp[:, s % 2, :], ACT.Silu).then_inc(v_ready.sem, 1)
            with act.Fori(0, M) as m:
                act.wait_ge(root4_asked.sem, root4_asked.after(m))
                act.activation(root4[:, :], root4_in[:, :], ACT.Sqrt).then_inc(root4_made.sem, 1)
                act.wait_ge(x2_ready.sem, x2_ready.after(m))
                act.dma_start(x2_d[ds(m * MT, MT), :].rearrange("(s p) d -> p s d", p=P), x2h)\
                    .then_inc(x2_stored.sem, 16)
                act.wait_ge(x2t_mm.sem, x2t_mm.after(m))
                act.wait_ge(logit_mm.sem, logit_mm.room(m))
                for k in range(KD):
                    ins = act.activation(x2t_s[:, k, :], bank[6 + k][:, :], ACT.Copy)
                ins.then_inc(x2t_ready.sem, 1)
            exponential(0)
            exponential(1)

            def turned(r, i, j):
                n = phase[r]
                act.wait_ge(n.xt_mm.sem, n.xt_mm.after(i))
                act.wait_ge(n.y_mm.sem, n.y_mm.room(i))
                w = 512 if r.matrix == "down" else D
                act.activation(rows_t[j % 2][:, 0:w], bank[2 * (j % 2)][:, 0:w], ACT.Copy).then_inc(n.xt_ready.sem, 1)

            def copied(r, i, j, turn):
                n = phase[r]
                act.wait_ge(n.y_mm.sem, n.y_mm.after(i))
                act.wait_ge(n.y_stored[j % 2].sem, n.y_stored[j % 2].sent(turn))
                w = D if r.matrix == "down" else 512
                act.activation(y_s[j % 2][:, 0:w], bank[4 + 2 * (j % 2)][:, 0:w], ACT.Copy)\
                    .then_inc(n.y0_ready.sem, 1)
                act.wait_ge(n.y0_ready.sem, n.y0_ready.after(i))
                if r.matrix != "down":
                    act.wait_ge(n.half_ready.sem, n.half_ready.after(i))
                y = y_s[j % 2][:, 0:D] if r.matrix == "down" else y_s[j % 2]
                act.dma_start(sorted_d[r][ds(i * P, P), :], y).then_inc(n.y_stored[j % 2].sem, 16)

            def sorted_tiles(r, beside=None):
                def body(it, last):
                    for j in range(BODY):
                        if not last or j < BODY - 1:
                            turned(r, it * BODY + j + 1, j + 1)
                        if beside is not None:
                            beside(it, j)
                        copied(r, it * BODY + j, j, it * (BODY // 2) + j // 2)

                turned(r, 0, 0)
                with act.Fori(0, r.nt // BODY - 1) as it:
                    body(it, False)
                body(r.nt // BODY - 1, True)

            def products_out(r):
                for b in range(2):
                    act.wait_ge(phase[r].y_stored[b].sem, phase[r].y_stored[b].landed(r.nt // 2 - 1))

            turned(GATE, 0, 0)
            with act.Fori(0, GATE.nt // 4 - 1) as it:
                for j in range(4):
                    turned(GATE, it * 4 + j + 1, j + 1)
                    copied(GATE, it * 4 + j, j, it * 2 + j // 2)
            for j in range(4):
                i = GATE.nt - 4 + j
                if j < 3:
                    turned(GATE, i + 1, j + 1)
                copied(GATE, i, j, i // 2)

            def inner(t, b, turn):
                act.wait_ge(c_got[b].sem, c_got[b].landed(turn, 64))
                gate_0, up_0 = in4[b][0], in4[b][2]
                act.activation(gate_0, gate_0, ACT.Copy, scale=comb["gate"][:, 0, ds(t, 1)]).then_inc(c_y0.sem, 1)
                act.activation(up_0, up_0, ACT.Copy, scale=comb["up"][:, 0, ds(t, 1)]).then_inc(c_z0.sem, 1)
                act.wait_ge(c_g.sem, c_g.after(t))
                act.activation(gate_0, gate_0, ACT.Silu).then_inc(c_h.sem, 1)

            def inner_turned(t, first):
                act.wait_ge(c_t_mm.sem, c_t_mm.after(t))
                act.wait_ge(c_log_mm.sem, c_log_mm.room(t))
                for h in range(2):
                    ins = act.activation(inter_t[:, h * 512:(h + 1) * 512], bank[first + 2 * h][:, :], ACT.Copy)
                ins.then_inc(c_t_ready.sem, 1)

            def inner_beside(h, first):
                def part(it, j):
                    if j in FIRST_PARTS:
                        k = FIRST_PARTS.index(j)
                        inner(it * 4 + (h * H + k), k % 2, it * 2 + (h * H // 2 + k // 2))
                    if j in SECOND_PARTS:
                        inner_turned(it * 4 + (h * H + SECOND_PARTS.index(j)), first)
                return part

            def output(t, b, turn):
                act.wait_ge(o_got[b].sem, o_got[b].landed(turn, 32))
                act.activation(in2[b][0], in2[b][0], ACT.Copy,
                               scale=comb["down"][:, 0, ds(t, 1)]).then_inc(o_y0.sem, 1)

            def output_beside(it, j):
                if j in SECOND_PARTS:
                    k = SECOND_PARTS.index(j)
                    output(it * 4 + k, k, it)

            products_out(GATE)
            sorted_tiles(UP[0])
            products_out(UP[0])
            sorted_tiles(UP[1], inner_beside(0, 1))
            products_out(UP[1])
            exponential(2)
            sorted_tiles(DOWN[0], inner_beside(1, 5))
            products_out(DOWN[0])
            exponential(3)
            sorted_tiles(DOWN[1], output_beside)
            with act.Fori(0, H // 4) as it:
                for b in range(4):
                    output(it * 4 + (H + b), b, it + H // 4)

        @block.tensor
        def _(pe):
            give(pe, v_mm, sim_mm, linkt_mm, kv_mm, mix_mm, proj_mm, x2t_mm, logit_mm, table_mm, c_t_mm, c_log_mm,
                 *(s for r in ROUTES for s in (phase[r].xt_mm, phase[r].y_mm)))
            pe.wait_ge(consts_made.sem, consts_made.after(0))
            pe.wait_ge(consts_loaded.sem, 16 * CONSTS)

            def turn_rows(src, first):
                for k in range(KD):
                    for s in range(SUB):
                        ins = pe.transpose(bank[first + k][:, s * P:(s + 1) * P], src[:, s, k * P:(k + 1) * P],
                                           ident[:, :])
                return ins

            def transposes(m):
                pe.wait_ge(xh_ready.sem, xh_ready.after(m))
                pe.wait_ge(nt_ready.sem, nt_ready.room(m))
                turn_rows(xh, 0).then_inc(xt_mm.sem, 1)

            def projections(m, b):
                pe.wait_ge(nt_ready.sem, nt_ready.after(m))
                pe.wait_ge(sim_read.sem, sim_read.room(m))
                for k in range(KD):
                    ins = pe.matmul(bank[2][:, :], wqk_sb[:, k, :], nt_s[b][:, k, :], start=(k == 0),
                                    stop=(k == KD - 1))
                ins.then_inc(qk_mm.sem, 1)
                for c in range(KH):
                    pe.wait_ge(gate_ready.sem, gate_ready.room(m * KH + c))
                    for k in range(KD):
                        ins = pe.matmul(bank[3 + c % 2][:, :], wh_sb[:, k, HID + c * P:HID + (c + 1) * P],
                                        nt_s[b][:, k, :], start=(k == 0), stop=(k == KD - 1))
                    ins.then_inc(gate_mm.sem, 1)
                for s in range(SUB):
                    pe.wait_ge(v_biased.sem, v_biased.room(m * SUB + s))
                    for k in range(KD):
                        ins = pe.matmul(bank[5 + s % 2][:, :], nt_s[b][:, k, s * P:(s + 1) * P], wh_sb[:, k, 0:HID],
                                        start=(k == 0), stop=(k == KD - 1))
                    ins.then_inc(v_mm.sem, 1)

            def groups(m, b):
                pe.wait_ge(quad_ready.sem, quad_ready.after(m))
                pe.wait_ge(qkt_ready.sem, qkt_ready.after(m))
                for s in range(SUB):
                    c = slice(s * P, (s + 1) * P)
                    ins = pe.matmul(bank[2][:, c], quad_k[:, c], quad_q[:, c], start=True, stop=True)
                ins.then_inc(sim_mm.sem, 1)
                pe.wait_ge(link_ready.sem, link_ready.after(m))
                pe.wait_ge(kv_used.sem, kv_used.room(m))
                for s in range(SUB):
                    c = slice(s * P, (s + 1) * P)
                    ins = pe.transpose(bank[7][:, c], lin_k[:, c], ident[:, :])
                ins.then_inc(linkt_mm.sem, 1)
                pe.wait_ge(linkn_ready.sem, linkn_ready.after(m))
                pe.wait_ge(v_ready.sem, v_ready.after(m * SUB + SUB - 1))
                for s in range(SUB):
                    ins = pe.matmul(bank[7][:, :], link_n[:, s, :], v_st[b][:, s, :], start=(s == 0),
                                    stop=(s == SUB - 1))
                ins.then_inc(kv_mm.sem, 1)

            transposes(0)
            with pe.Fori(0, M // 2 - 1) as it:
                for b in range(2):
                    m = it * 2 + b
                    projections(m, b)
                    transposes(m + 1)
                    groups(m, b)
            for b in range(2):
                m = M - 2 + b
                projections(m, b)
                if b == 0:
                    transposes(m + 1)
                groups(m, b)

            pe.wait_ge(kv_final.sem, kv_final.after(0))
            pe.wait_ge(linq_ready.sem, linq_ready.after(M - 1))
            def mix(m, b, turn):
                pe.wait_ge(v_back[b].sem, v_back[b].landed(turn))
                for c in range(KH):
                    pe.wait_ge(gated_ready.sem, gated_ready.after(m * KH + c - KH))
                    pe.matmul(bank[c][:, :], lin_kv[:, c * P:(c + 1) * P], linq_t[:, ds(m * MT, MT)],
                              start=True, stop=False, skip_group_check=True)
                    for s in range(SUB):
                        ins = pe.matmul(bank[c][:, s * P:(s + 1) * P], v_st[b][:, s, c * P:(c + 1) * P],
                                        attn_t[:, ds(m * SUB + s, 1), :].rearrange("p a b -> p (a b)"),
                                        start=False, stop=(s == SUB - 1), skip_group_check=True)
                    ins.then_inc(mix_mm.sem, 1)

            def project(m):
                pe.wait_ge(gated_ready.sem, gated_ready.after(m * KH + KH - 1))
                for h in range(2):
                    pe.wait_ge(proj_used.sem, proj_used.room(m * 2 + h))
                    for s in (2 * h, 2 * h + 1):
                        for c in range(KH):
                            ins = pe.matmul(bank[4 + h][:, (s % 2) * D:(s % 2 + 1) * D],
                                            gated[c][:, s * P:(s + 1) * P], wo_sb[:, c, :], start=(c == 0),
                                            stop=(c == KH - 1))
                    ins.then_inc(proj_mm.sem, 1)

            def turn_x2(m):
                pe.wait_ge(x2_ready.sem, x2_ready.after(m))
                pe.wait_ge(lg_ready.sem, lg_ready.room(m))
                turn_rows(x2h, 6).then_inc(x2t_mm.sem, 1)

            def logits(m):
                pe.wait_ge(x2t_ready.sem, x2t_ready.after(m))
                for s in range(SUB):
                    for k in range(KD):
                        ins = pe.matmul(bank[6][:, s * 2 * E:(s + 1) * 2 * E], x2t_s[:, k, s * P:(s + 1) * P],
                                        rt_sb[:, k, :], start=(k == 0), stop=(k == KD - 1))
                ins.then_inc(logit_mm.sem, 1)

            mix(0, 0, 0)
            project(0)
            mix(1, 1, 0)
            project(1)
            turn_x2(0)
            with pe.Fori(0, M // 2 - 1) as it:
                for b in range(2):
                    m = it * 2 + b
                    mix(m + 2, b, it + 1)
                    logits(m)
                    project(m + 2)
                    turn_x2(m + 1)
            logits(M - 2)
            turn_x2(M - 1)
            logits(M - 1)

            def ranks(g, first):
                pe.wait_ge(occ_ready.sem, occ_ready.after(g.n))
                o = occ[g.n % 2][:, 0:g.words]
                pe.matmul(bank[first][:, 0:g.words], before[:, :], o, start=True, stop=True)
                pe.matmul(bank[first + 1][:, 0:g.words], ones[:, :], o, start=True, stop=True)\
                    .then_inc(rank_mm.sem, 1)

            def open_table(r, at):
                for part in range(2):
                    pe.matmul(bank[at][:, part * r.nt:(part + 1) * r.nt], zeros[:, :], zeros[:, 0:r.nt], start=True,
                              stop=False, skip_group_check=True)

            def add_to_table(r, batch, b, at):
                pe.wait_ge(onehot_ready.sem, onehot_ready.after(batch + r.batches_before))
                w = 2 * r.nt
                for k in range(2 * B):
                    ins = pe.matmul(bank[at][:, 0:w], row_oh[b][:, k, :], tile_oh[b][:, k * w:(k + 1) * w],
                                    start=False, stop=False, skip_group_check=True)
                ins.then_inc(table_mm.sem, 1)

            def table(r, at):
                open_table(r, at)
                with pe.Fori(0, r.tiles // B // 2) as it:
                    for b in range(2):
                        add_to_table(r, it * 2 + b, b, at)

            def turn(r, i, j, landing):
                n = phase[r]
                pe.wait_ge(n.gathered[j % n.ring].sem, n.gathered[j % n.ring].landed(landing))
                pe.wait_ge(n.xt_ready.sem, n.xt_ready.room(i))
                kc, rows = KD, rows_in
                if r.matrix == "down":
                    pe.wait_ge(n.half_ready.sem, n.half_ready.room(i))
                    kc, rows = KI, rows_down
                for k in range(kc):
                    ins = pe.transpose(bank[2 * (j % 2) + k // 4][:, (k % 4) * P:(k % 4 + 1) * P],
                                       rows[j % n.ring][:, k * P:(k + 1) * P], ident[:, :])
                ins.then_inc(n.xt_mm.sem, 1)

            def product(r, i, j):
                n = phase[r]
                e = pe.value_load(expert_of[r.group][0:1, ds(i + r.tiles_before, 1)], min_val=0, max_val=E - 1)
                pe.wait_ge(w_ready.sem, w_ready.after(e + r.column * E))
                pe.wait_ge(n.xt_ready.sem, n.xt_ready.after(i))
                kc, width = KD, INNER
                if r.matrix == "down":
                    kc, width = KI, D
                    pe.wait_ge(n.half_ready.sem, n.half_ready.after(i))
                pe.wait_ge(n.y0_ready.sem, n.y0_ready.room(i))
                if r.matrix != "down":
                    pe.wait_ge(n.half_ready.sem, n.half_ready.room(i))
                w = min(width, 512)
                for h in range(width // w):
                    for k in range(kc):
                        ins = pe.matmul(bank[4 + 2 * (j % 2) + h][:, 0:w], rows_t[j % 2][:, k * P:(k + 1) * P],
                                        w_sb[:, ds(e * SLAB + (k * width + h * w), w)],
                                        start=(k == 0), stop=(k == kc - 1))
                ins.then_inc(n.y_mm.sem, 1)

            ranks(GROUPS[0], 0)
            ranks(GROUPS[1], 2)
            table(GATE, 4)
            pe.wait_ge(routed.sem, routed.after(GATE.n))
            open_table(UP[0], 1)
            open_table(UP[1], 3)
            turn(GATE, 0, 0, 0)

            def gate_tiles(it):
                for j in range(4):
                    turn(GATE, it * 4 + j + 1, j + 1, it + (j + 1) // 4)
                    product(GATE, it * 4 + j, j)

            for h in range(2):
                with pe.Fori(0, H // B // 2) as it:
                    for half in range(2):
                        gate_tiles(it * 2 + (h * H // B + half))
                        add_to_table(UP[h], it * 2 + half, half, 1 + 2 * h)
            with pe.Fori(T // B, GATE.nt // 4 - 1) as it:
                gate_tiles(it)
            for j in range(4):
                if j < 3:
                    turn(GATE, GATE.nt - 4 + j + 1, j + 1, GATE.nt // 4 - 1)
                product(GATE, GATE.nt - 4 + j, j)

            def turn_inner(t, b, first):
                pe.wait_ge(c_done.sem, c_done.after(t))
                pe.wait_ge(c_lg.sem, c_lg.room(t))
                for k in range(KI):
                    ins = pe.transpose(bank[first + 2 * (k // 4)][:, (k % 4) * P:(k % 4 + 1) * P],
                                       inter[b][:, k * P:(k + 1) * P], ident[:, :])
                ins.then_inc(c_t_mm.sem, 1)

            def inner_logits(t, first):
                pe.wait_ge(c_t_ready.sem, c_t_ready.after(t))
                for k in range(KI):
                    ins = pe.matmul(bank[first][:, 0:E], inter_t[:, k * P:(k + 1) * P], rd_sb[:, k, :],
                                    start=(k == 0), stop=(k == KI - 1))
                ins.then_inc(c_log_mm.sem, 1)

            def sorted_tiles(r, inner_of=None, first=None):
                def body(it, last):
                    for j in range(BODY):
                        if not last or j < BODY - 1:
                            turn(r, it * BODY + j + 1, j + 1, it * 2 + (j + 1) // 5)
                        beside = j in SECOND_PARTS and inner_of is not None
                        if beside:
                            k = SECOND_PARTS.index(j)
                            turn_inner(it * 4 + (inner_of * H + k), k % 2, first)
                        product(r, it * BODY + j, j)
                        if beside:
                            inner_logits(it * 4 + (inner_of * H + k), first)

                turn(r, 0, 0, 0)
                with pe.Fori(0, r.nt // BODY - 1) as it:
                    body(it, False)
                body(r.nt // BODY - 1, True)

            def products_copied(r):
                pe.wait_ge(phase[r].y0_ready.sem, phase[r].y0_ready.after(r.nt - 1))
                if r.matrix != "down":
                    pe.wait_ge(phase[r].half_ready.sem, phase[r].half_ready.after(r.nt - 1))

            products_copied(GATE)
            pe.wait_ge(routed.sem, routed.after(UP[1].n))
            sorted_tiles(UP[0])
            products_copied(UP[0])
            sorted_tiles(UP[1], 0, 1)
            products_copied(UP[1])
            ranks(GROUPS[2], 0)
            table(DOWN[0], 4)
            pe.wait_ge(routed.sem, routed.after(DOWN[0].n))
            sorted_tiles(DOWN[0], 1, 5)
            products_copied(DOWN[0])
            ranks(GROUPS[3], 0)
            table(DOWN[1], 4)
            pe.wait_ge(routed.sem, routed.after(DOWN[1].n))
            sorted_tiles(DOWN[1])

        @block.vector
        def _(dve):
            give(dve, quad_ready, v_biased, sim_read, kv_used, gated_ready, proj_used, lg_ready, c_done, c_lg,
                 o_ready, *(phase[r].half_ready for r in ROUTES))
            step = Steps()
            for a, n in ((keep, T), (keep_half, H), (restart_e, E)):
                dve.memset(a[:, :], 1.0).then_inc(dve_step.sem, 1)
                dve.wait_ge(dve_step.sem, step.next())
                dve.memset(a[:, :].rearrange("p (e t) -> p e t", t=n)[:, :, 0:1], 0.0).then_inc(dve_step.sem, 1)
                dve.wait_ge(dve_step.sem, step.next())
            roots = [0]

            def inverse_root(dst, src):
                dve.tensor_scalar(root_in[:, :], src[:, :], EPS, None, ALU.add).then_inc(root_asked.sem, 1)
                dve.wait_ge(root_asked.sem, root_asked.after(roots[0]))
                dve.wait_ge(root_made.sem, root_made.after(roots[0]))
                roots[0] += 1
                dve.reciprocal(dst[:, :], root[:, :]).then_inc(dve_step.sem, 1)
                dve.wait_ge(dve_step.sem, step.next())
                dve.tensor_tensor(corr[:, :], root_in[:, :], dst[:, :], ALU.mult).then_inc(dve_step.sem, 1)
                dve.wait_ge(dve_step.sem, step.next())
                dve.tensor_tensor(corr[:, :], corr[:, :], dst[:, :], ALU.mult).then_inc(dve_step.sem, 1)
                dve.wait_ge(dve_step.sem, step.next())
                dve.tensor_scalar(corr[:, :], corr[:, :], -0.5, 1.5, ALU.mult, ALU.add).then_inc(dve_step.sem, 1)
                dve.wait_ge(dve_step.sem, step.next())
                dve.tensor_tensor(dst[:, :], dst[:, :], corr[:, :], ALU.mult).then_inc(dve_step.sem, 1)
                dve.wait_ge(dve_step.sem, step.next())

            def tile_of(t):
                return x_sb[:, ds(t, 1), :].rearrange("p a d -> p (a d)")

            def centred(dst, m, scale):
                for s in range(SUB):
                    t = m * SUB + s
                    ins = dve.tensor_scalar(dst[:, s, :], tile_of(t), mean[:, ds(t, 1)], scale[:, ds(t, 1)],
                                            ALU.subtract, ALU.mult)
                return ins

            for c in range(4):
                dve.wait_ge(x_loaded[c].sem, x_loaded[c].landed(0))
                n = T // 4
                for t in range(n):
                    ins = dve.bn_stats(stats[:, t, :], x_sb[:, c * n + t, :])
                ins.then_inc(dve_step.sem, 1)
                dve.wait_ge(dve_step.sem, step.next())
                alone(dve)
                for t in range(n):
                    ins = dve.bn_aggr(mv[:, t, :], stats[:, t, :])
                ins.then_inc(dve_step.sem, 1)
                dve.wait_ge(dve_step.sem, step.next())
                dve.tensor_copy(mean[:, c * n:(c + 1) * n], mv[:, :, 0])
                dve.tensor_copy(var[:, c * n:(c + 1) * n], mv[:, :, 1]).then_inc(dve_step.sem, 1)
                dve.wait_ge(dve_step.sem, step.next())
                if c == 0:
                    dve.wait_ge(buckets_loaded.sem, buckets_loaded.landed(0))
                    dve.wait_ge(consts_made.sem, consts_made.after(0))
                    dve.tensor_tensor(bias_oh, buckets.unsqueeze(2).to_broadcast([P, G, BUCKETS]),
                                      iota[:, 0:BUCKETS].unsqueeze(1).to_broadcast([P, G, BUCKETS]),
                                      ALU.is_equal).then_inc(bucket_oh.sem, 1)
            inverse_root(rstd, var)
            dve.tensor_tensor(corr[:, :], rstd[:, :], rstd[:, :], ALU.mult).then_inc(dve_step.sem, 1)
            dve.wait_ge(dve_step.sem, step.next())
            dve.tensor_tensor(var[:, :], var[:, :], corr[:, :], ALU.mult).then_inc(dve_step.sem, 1)
            dve.wait_ge(dve_step.sem, step.next())
            inverse_root(rstd12, var)
            dve.tensor_tensor(rstd12[:, :], rstd12[:, :], rstd[:, :], ALU.mult).then_inc(dve_step.sem, 1)
            dve.wait_ge(dve_step.sem, step.next())
            centred(xh, 0, rstd12).then_inc(xh_ready.sem, 1)

            dve.wait_ge(consts_loaded.sem, 16 * CONSTS)
            dve.wait_ge(emb_chosen.sem, emb_chosen.after(0))
            dve.tensor_reduce(sim_s[:, 0, 0:G], bias_oh, AX.X, ALU.add).then_inc(dve_step.sem, 1)
            dve.wait_ge(dve_step.sem, step.next())
            dve.memset(bias_t, OFF_GROUP).then_inc(dve_step.sem, 1)
            dve.wait_ge(dve_step.sem, step.next())
            dve.memset(lin_kv, 0.0).then_inc(dve_step.sem, 1)
            dve.wait_ge(dve_step.sem, step.next())
            for h in range(2):
                block_h = slice(h * G, (h + 1) * G)
                dve.tensor_scalar(bias_t[block_h, block_h], sim_s[block_h, 0, 0:G], BIAS_SCALE, None,
                                  ALU.mult).then_inc(dve_step.sem, 1)
                dve.wait_ge(dve_step.sem, step.next())

            def first_pass(m, last):
                if not last:
                    dve.wait_ge(xt_mm.sem, xt_mm.after(m))
                    centred(xh, m + 1, rstd12).then_inc(xh_ready.sem, 1)
                dve.wait_ge(qkt_ready.sem, qkt_ready.after(m))
                dve.wait_ge(sim_mm.sem, sim_mm.room(m))
                dve.tensor_scalar(quad_q, qk_t, gamma_col[:, 0:1], beta_col[:, 0:1], ALU.mult, ALU.add)
                dve.tensor_scalar(quad_k, qk_t, gamma_col[:, 2:3], beta_col[:, 2:3], ALU.mult,
                                  ALU.add).then_inc(quad_ready.sem, 1)
                for s in range(SUB):
                    dve.wait_ge(v_mm.sem, v_mm.after(m * SUB + s))
                    dve.wait_ge(v_ready.sem, v_ready.room(m * SUB + s))
                    dve.tensor_tensor(v_tmp[:, s % 2, :], bank[5 + s % 2][:, :], bv_row, ALU.add)\
                        .then_inc(v_biased.sem, 1)
                dve.wait_ge(sim_mm.sem, sim_mm.after(m))
                dve.scalar_tensor_tensor(
                    out=sim_s, in0=bank[2][:, :].rearrange("p (s q) -> p s q", s=SUB), scalar=SIM_SCALE,
                    in1=bias_t.unsqueeze(1).to_broadcast([P, SUB, P]), op0=ALU.mult, op1=ALU.add)\
                    .then_inc(sim_read.sem, 1)
                dve.wait_ge(sim_read.sem, sim_read.after(m))
                dve.scalar_tensor_tensor(out=attn_t[:, ds(m * SUB, SUB), :], in0=sim_s, scalar=0.0, in1=sim_s,
                                         op0=ALU.max, op1=ALU.mult)
                dve.wait_ge(linkt_mm.sem, linkt_mm.after(m))
                dve.wait_ge(kv_mm.sem, kv_mm.after(m - 1))
                dve.tensor_copy(link_n.rearrange("p s q -> p (s q)"), bank[7][:, :]).then_inc(linkn_ready.sem, 1)
                dve.wait_ge(kv_mm.sem, kv_mm.after(m))
                dve.tensor_tensor(lin_kv, lin_kv, bank[7][:, :], ALU.add).then_inc(kv_used.sem, 1)

            with dve.Fori(0, M - 1) as m:
                first_pass(m, False)
            first_pass(M - 1, True)
            dve.wait_ge(kv_used.sem, kv_used.after(M - 1))
            dve.tensor_scalar(lin_kv, lin_kv, 1.0 / TOK, None, ALU.mult).then_inc(kv_final.sem, 1)

            def second_pass(m, b, turn, x2_before, top_before):
                dve.wait_ge(x1_ready.sem, x1_ready.room(m))
                centred(xn_s, m, rstd).then_inc(xn_ready.sem, 1)
                dve.wait_ge(gate_back[b].sem, gate_back[b].landed(turn))
                dve.wait_ge(proj_mm.sem, proj_mm.after(m * 2 - 1))
                for c in range(KH):
                    dve.wait_ge(mix_mm.sem, mix_mm.after(m * KH + c))
                    dve.tensor_tensor(gated[c], bank[c][:, :], gate_st[b][:, c, :], ALU.mult)\
                        .then_inc(gated_ready.sem, 1)
                if top_before:
                    take_logits(m - 2)
                if x2_before:
                    normalise(m - 1)
                for h in range(2):
                    dve.wait_ge(proj_mm.sem, proj_mm.after(m * 2 + h))
                    dve.tensor_tensor(proj_s[:, 2 * h:2 * h + 2, :],
                                      bank[4 + h][:, :].rearrange("p (s d) -> p s d", s=2),
                                      bo_row.unsqueeze(1).to_broadcast([P, 2, D]), ALU.add)\
                        .then_inc(proj_used.sem, 1)
                if top_before:
                    top_of_macro(m - 2)

            def normalise(m):
                dve.wait_ge(x1_ready.sem, x1_ready.after(m))
                alone(dve)
                for s in range(SUB):
                    ins = dve.bn_stats(stats[:, s, :], tile_of(m * SUB + s))
                ins.then_inc(dve_step.sem, 1)
                dve.wait_ge(dve_step.sem, step.next())
                alone(dve)
                for s in range(SUB):
                    ins = dve.bn_aggr(mv[:, s, :], stats[:, s, :])
                ins.then_inc(dve_step.sem, 1)
                dve.wait_ge(dve_step.sem, step.next())
                dve.tensor_scalar(root4_in[:, :], mv[:, 0:SUB, 1], EPS, None, ALU.add).then_inc(root4_asked.sem, 1)
                dve.wait_ge(root4_asked.sem, root4_asked.after(m))
                dve.wait_ge(root4_made.sem, root4_made.after(m))
                dve.reciprocal(rstd4[:, :], root4[:, :]).then_inc(dve_step.sem, 1)
                dve.wait_ge(dve_step.sem, step.next())
                dve.tensor_tensor(corr4[:, :], root4_in[:, :], rstd4[:, :], ALU.mult).then_inc(dve_step.sem, 1)
                dve.wait_ge(dve_step.sem, step.next())
                dve.tensor_tensor(corr4[:, :], corr4[:, :], rstd4[:, :], ALU.mult).then_inc(dve_step.sem, 1)
                dve.wait_ge(dve_step.sem, step.next())
                dve.tensor_scalar(corr4[:, :], corr4[:, :], -0.5, 1.5, ALU.mult, ALU.add).then_inc(dve_step.sem, 1)
                dve.wait_ge(dve_step.sem, step.next())
                dve.tensor_tensor(rstd4[:, :], rstd4[:, :], corr4[:, :], ALU.mult).then_inc(dve_step.sem, 1)
                dve.wait_ge(dve_step.sem, step.next())
                dve.wait_ge(x2t_mm.sem, x2t_mm.room(m))
                dve.wait_ge(x2_stored.sem, x2_stored.sent(m))
                for s in range(SUB):
                    ins = dve.tensor_scalar(x2h[:, s, :], tile_of(m * SUB + s), mv[:, s, 0:1], rstd4[:, s:s + 1],
                                            ALU.subtract, ALU.mult)
                ins.then_inc(x2_ready.sem, 1)

            def take_logits(m):
                dve.wait_ge(logit_mm.sem, logit_mm.after(m))
                dve.tensor_copy(lg[:, :, :, :].rearrange("p s j e -> p (s j e)"), bank[6][:, 0:SUB * 2 * E])\
                    .then_inc(lg_ready.sem, 1)

            def top_of_macro(m):
                dve.wait_ge(lg_ready.sem, lg_ready.after(m))
                alone(dve)
                pick_two(SUB, 2, lambda table, got, j: dve.tensor_copy(
                    table[:, j, :, ds(m * SUB, SUB)].rearrange("p k s -> p s k"), got[:, :, j, 0:2]))

            def pick_two(subs, routes, put):
                pairs = [(s, j) for s in range(subs) for j in range(routes)]
                for s, j in pairs:
                    ins = dve.max(mx[:, s, j, :], lg[:, s, j, :])
                ins.then_inc(dve_step.sem, 1)
                dve.wait_ge(dve_step.sem, step.next())
                alone(dve)
                for s, j in pairs:
                    ins = dve.max_index(mi[:, s, j, :], mx[:, s, j, :], lg[:, s, j, :])
                ins.then_inc(dve_step.sem, 1)
                dve.wait_ge(dve_step.sem, step.next())
                alone(dve)
                for table, got in ((top_v, mx), (top_i, mi)):
                    for j in range(routes):
                        ins = put(table, got, j)
                ins.then_inc(dve_step.sem, 1)
                dve.wait_ge(dve_step.sem, step.next())

            second_pass(0, 0, 0, False, False)
            second_pass(1, 1, 0, True, False)
            with dve.Fori(0, M // 2 - 1) as it:
                step.enter(it, 20)
                for b in range(2):
                    second_pass(it * 2 + (b + 2), b, it + 1, True, True)
            step.leave(M // 2 - 1)
            take_logits(M - 2)
            normalise(M - 1)
            top_of_macro(M - 2)
            take_logits(M - 1)
            top_of_macro(M - 1)

            def sized(a, g):
                return a[:, 0:g.words].rearrange("p (g e t) -> p g e t", g=g.count, e=E)

            def by_expert(a, g, n):
                return a[:, 0:g.count * E].rearrange("p (g e) -> p g e", e=E).unsqueeze(3).to_broadcast(
                    [P, g.count, E, n])

            def occupancy(g):
                c, at = comb[g.matrix], g.at
                dve.tensor_tensor(c[:, 0, at], top_v[:, g.column, 1, at], top_v[:, g.column, 0, at], ALU.subtract)\
                    .then_inc(exp_asked.sem, 1)
                o, shape = oh[g.n % 2], [P, g.count, E, g.tiles]
                for k in range(2):
                    ins = dve.tensor_tensor(
                        sized(o[k], g), iota[:, 0:E].unsqueeze(1).unsqueeze(3).to_broadcast(shape),
                        top_i[:, g.column, k, at].rearrange("p (g t) -> p g t", g=g.count).unsqueeze(2)
                        .to_broadcast(shape), ALU.is_equal)
                ins.then_inc(dve_step.sem, 1)
                dve.wait_ge(dve_step.sem, step.next())
                w = g.words
                dve.tensor_tensor(occ[g.n % 2][:, 0:w], o[0][:, 0:w], o[1][:, 0:w], ALU.add)\
                    .then_inc(occ_ready.sem, 1)

            def take_ranks(g, first):
                dve.wait_ge(rank_mm.sem, rank_mm.after(g.n))
                w = g.words
                dve.tensor_copy(within[g.n % 2][:, 0:w], bank[first][:, 0:w])
                dve.tensor_copy(tot[g.n % 2][:, 0:w], bank[first + 1][:, 0:w]).then_inc(dve_step.sem, 1)
                dve.wait_ge(dve_step.sem, step.next())

            def places(g):
                def then(ins):
                    ins.then_inc(dve_step.sem, 1)
                    dve.wait_ge(dve_step.sem, step.next())

                c, at, n, w, ge = comb[g.matrix], g.at, g.tiles, g.words, g.count * E
                t_f, in_f, ra_f = tot[g.n % 2][:, 0:w], incl[:, 0:w], rank[:, 0:w]
                restart = (keep if n == T else keep_half)[:, 0:w]
                then(dve.tensor_tensor_scan(in_f, restart, t_f, 0.0, ALU.mult, ALU.add))
                then(dve.tensor_tensor(ra_f, in_f, t_f, ALU.subtract))
                dve.tensor_tensor(ra_f, ra_f, within[g.n % 2][:, 0:w], ALU.add)
                then(dve.tensor_scalar(load_e[:, 0:ge].rearrange("p (g e) -> p g e", e=E),
                                       sized(incl, g)[:, :, :, n - 1], 1.0 / P, None, ALU.mult))
                then(dve.tensor_tensor(sized(full, g), by_expert(load_e, g, n),
                                       iota[:, 0:n].unsqueeze(1).unsqueeze(1).to_broadcast([P, g.count, E, n]),
                                       ALU.is_gt))
                then(dve.tensor_reduce(tiles_e[:, 0:ge], full[:, 0:w].rearrange("p (e t) -> p e t", t=n), AX.X,
                                       ALU.add))
                then(dve.tensor_tensor_scan(end_e[:, 0:ge], restart_e[:, 0:ge], tiles_e[:, 0:ge], 0.0, ALU.mult,
                                            ALU.add))
                then(dve.tensor_tensor(base_e[:, 0:ge], end_e[:, 0:ge], tiles_e[:, 0:ge], ALU.subtract))
                then(dve.tensor_scalar(base_e[:, 0:ge], base_e[:, 0:ge], float(P), None, ALU.mult))
                then(dve.tensor_tensor(sized(rank, g), sized(rank, g), by_expert(base_e, g, n), ALU.add))
                for k in range(2):
                    then(dve.tensor_tensor(full[:, 0:w], oh[g.n % 2][k][:, 0:w], ra_f, ALU.mult))
                    then(dve.tensor_reduce(pos_f[:, at, k].rearrange("p (g t) -> p g t", g=g.count),
                                           sized(full, g).rearrange("p g e t -> p g t e"), AX.X, ALU.add))
                p = pos[g.matrix]
                then(dve.tensor_copy(p[:, at, :], pos_f[:, at, :]))
                dve.tensor_scalar(pa_i[:, at, :], p[:, at, :], 7, None, ALU.logical_shift_right)
                then(dve.tensor_scalar(pb_i[:, at, :], p[:, at, :], P - 1, None, ALU.bitwise_and))
                dve.tensor_copy(pa_h[:, at, :], pa_i[:, at, :])
                then(dve.tensor_copy(pb_h[:, at, :], pb_i[:, at, :]))

            def experts(g):
                def then(ins):
                    ins.then_inc(dve_step.sem, 1)
                    dve.wait_ge(dve_step.sem, step.next())

                c, at, n, ge = comb[g.matrix], g.at, g.count * g.nt, g.count * E
                e4 = ends[:, 0:n * E].rearrange("p (g i e) -> p g i e", g=g.count, e=E)
                dve.wait_ge(exp_made.sem, exp_made.after(g.n))
                dve.tensor_scalar(c[:, 0, at], c[:, 1, at], 1.0, None, ALU.add)
                then(dve.tensor_tensor(
                    e4, end_e[0:1, 0:ge].rearrange("p (g e) -> p g e", e=E).unsqueeze(2).to_broadcast(
                        [1, g.count, g.nt, E]),
                    iota[0:1, 0:g.nt].unsqueeze(1).unsqueeze(3).to_broadcast([1, g.count, g.nt, E]), ALU.is_le))
                dve.reciprocal(c[:, 0, at], c[:, 0, at])
                then(dve.tensor_reduce(ex_f[:, 0:n], ends[:, 0:n * E].rearrange("p (i e) -> p i e", e=E), AX.X,
                                       ALU.add))
                dve.tensor_tensor(c[:, 1, at], c[:, 1, at], c[:, 0, at], ALU.mult)
                then(dve.tensor_scalar(ex_f[:, 0:n], ex_f[:, 0:n], float(E - 1), None, ALU.min))
                if g.routes[0] is GATE:
                    credits = phase[GATE].y_mm.credits
                    dve.memset(run_counts[:, E - 1:E], GATE.nt + credits)
                    then(dve.tensor_scalar(load_e[0:1, 0:E], end_e[0:1, 0:E], float(credits), None, ALU.add))
                    dve.tensor_copy(run_counts[:, 0:E - 1], load_e[0:1, 0:E - 1])
                then(dve.tensor_copy(expert_of[g][:, :], ex_f[:, 0:n]))

            def one_hots(r, batch, b):
                dve.wait_ge(table_mm.sem, table_mm.room(batch + r.batches_before))

                def spread(a, width, first=r.first):
                    rows = a[:, ds(batch * B + first, B), :].rearrange("p t k -> p (t k)")
                    return rows.unsqueeze(2).to_broadcast([P, 2 * B, width])

                parts = tile_oh[b][:, 0:4 * B * r.nt].rearrange("p (t c i) -> p t c i", c=2, i=r.nt)
                of_part, of_start = parts[:, :, 0, :], parts[:, :, 1, :]
                dve.tensor_tensor(of_start, iota_h[:, 0:r.nt].unsqueeze(1).to_broadcast([P, 2 * B, r.nt]),
                                  spread(pa_h, r.nt), ALU.is_equal).then_inc(dve_step.sem, 1)
                dve.tensor_tensor(row_oh[b], iota_h[:, :].unsqueeze(1).to_broadcast([P, 2 * B, P]), spread(pb_h, P),
                                  ALU.is_equal)
                dve.wait_ge(dve_step.sem, step.next())
                dve.tensor_scalar(of_part, of_start, part[:, :], None, ALU.mult)
                dve.tensor_tensor(of_start, of_start, spread(start_h, r.nt, 0 if r.matrix == "down" else r.first),
                                  ALU.mult).then_inc(onehot_ready.sem, 1)

            def table(r, at):
                with dve.Fori(0, r.tiles // B // 2) as it:
                    step.enter(it, 2)
                    for b in range(2):
                        one_hots(r, it * 2 + b, b)
                step.leave(r.tiles // B // 2)
                close_table(r, at)

            def close_table(r, at):
                dve.wait_ge(table_mm.sem, table_mm.after(r.tiles // B - 1 + r.batches_before))
                dve.tensor_copy(id_f[:, 0:r.nt], bank[at][:, 0:r.nt]).then_inc(dve_step.sem, 1)
                dve.wait_ge(dve_step.sem, step.next())
                dve.tensor_tensor(ids[r][:, :], id_f[:, 0:r.nt], bank[at][:, r.nt:2 * r.nt], ALU.add)\
                    .then_inc(routed.sem, 1)

            def copied(r, i, j, turn):
                n = phase[r]
                dve.wait_ge(n.y_mm.sem, n.y_mm.after(i))
                dve.wait_ge(n.y_stored[j % 2].sem, n.y_stored[j % 2].sent(turn))
                dve.tensor_copy(y_s[j % 2][:, 512:1024], bank[5 + 2 * (j % 2)][:, :]).then_inc(n.half_ready.sem, 1)

            occupancy(GROUPS[0])
            occupancy(GROUPS[1])
            take_ranks(GROUPS[0], 0)
            take_ranks(GROUPS[1], 2)
            places(GROUPS[0])
            dve.wait_ge(x2_stored.sem, x2_stored.landed(M - 1))
            experts(GROUPS[0])
            table(GATE, 4)
            dve.wait_ge(routed.sem, routed.after(GATE.n))
            places(GROUPS[1])
            experts(GROUPS[1])
            for h in range(2):
                with dve.Fori(0, H // B // 2) as it:
                    step.enter(it, 2)
                    for half in range(2):
                        for j in range(4):
                            i = it * 8 + (h * H + half * 4 + j)
                            copied(GATE, i, j, it * 4 + (h * H // 2 + half * 2 + j // 2))
                            if j == 1:
                                one_hots(UP[h], it * 2 + half, half)
                step.leave(H // B // 2)
            close_table(UP[0], 1)
            dve.wait_ge(routed.sem, routed.after(UP[0].n))
            close_table(UP[1], 3)
            with dve.Fori(T // 2, GATE.nt // 2) as it:
                for j in range(2):
                    copied(GATE, it * 2 + j, j, it)

            def products_out(r):
                for b in range(2):
                    dve.wait_ge(phase[r].y_stored[b].sem, phase[r].y_stored[b].landed(r.nt // 2 - 1))

            products_out(GATE)
            with dve.Fori(0, UP[0].nt // 2) as it:
                for j in range(2):
                    copied(UP[0], it * 2 + j, j, it)
            products_out(UP[0])

            def inner_part(t, b, turn):
                dve.wait_ge(c_y0.sem, c_y0.after(t))
                gate_0, up_0 = in4[b][0], in4[b][2]
                dve.scalar_tensor_tensor(out=gate_0, in0=in4[b][1], scalar=comb["gate"][:, 1, ds(t, 1)], in1=gate_0,
                                         op0=ALU.mult, op1=ALU.add).then_inc(c_g.sem, 1)
                dve.wait_ge(c_z0.sem, c_z0.after(t))
                dve.scalar_tensor_tensor(out=up_0, in0=in4[b][3], scalar=comb["up"][:, 1, ds(t, 1)],
                                         in1=up_0, op0=ALU.mult, op1=ALU.add).then_inc(c_u.sem, 1)
                dve.wait_ge(c_u.sem, c_u.after(t))
                dve.wait_ge(c_h.sem, c_h.after(t))
                dve.wait_ge(c_t_mm.sem, c_t_mm.room(t))
                dve.wait_ge(c_stored[b].sem, c_stored[b].sent(turn))
                dve.tensor_tensor(inter[b], gate_0, up_0, ALU.mult).then_inc(c_done.sem, 1)

            def inner_top(t, first):
                dve.wait_ge(c_log_mm.sem, c_log_mm.after(t))
                dve.tensor_copy(lg[:, 0, 0, :], bank[first][:, 0:E]).then_inc(c_lg.sem, 1)
                dve.wait_ge(c_lg.sem, c_lg.after(t))
                alone(dve)
                pick_two(1, 1, lambda table, got, j: dve.tensor_copy(table[:, 2, :, ds(t, 1)],
                                                                    got[:, 0, 0, 0:2].unsqueeze(2)))

            def turned(r, i, j):
                n = phase[r]
                dve.wait_ge(n.xt_mm.sem, n.xt_mm.after(i))
                dve.wait_ge(n.y_mm.sem, n.y_mm.room(i))
                dve.tensor_copy(rows_t[j % 2][:, 512:1024], bank[2 * (j % 2) + 1][:, :]).then_inc(n.half_ready.sem, 1)

            def output_part(t, b, turn):
                dve.wait_ge(o_y0.sem, o_y0.after(t))
                dve.scalar_tensor_tensor(out=in2[b][0], in0=in2[b][1], scalar=comb["down"][:, 1, ds(t, 1)],
                                         in1=in2[b][0], op0=ALU.mult, op1=ALU.add).then_inc(o_sum.sem, 1)
                dve.wait_ge(o_sum.sem, o_sum.after(t))
                dve.wait_ge(o_stored[b].sem, o_stored[b].sent(turn))
                dve.tensor_tensor(out_s[b], in2[b][0], tile_of(t), ALU.add).then_inc(o_ready.sem, 1)

            def first_part(it, j, h):
                if j in FIRST_PARTS:
                    k = FIRST_PARTS.index(j)
                    inner_part(it * 4 + (h * H + k), k % 2, it * 2 + (h * H // 2 + k // 2))

            def second_part(it, j, h, first):
                if j in SECOND_PARTS:
                    inner_top(it * 4 + (h * H + SECOND_PARTS.index(j)), first)

            def up_body(it):
                for j in range(BODY):
                    first_part(it, j, 0)
                    copied(UP[1], it * BODY + j, j, it * (BODY // 2) + j // 2)
                    second_part(it, j, 0, 1)

            with dve.Fori(0, UP[1].nt // BODY) as it:
                step.enter(it, 3 * len(SECOND_PARTS))
                up_body(it)
            step.leave(UP[1].nt // BODY)

            for h in range(2):
                r = DOWN[h]
                occupancy(r.group)
                take_ranks(r.group, 0)
                places(r.group)
                experts(r.group)
                table(r, 4)

                def down_body(it, last):
                    for j in range(BODY):
                        if not last or j < BODY - 1:
                            turned(r, it * BODY + j + 1, j + 1)
                        if h == 0:
                            first_part(it, j, 1)
                            second_part(it, j, 1, 5)
                        elif j in SECOND_PARTS:
                            k = SECOND_PARTS.index(j)
                            output_part(it * 4 + k, k, it)

                turned(r, 0, 0)
                with dve.Fori(0, r.nt // BODY - 1) as it:
                    if h == 0:
                        step.enter(it, 3 * len(SECOND_PARTS))
                    down_body(it, False)
                if h == 0:
                    step.leave(r.nt // BODY - 1)
                down_body(r.nt // BODY - 1, True)
            with dve.Fori(0, H // 4) as it:
                for b in range(4):
                    output_part(it * 4 + (H + b), b, it + H // 4)


def buckets_of_pairs():
    n = np.arange(G)[None, :] - np.arange(G)[:, None]
    half = BUCKETS // 2
    exact = half // 2
    size = np.abs(n)
    ratio = np.log(np.maximum(size, 1).astype(np.float32) / np.float32(exact)) / np.float32(np.log(128 / exact))
    large = np.minimum(exact + (ratio * np.float32(half - exact)).astype(np.int32), half - 1)
    bucket = np.where(n < 0, half, 0) + np.where(size < exact, size, large)
    return np.concatenate([bucket, bucket]).astype(np.float32)


def kernel(**inputs):
    import concourse.bacc as bacc
    from concourse.bass_utils import run_bass_kernel_spmd

    a = {k: np.asarray(v) for k, v in inputs.items()}
    c = np.ascontiguousarray

    def columns(v, k):
        return c(v.reshape(k, P).T)

    def experts_in(w, kc):
        n_out = w.shape[1]
        return c(w.transpose(2, 0, 1).reshape(kc, P, E, n_out).transpose(1, 2, 0, 3).reshape(P, -1))

    arrays = {
        "x": a["L0_attn_x"].reshape(TOK, D), "ln_g": columns(a["L0_attn_ln_g"], KD),
        "ln_b": columns(a["L0_attn_ln_b"], KD), "w_h": a["L0_attn_W_h"], "bh_value": a["L0_attn_b_h"][:HID],
        "bh_gate": columns(a["L0_attn_b_h"][HID:], KH), "w_qk": a["L0_attn_W_qk"],
        "b_qk": columns(a["L0_attn_b_qk"], 1), "os_gamma": a["L0_attn_os_gamma"].T,
        "os_beta": a["L0_attn_os_beta"].T, "rel_emb": a["L0_attn_rel_emb"].reshape(-1), "w_out": a["L0_attn_W_out"],
        "b_out": a["L0_attn_b_out"], "r_gate": a["L0_ffn_router_gate"].T,
        "w_gate": experts_in(a["L0_ffn_w_gate"], KD), "r_up": a["L0_ffn_router_up"].T,
        "w_up": experts_in(a["L0_ffn_w_up"], KD), "r_down": a["L0_ffn_router_down"].T,
        "w_down": experts_in(a["L0_ffn_w_down"], KI), "buckets": buckets_of_pairs(),
    }
    arrays = {f"in_{k}": c(v) for k, v in arrays.items()}
    nc = bacc.Bacc("TRN2", target_bir_lowering=False, num_devices=1)
    args = [nc.dram_tensor(k, v.shape, mybir.dt.from_np(v.dtype), kind="ExternalInput").ap()
            for k, v in arrays.items()]
    out = nc.dram_tensor("out", (TOK, D), F32, kind="ExternalOutput").ap()
    block_kernel(nc, *args, out)
    r = run_bass_kernel_spmd(nc, [arrays], core_ids=[0])
    return r.results[0]["out"].reshape(1, TOK, D)
```

```python
from contextlib import ExitStack

import numpy as np

import concourse.bass as bass
from concourse import mybir

F32 = mybir.dt.float32
BF16 = mybir.dt.bfloat16
I32 = mybir.dt.int32
U32 = mybir.dt.uint32
ALU = mybir.AluOpType
ACT = mybir.ActivationFunctionType
AX = mybir.AxisListType
ds = bass.ds

P = 128
TOK = 4096
D = 256
HID = 512
G = 64
E = 8
INNER = 1024
T = TOK // P
KD = D // P
KI = INNER // P
SLAB = D * INNER // P
KH = HID // P
SUB = 4
M = T // SUB
MT = SUB * P
H = T // 2
B = 4
EPS = 1e-5
BUCKETS = 32
SIM_SCALE = 1.0 / G
BIAS_SCALE = float(P) ** 0.5
OFF_GROUP = -1.0e30


class Route:

    def __init__(self, n, matrix, column, first, tiles, batches_before):
        self.n, self.matrix, self.column, self.first, self.tiles = n, matrix, column, first, tiles
        self.nt = 2 * tiles + E
        self.whole_from = self.nt
        self.batches_before = batches_before


class Group:

    def __init__(self, n, *routes):
        self.n, self.routes, self.matrix, self.column = n, routes, routes[0].matrix, routes[0].column
        self.tiles, self.nt, self.count = routes[0].tiles, routes[0].nt, len(routes)
        self.at = slice(routes[0].first, routes[0].first + self.count * self.tiles)
        self.words = self.count * E * self.tiles
        for k, r in enumerate(routes):
            r.group, r.tiles_before = self, k * self.nt


GATE = Route(0, "gate", 0, 0, T, 0)
UP = [Route(1 + h, "up", 1, h * H, H, (T + h * H) // B) for h in range(2)]
DOWN = [Route(3 + h, "down", 2, h * H, H, (2 * T + h * H) // B) for h in range(2)]
ROUTES = (GATE, *UP, *DOWN)
GROUPS = (Group(0, GATE), Group(1, *UP), Group(2, DOWN[0]), Group(3, DOWN[1]))
BODY = 8
for r in (UP[1], DOWN[0]):
    r.whole_from = r.nt - BODY
BODIES = UP[0].nt // BODY


class Steps:

    def __init__(self):
        self.base, self.n = 0, 0

    def next(self):
        self.n += 1
        return self.base + self.n

    def enter(self, turn, per):
        self.outer, self.per = self.base + self.n, per
        self.base, self.n = turn * per + self.outer, 0

    def leave(self, turns):
        assert self.n == self.per, (self.n, self.per)
        self.base, self.n = self.outer + turns * self.per, 0


class Signal:

    def __init__(self, ctx, nc, name, credits=0):
        self.sem, self.credits = ctx.enter_context(nc.semaphore(name)), credits

    def after(self, n):
        return n + (1 + self.credits)

    def room(self, n):
        return n + 1

    def landed(self, turn, each=16):
        return turn * each + (each + self.credits)

    def sent(self, turn):
        return turn * 16 + 16


def block_kernel(nc, x_in, ln_g, ln_b, w_h, bh_value, bh_gate, w_qk, b_qk, os_gamma, os_beta, rel_emb, w_out,
                 b_out, r_gate, w_gate, r_up, w_up, r_down, w_down, bucket_in, out):
    with ExitStack() as ctx:
        def sb(name, shape, dt=F32):
            return ctx.enter_context(nc.sbuf_tensor(name, shape, dt))

        def sig(name, credits=0):
            return Signal(ctx, nc, name, credits)

        def dram(name, shape):
            return nc.dram_tensor(name, shape, F32, kind="Internal").ap()

        gate_d = dram("gate_d", [M * P, KH * MT])
        v_d = dram("v_d", [M * P, SUB * HID])
        x2_d = dram("x2_d", [TOK, D])
        inter_d = [dram(f"inter_d{h}", [H * P, INNER]) for h in range(2)]
        sorted_d = {r: dram(f"sorted{r.n}", [r.nt * P, D if r.matrix == "down" else INNER]) for r in ROUTES}

        bank = [ctx.enter_context(nc.psum_tensor(f"bank{i}", [P, 512], F32)) for i in range(8)]

        x_sb = sb("x_sb", [P, T, D])
        ident = sb("ident", [P, P])
        before = sb("before", [P, P])
        ones = sb("ones", [P, P])
        zeros = sb("zeros", [P, P])
        iota = sb("iota", [P, P])
        iota_i = sb("iota_i", [P, P], I32)
        iota_h = sb("iota_h", [P, P], BF16)
        part_i, part = sb("part_i", [P, 1], I32), sb("part", [P, 1])
        start_i = sb("start_i", [P, T, 2], I32)
        start_h = sb("start_h", [P, T, 2], BF16)
        mean, rstd, rstd12 = (sb(n, [P, T]) for n in ("mean", "rstd", "rstd12"))
        var8, rstd8, rstd8_2, root_in, root, corr = (sb(n, [P, T // 4]) for n in (
            "var8", "rstd8", "rstd8_2", "root_in", "root", "corr"))
        stats = sb("stats", [P, T // 4, 6])
        mv = sb("mv", [P, T // 4, 2])
        root4_in, root4, rstd4, corr4 = (sb(n, [P, SUB]) for n in ("root4_in", "root4", "rstd4", "corr4"))
        g_col, b_col = sb("g_col", [P, KD]), sb("b_col", [P, KD])
        bqk_col, bgate_col = sb("bqk_col", [P, 1]), sb("bgate_col", [P, KH])
        gamma_col, beta_col = sb("gamma_col", [P, 4]), sb("beta_col", [P, 4])
        rt_sb = sb("rt_sb", [P, KD, 2 * E])
        rd_sb = sb("rd_sb", [P, KI, E])
        top_v = sb("top_v", [P, 3, 2, T])
        top_i = sb("top_i", [P, 3, 2, T])
        comb = {m: sb(f"comb_{m}", [P, 2, T]) for m in ("gate", "up", "down")}
        pos = {m: sb(f"pos_{m}", [P, T, 2], I32) for m in ("gate", "up", "down")}
        id_f = sb("id_f", [P, GATE.nt])
        ids = {r: sb(f"ids{r.n}", [P, r.nt], I32) for r in ROUTES}
        expert_of = {g: sb(f"expert_of{g.n}", [1, g.count * g.nt], I32) for g in GROUPS}
        run_counts = {r: sb(f"run_counts{r.n}", [1, E], I32) for r in (GATE, UP[1])}
        lg = sb("lg", [P, SUB, 2, E])
        mx = sb("mx", [P, SUB, 2, 8])
        mi = sb("mi", [P, SUB, 2, 8], U32)
        idx_s = [sb(f"idx_s{b}", [P, 1], I32) for b in range(4)]
        idx2 = [sb(f"idx2_{b}", [P, 2], I32) for b in range(4)]
        idx4 = [sb(f"idx4_{b}", [P, 4], I32) for b in range(2)]
        ET = E * T
        oh = [[sb(f"oh{n}{k}", [P, ET]) for k in range(2)] for n in range(2)]
        occ, tot, within = ([sb(f"{w}{n}", [P, ET]) for n in range(2)] for w in ("occ", "tot", "within"))
        keep, keep_half, incl, rank, full = (sb(n, [P, ET]) for n in ("keep", "keep_half", "incl", "rank", "full"))
        tiles_e, end_e, base_e, restart_e, load_e = (sb(n, [P, 2 * E]) for n in (
            "tiles_e", "end_e", "base_e", "restart_e", "load_e"))
        pos_f = sb("pos_f", [P, T, 2])
        pa_h, pb_h = sb("pa_h", [P, T, 2], BF16), sb("pb_h", [P, T, 2], BF16)
        pa_i, pb_i = sb("pa_i", [P, T, 2], I32), sb("pb_i", [P, T, 2], I32)
        ex_f = sb("ex_f", [1, 2 * UP[0].nt])

        WORDS = 36900
        arena = sb("arena", [P, WORDS])
        used = [0]

        def cut(*shape):
            n = int(np.prod(shape))
            a = arena[:, used[0]:used[0] + n]
            used[0] += n
            assert used[0] <= WORDS, used[0]
            if len(shape) == 1:
                return a
            names = "abc"[:len(shape)]
            return a.rearrange(f"p ({' '.join(names)}) -> p {' '.join(names)}", **dict(zip(names, shape)))

        wh_sb = cut(KD, 2 * HID)
        wqk_sb = cut(KD, P)
        wo_sb = cut(KH, D)
        bv_row = cut(HID)
        bo_row = cut(D)
        emb_row = cut(BUCKETS)
        buckets = cut(G)
        bias_oh = cut(G, BUCKETS)
        bias_t = cut(P)
        attn_t = cut(T, P)
        linq_t = cut(TOK)
        v_st = [cut(SUB, HID) for _ in range(2)]
        assert used[0] >= E * KD * INNER
        xh = cut(SUB, D)
        xn_s = cut(SUB, D)
        nt_s = [cut(KD, MT) for _ in range(2)]
        x2t_s = cut(KD, MT)
        qk_t, quad_q = x2t_s[:, 0, :], x2t_s[:, 1, :]
        quad_k, lin_k = (cut(MT) for _ in range(2))
        link_n = cut(SUB, P)
        v_tmp = cut(2, HID)
        gate_st = [cut(KH, MT) for _ in range(2)]
        lin_kv = cut(HID)
        sim_s = cut(SUB, P)
        proj_s = cut(SUB, D)
        gated = [nt_s[c // 2][:, c % 2, :] for c in range(KH)]
        x2h = xh

        used[0] = 0
        w_sb = cut(E * SLAB)
        ring = cut(4 * INNER)
        rows_in = [ring[:, b * D:(b + 1) * D] for b in range(4)]
        rows_down = [ring[:, b * INNER:(b + 1) * INNER] for b in range(4)]
        rows_t = [cut(INNER) for _ in range(2)]
        y_s = [cut(INNER) for _ in range(2)]
        in8 = cut(8 * INNER)
        in4 = [[in8[:, (4 * b + k) * INNER:(4 * b + k + 1) * INNER] for k in range(4)]
               for b in range(2)]

        class OneHots:

            def __init__(self, area):
                rows, tiles = B * P, 2 * B * GATE.nt
                self.row = [area[:, b * rows:(b + 1) * rows].bitcast(BF16).rearrange("p (t q) -> p t q", t=2 * B)
                            for b in range(2)]
                self.tile = [area[:, 2 * rows + b * tiles:2 * rows + (b + 1) * tiles].bitcast(BF16)
                             for b in range(2)]
                self.ends = area[0:1, 2 * (rows + tiles):]

        in_ring, in_in4 = OneHots(ring[:, 4 * D:]), OneHots(in8[:, 0:4 * INNER])
        one_hots_of = {r: in_in4 if r is DOWN[1] else in_ring for r in ROUTES}
        inter_t = cut(INNER)
        inter = [cut(INNER) for _ in range(2)]
        in2 = [[in4[b // 2][b % 2 * 2 + k][:, 0:D] for k in range(2)] for b in range(4)]
        out_s = [inter[b // 2][:, b % 2 * D:(b % 2 + 1) * D] for b in range(4)]

        dve_step, pool_step = sig("vector_step"), sig("pool_step")
        x_loaded = [sig(f"x_loaded{c}") for c in range(4)]
        consts_loaded, consts_made = sig("consts_loaded"), sig("consts_made")
        buckets_loaded, bucket_oh, emb_chosen = sig("buckets_loaded"), sig("bucket_oh"), sig("emb_chosen")
        root_asked, root_made = sig("root_asked"), sig("root_made")
        exp_asked, exp_made = sig("exp_asked"), sig("exp_made")
        xh_ready, xt_mm, nt_ready = sig("xh_ready"), sig("xt_mm"), sig("nt_ready", 1)
        qk_mm, qkt_ready = sig("qk_mm"), sig("qkt_ready")
        quad_ready, link_ready, linq_ready = sig("quad_ready", 1), sig("link_ready", 1), sig("linq_ready")
        gate_mm, gate_ready = sig("gate_mm"), sig("gate_ready", 2)
        v_mm, v_biased, v_ready = sig("v_mm", 8), sig("v_biased", 2), sig("v_ready", 2)
        sim_mm, sim_read = sig("sim_mm", 1), sig("sim_read", 1)
        linkt_mm, linkn_ready = sig("linkt_mm", 1), sig("linkn_ready")
        kv_mm, kv_used = sig("kv_mm", 2), sig("kv_used", 1)
        gate_stored, v_stored = ([sig(f"{n}_stored{b}", 16) for b in range(2)] for n in ("gate", "v"))
        kv_final = sig("kv_final")
        gate_back, v_back = ([sig(f"{n}_back{b}") for b in range(2)] for n in ("gate", "v"))
        mix_mm, gated_ready = sig("mix_mm", 8), sig("gated_ready", 8)
        proj_mm, proj_used = sig("proj_mm", 2), sig("proj_used", 2)
        xn_ready, x1_ready = sig("xn_ready"), sig("x1_ready", 1)
        root4_asked, root4_made = sig("root4_asked"), sig("root4_made")
        x2_ready, x2t_mm, x2t_ready = sig("x2_ready"), sig("x2t_mm", 1), sig("x2t_ready", 1)
        x2_stored = sig("x2_stored", 16)
        logit_mm, lg_ready = sig("logit_mm", 1), sig("lg_ready", 1)
        occ_ready, rank_mm = sig("occ_ready"), sig("rank_mm")
        onehot_ready, table_mm, routed = sig("onehot_ready"), sig("table_mm", 2), sig("routed")
        w_landed, w_ready = sig("w_landed"), sig("w_ready")

        class Phase:

            def __init__(self, r):
                self.idx_ready = sig(f"idx_ready{r.n}")
                self.gathered = [sig(f"gathered{r.n}_{b}") for b in range(4)]
                self.xt_mm = sig(f"xt_mm{r.n}", 4)
                self.xt_ready = sig(f"xt_ready{r.n}", 2)
                self.half_ready = sig(f"half_ready{r.n}", 2)
                self.y_mm = sig(f"y_mm{r.n}", 2)
                self.y0_ready = sig(f"y0_ready{r.n}", 2)
                self.y_stored = [sig(f"y_stored{r.n}_{b}", 16) for b in range(2)]

        phase = {r: Phase(r) for r in ROUTES}
        c_idx, c_got = sig("c_idx"), [sig(f"c_got{b}") for b in range(2)]
        c_y0, c_z0, c_g, c_h, c_done = sig("c_y0"), sig("c_z0"), sig("c_g"), sig("c_h"), sig("c_done", 2)
        c_u = sig("c_u")
        c_t_mm, c_t_ready, c_log_mm, c_lg = sig("c_t_mm", 2), sig("c_t_ready", 1), sig("c_log_mm", 1), sig("c_lg", 1)
        c_stored = [sig(f"c_stored{b}", 16) for b in range(2)]
        o_idx, o_got = sig("o_idx"), [sig(f"o_got{b}") for b in range(4)]
        o_y0, o_sum, o_ready = sig("o_y0"), sig("o_sum"), sig("o_ready", 4)
        o_stored = [sig(f"o_stored{b}", 16) for b in range(4)]

        def give(eng, *signals):
            for s in signals:
                eng.sem_inc(s.sem, s.credits)

        waited = {}

        def alone(eng):
            if eng not in waited:
                waited[eng] = sig(f"waited{len(waited)}")
            eng.sem_inc(waited[eng].sem, 1)

        GATHERS, FIRST_PARTS, SECOND_PARTS = (1, 3, 5, 7), (0, 2, 4, 6), (1, 3, 5, 7)
        AHEAD = 3

        CONSTS = 15

        block = ctx.enter_context(nc.Block())

        @block.sync
        def _(sp):
            give(sp, *gate_stored, *v_stored, *c_stored, *o_stored)
            x_v = x_in.rearrange("(t p) d -> p t d", p=P)
            for c in range(4):
                sp.dma_start(x_sb[:, c * 8:(c + 1) * 8, :], x_v[:, c * 8:(c + 1) * 8, :])\
                    .then_inc(x_loaded[c].sem, 16)

            def flat(a):
                return a.rearrange("p a b -> p (a b)")

            def store(m, b):
                sp.wait_ge(gate_ready.sem, gate_ready.after(m * KH + KH - 1))
                sp.dma_start(gate_d[ds(m * P, P), :], flat(gate_st[b])).then_inc(gate_stored[b].sem, 16)
                sp.wait_ge(v_ready.sem, v_ready.after(m * SUB + SUB - 1))
                sp.dma_start(v_d[ds(m * P, P), :], flat(v_st[b])).then_inc(v_stored[b].sem, 16)

            with sp.Fori(0, M // 2 - 1) as it:
                for b in range(2):
                    store(it * 2 + b, b)
            for b in range(2):
                store(M - 2 + b, b)
                sp.wait_ge(gate_stored[b].sem, gate_stored[b].landed(M // 2 - 1))
                sp.dma_start(flat(gate_st[b]), gate_d[b * P:(b + 1) * P, :]).then_inc(gate_back[b].sem, 16)
                sp.wait_ge(v_stored[b].sem, v_stored[b].landed(M // 2 - 1))
                sp.wait_ge(kv_mm.sem, kv_mm.after(M - 2 + b))
                sp.dma_start(flat(v_st[b]), v_d[b * P:(b + 1) * P, :]).then_inc(v_back[b].sem, 16)
            with sp.Fori(1, M // 2) as it:
                for b in range(2):
                    m = it * 2 + b
                    sp.wait_ge(gated_ready.sem, gated_ready.room(m * KH + KH - 1))
                    sp.dma_start(flat(gate_st[b]), gate_d[ds(m * P, P), :]).then_inc(gate_back[b].sem, 16)
                    sp.wait_ge(mix_mm.sem, mix_mm.room(m * KH + KH - 1))
                    sp.dma_start(flat(v_st[b]), v_d[ds(m * P, P), :]).then_inc(v_back[b].sem, 16)
            sp.wait_ge(proj_mm.sem, proj_mm.after(2 * M - 1))
            sp.wait_ge(proj_used.sem, proj_used.after(2 * M - 1))

            def load_expert(e, w):
                sp.dma_start(w_sb[:, ds(e * SLAB, SLAB)], w[:, ds(e * SLAB, SLAB)]).then_inc(w_landed.sem, 16)

            with sp.Fori(0, E) as e:
                load_expert(e, w_gate)
                sp.wait_ge(w_landed.sem, w_landed.landed(e))
                sp.sem_inc(w_ready.sem, 1)

            def load_as_freed(n, w, before):
                y_mm = phase[before].y_mm
                with sp.Fori(0, E) as e:
                    products = sp.value_load(run_counts[before][0:1, ds(e, 1)], min_val=y_mm.credits,
                                             max_val=before.nt + y_mm.credits)
                    sp.wait_ge(y_mm.sem, products)
                    load_expert(e, w)
                    sp.wait_ge(w_landed.sem, w_landed.landed(e + n * E))
                    sp.sem_inc(w_ready.sem, 1)

            sp.wait_ge(routed.sem, routed.after(GATE.n))
            load_as_freed(1, w_up, GATE)
            for h in range(2):
                with sp.Fori(0, H // 2) as it:
                    for b in range(2):
                        t = it * 2 + b
                        sp.wait_ge(c_done.sem, c_done.after(t + h * H))
                        sp.dma_start(inter_d[h][ds(t * P, P), :], inter[b]).then_inc(c_stored[b].sem, 16)
                if h == 0:
                    sp.wait_ge(routed.sem, routed.after(UP[1].n))
                    load_as_freed(2, w_down, UP[1])
            with sp.Fori(0, T // 4) as it:
                for b in range(4):
                    t = it * 4 + b
                    sp.wait_ge(o_ready.sem, o_ready.after(t))
                    sp.dma_start(out[ds(t * P, P), :], out_s[b]).then_inc(o_stored[b].sem, 16)
            for b in range(4):
                sp.wait_ge(o_stored[b].sem, o_stored[b].landed(T // 4 - 1))
            for b in range(2):
                sp.wait_ge(c_stored[b].sem, c_stored[b].landed(T // 2 - 1))
                for r in ROUTES:
                    sp.wait_ge(phase[r].y_stored[b].sem, phase[r].y_stored[b].landed(r.nt // 2 - 1))

        @block.gpsimd
        def _(pool):
            give(pool, link_ready, x1_ready)
            step = Steps()

            pool.memset(ident[:, :], 0.0).then_inc(pool_step.sem, 1)
            pool.wait_ge(pool_step.sem, step.next())
            pool.memset(before[:, :], 1.0).then_inc(pool_step.sem, 1)
            pool.wait_ge(pool_step.sem, step.next())
            pool.memset(ones[:, :], 1.0).then_inc(pool_step.sem, 1)
            pool.wait_ge(pool_step.sem, step.next())
            pool.memset(zeros[:, :], 0.0).then_inc(pool_step.sem, 1)
            pool.wait_ge(pool_step.sem, step.next())
            pool.iota(iota_i[:, :], pattern=[[1, P]], base=0, channel_multiplier=0).then_inc(pool_step.sem, 1)
            pool.wait_ge(pool_step.sem, step.next())
            pool.iota(part_i[:, :], pattern=[[0, 1]], base=0, channel_multiplier=1).then_inc(pool_step.sem, 1)
            pool.wait_ge(pool_step.sem, step.next())
            pool.iota(start_i[:, :, :], pattern=[[P, T], [0, 2]], base=0,
                      channel_multiplier=0).then_inc(pool_step.sem, 1)
            pool.wait_ge(pool_step.sem, step.next())
            pool.affine_select(out=ident[:, :], in_=ident[:, :], compare_op=ALU.not_equal, fill=1.0,
                               base=0, pattern=[[-1, P]], channel_multiplier=1).then_inc(pool_step.sem, 1)
            pool.wait_ge(pool_step.sem, step.next())
            pool.affine_select(out=before[:, :], in_=before[:, :], compare_op=ALU.is_gt, fill=0.0,
                               base=0, pattern=[[1, P]], channel_multiplier=-1).then_inc(pool_step.sem, 1)
            pool.wait_ge(pool_step.sem, step.next())
            pool.tensor_copy(iota[:, :], iota_i[:, :]).then_inc(pool_step.sem, 1)
            pool.wait_ge(pool_step.sem, step.next())
            pool.tensor_copy(iota_h[:, :], iota_i[:, :]).then_inc(pool_step.sem, 1)
            pool.wait_ge(pool_step.sem, step.next())
            pool.tensor_copy(part[:, :], part_i[:, :]).then_inc(pool_step.sem, 1)
            pool.wait_ge(pool_step.sem, step.next())
            pool.tensor_copy(start_h[:, :, :], start_i[:, :, :]).then_inc(pool_step.sem, 1)
            pool.wait_ge(pool_step.sem, step.next())
            pool.sem_inc(consts_made.sem, 1)
            pool.wait_ge(consts_loaded.sem, 16 * CONSTS)
            pool.wait_ge(bucket_oh.sem, bucket_oh.after(0))
            pool.tensor_tensor(bias_oh, bias_oh, emb_row.unsqueeze(1).to_broadcast([P, G, BUCKETS]),
                               ALU.mult).then_inc(emb_chosen.sem, 1)
            with pool.Fori(0, M) as m:
                pool.wait_ge(qkt_ready.sem, qkt_ready.after(m))
                pool.wait_ge(linkt_mm.sem, linkt_mm.room(m))
                alone(pool)
                pool.tensor_scalar(lin_k, qk_t, gamma_col[:, 3:4], beta_col[:, 3:4], ALU.mult,
                                   ALU.add).then_inc(link_ready.sem, 1)
            with pool.Fori(0, M) as m:
                step.enter(m, 1)
                pool.wait_ge(xn_ready.sem, xn_ready.after(m))
                alone(pool)
                x_m = x_sb[:, ds(m * SUB, SUB), :]
                pool.tensor_tensor(xn_s, xn_s, x_m, ALU.add).then_inc(pool_step.sem, 1)
                pool.wait_ge(pool_step.sem, step.next())
                pool.wait_ge(proj_used.sem, proj_used.after(m * 2 + 1))
                alone(pool)
                pool.tensor_tensor(x_m, xn_s, proj_s, ALU.add).then_inc(x1_ready.sem, 1)
            step.leave(M)

            def indexed(a, k):
                return bass.IndirectOffsetOnAxis(ap=a[:, k:k + 1].bitcast(U32), axis=0)

            def gather_rows(r, i, b):
                n = phase[r]
                dst, source = (rows_down[b], inter_d[r.first // H]) if r.matrix == "down" else (rows_in[b], x2_d)
                pool.wait_ge(n.xt_mm.sem, n.xt_mm.room(i))
                pool.tensor_copy(idx_s[b][:, :], ids[r][:, ds(i, 1)]).then_inc(n.idx_ready.sem, 1)
                pool.wait_ge(n.idx_ready.sem, n.idx_ready.after(i))
                alone(pool)
                pool.indirect_dma_start(dst, None, source[:, :], indexed(idx_s[b], 0)).then_inc(n.gathered[b].sem, 16)

            def gather_products(t, b, h):
                pool.wait_ge(c_done.sem, c_done.room(t))
                pool.tensor_copy(idx4[b][:, 0:2], pos["gate"][:, ds(t, 1), :].rearrange("p a k -> p (a k)"))
                pool.tensor_copy(idx4[b][:, 2:4], pos["up"][:, ds(t, 1), :].rearrange("p a k -> p (a k)"))\
                    .then_inc(c_idx.sem, 1)
                pool.wait_ge(c_idx.sem, c_idx.after(t))
                alone(pool)
                for k in range(4):
                    pool.indirect_dma_start(in4[b][k], None, sorted_d[(GATE, UP[h])[k // 2]][:, :],
                                            indexed(idx4[b], k)).then_inc(c_got[b].sem, 16)

            def gather_outputs(r, t, b):
                pool.wait_ge(o_ready.sem, o_ready.room(t))
                pool.tensor_copy(idx2[b][:, :], pos["down"][:, ds(t, 1), :].rearrange("p a k -> p (a k)"))\
                    .then_inc(o_idx.sem, 1)
                pool.wait_ge(o_idx.sem, o_idx.after(t))
                alone(pool)
                for k in range(2):
                    pool.indirect_dma_start(in2[b][k], None, sorted_d[r][:, :], indexed(idx2[b], k))\
                        .then_inc(o_got[b].sem, 16)

            def products_stored(r):
                for b in range(2):
                    pool.wait_ge(phase[r].y_stored[b].sem, phase[r].y_stored[b].landed(r.nt // 2 - 1))

            pool.wait_ge(x2_stored.sem, x2_stored.landed(M - 1))
            pool.wait_ge(routed.sem, routed.after(GATE.n))
            with pool.Fori(0, GATE.nt // 4) as it:
                for b in range(4):
                    gather_rows(GATE, it * 4 + b, b)

            def gather_sorted(r, beside=None):
                def body(it, tiles):
                    for j in range(BODY):
                        if j < tiles:
                            gather_rows(r, it * BODY + (j + AHEAD), (j + AHEAD) % 4)
                        if j in GATHERS and beside is not None and tiles == BODY:
                            beside(it, GATHERS.index(j))

                with pool.Fori(0, BODIES - 2) as it:
                    body(it, BODY)
                body(BODIES - 2, BODY)
                body(BODIES - 1, BODY - AHEAD)

            def first_rows(r, before):
                pool.wait_ge(routed.sem, routed.after(r.n))
                xt_mm = phase[before].xt_mm
                for i in range(AHEAD):
                    pool.wait_ge(xt_mm.sem, xt_mm.after(before.nt - 4 + i))
                    gather_rows(r, i, i)
                pool.wait_ge(xt_mm.sem, xt_mm.after(before.nt - 1))

            def products_beside(h):
                def gather(it, k):
                    if not isinstance(it, int) or k < 2:
                        gather_products(it * 4 + (h * H + 2 + k), k % 2, h)
                return gather

            first_rows(UP[0], GATE)
            gather_sorted(UP[0])
            first_rows(UP[1], UP[0])
            products_stored(GATE)
            products_stored(UP[0])
            for b in range(2):
                gather_products(b, b, 0)
            gather_sorted(UP[1], products_beside(0))
            for b in range(2):
                pool.wait_ge(c_stored[b].sem, c_stored[b].landed(H // 2 - 1))
            first_rows(DOWN[0], UP[1])
            products_stored(UP[1])
            for b in range(2):
                gather_products(H + b, b, 1)
            gather_sorted(DOWN[0], products_beside(1))
            for b in range(2):
                pool.wait_ge(c_stored[b].sem, c_stored[b].landed(T // 2 - 1))
            first_rows(DOWN[1], DOWN[0])
            products_stored(DOWN[0])
            gather_sorted(DOWN[1], lambda it, k: gather_outputs(DOWN[0], it * 4 + k, k))
            products_stored(DOWN[1])
            with pool.Fori(0, H // 4) as it:
                for b in range(4):
                    gather_outputs(DOWN[1], it * 4 + (H + b), b)

        @block.scalar
        def _(act):
            give(act, nt_ready, gate_ready, v_ready, x2t_ready, x2_stored, c_t_ready,
                 *(s for r in ROUTES for s in (phase[r].xt_ready, phase[r].y0_ready, *phase[r].y_stored)))

            def load(dst, src):
                act.dma_start(dst, src).then_inc(consts_loaded.sem, 16)

            act.dma_start(buckets, bucket_in).then_inc(buckets_loaded.sem, 16)
            load(wh_sb, w_h.rearrange("(k p) n -> p k n", p=P))
            load(wqk_sb, w_qk.rearrange("(k p) n -> p k n", p=P))
            load(wo_sb, w_out.rearrange("(k p) n -> p k n", p=P))
            load(g_col[:, :], ln_g)
            load(b_col[:, :], ln_b)
            load(bqk_col[:, :], b_qk)
            load(bgate_col[:, :], bh_gate)
            load(bv_row, bh_value.partition_broadcast(P))
            load(bo_row, b_out.partition_broadcast(P))
            load(emb_row, rel_emb.partition_broadcast(P))
            load(gamma_col[:, :], os_gamma)
            load(beta_col[:, :], os_beta)
            load(rt_sb[:, :, 0:E], r_gate.rearrange("(k p) n -> p k n", p=P))
            load(rt_sb[:, :, E:2 * E], r_up.rearrange("(k p) n -> p k n", p=P))
            load(rd_sb[:, :, :], r_down.rearrange("(k p) n -> p k n", p=P))
            def square_roots(c):
                for k in range(2):
                    act.wait_ge(root_asked.sem, root_asked.after(c * 2 + k))
                    act.activation(root[:, :], root_in[:, :], ACT.Sqrt).then_inc(root_made.sem, 1)

            def exponential(n):
                act.wait_ge(exp_asked.sem, exp_asked.after(n))
                c, at = comb[GROUPS[n].matrix], GROUPS[n].at
                act.activation(c[:, 1, at], c[:, 0, at], ACT.Exp).then_inc(exp_made.sem, 1)

            square_roots(0)
            act.wait_ge(consts_loaded.sem, 16 * CONSTS)
            def two_macros(it, roots_after):
                for b in range(2):
                    m = it * 2 + b
                    act.wait_ge(xt_mm.sem, xt_mm.after(m))
                    act.wait_ge(v_mm.sem, v_mm.room(m * SUB + SUB - 1))
                    for k in range(KD):
                        ins = act.activation(nt_s[b][:, k, :], bank[k][:, :], ACT.Identity, bias=b_col[:, k:k + 1],
                                             scale=g_col[:, k:k + 1])
                    ins.then_inc(nt_ready.sem, 1)
                    act.wait_ge(qk_mm.sem, qk_mm.after(m))
                    act.wait_ge(quad_ready.sem, quad_ready.room(m))
                    act.wait_ge(link_ready.sem, link_ready.room(m))
                    act.activation(qk_t, bank[2][:, :], ACT.Silu, bias=bqk_col[:, :]).then_inc(qkt_ready.sem, 1)
                    act.wait_ge(qkt_ready.sem, qkt_ready.after(m))
                    act.activation(linq_t[:, ds(m * MT, MT)], qk_t, ACT.Identity, bias=beta_col[:, 1:2],
                                   scale=gamma_col[:, 1:2]).then_inc(linq_ready.sem, 1)
                    act.wait_ge(gate_stored[b].sem, gate_stored[b].sent(it))
                    for c in range(KH):
                        if c == 2 and b == 1 and roots_after:
                            square_roots(it + 1)
                        act.wait_ge(gate_mm.sem, gate_mm.after(m * KH + c))
                        act.activation(gate_st[b][:, c, :], bank[3 + c % 2][:, :], ACT.Silu,
                                       bias=bgate_col[:, c:c + 1]).then_inc(gate_ready.sem, 1)
                    act.wait_ge(v_stored[b].sem, v_stored[b].sent(it))
                    act.wait_ge(kv_mm.sem, kv_mm.room(m))
                    for s in range(SUB):
                        act.wait_ge(v_biased.sem, v_biased.after(m * SUB + s))
                        act.activation(v_st[b][:, s, :], v_tmp[:, s % 2, :], ACT.Silu).then_inc(v_ready.sem, 1)

            with act.Fori(0, M // 2 - 1) as it:
                two_macros(it, True)
            two_macros(M // 2 - 1, False)
            with act.Fori(0, M) as m:
                act.wait_ge(root4_asked.sem, root4_asked.after(m))
                act.activation(root4[:, :], root4_in[:, :], ACT.Sqrt).then_inc(root4_made.sem, 1)
                act.wait_ge(x2_ready.sem, x2_ready.after(m))
                act.dma_start(x2_d[ds(m * MT, MT), :].rearrange("(s p) d -> p s d", p=P), x2h)\
                    .then_inc(x2_stored.sem, 16)
                act.wait_ge(x2t_mm.sem, x2t_mm.after(m))
                act.wait_ge(logit_mm.sem, logit_mm.room(m))
                for k in range(KD):
                    ins = act.activation(x2t_s[:, k, :], bank[6 + k][:, :], ACT.Copy)
                ins.then_inc(x2t_ready.sem, 1)
            exponential(0)
            exponential(1)

            def turned(r, i, j, whole=False):
                n = phase[r]
                act.wait_ge(n.xt_mm.sem, n.xt_mm.after(i))
                act.wait_ge(n.y_mm.sem, n.y_mm.room(i))
                w = 512 if r.matrix == "down" else D
                ins = act.activation(rows_t[j % 2][:, 0:w], bank[2 * (j % 2)][:, 0:w], ACT.Copy)
                if whole and r.matrix == "down":
                    ins = act.activation(rows_t[j % 2][:, 512:1024], bank[2 * (j % 2) + 1][:, :], ACT.Copy)
                ins.then_inc(n.xt_ready.sem, 1)

            def copied(r, i, j, turn, whole=False):
                n = phase[r]
                act.wait_ge(n.y_mm.sem, n.y_mm.after(i))
                act.wait_ge(n.y_stored[j % 2].sem, n.y_stored[j % 2].sent(turn))
                w = D if r.matrix == "down" else 512
                ins = act.activation(y_s[j % 2][:, 0:w], bank[4 + 2 * (j % 2)][:, 0:w], ACT.Copy)
                if whole and r.matrix != "down":
                    ins = act.activation(y_s[j % 2][:, 512:1024], bank[5 + 2 * (j % 2)][:, :], ACT.Copy)
                ins.then_inc(n.y0_ready.sem, 1)
                act.wait_ge(n.y0_ready.sem, n.y0_ready.after(i))
                if not whole and r.matrix != "down":
                    act.wait_ge(n.half_ready.sem, n.half_ready.after(i))
                y = y_s[j % 2][:, 0:D] if r.matrix == "down" else y_s[j % 2]
                act.dma_start(sorted_d[r][ds(i * P, P), :], y).then_inc(n.y_stored[j % 2].sem, 16)

            def sorted_tiles(r, before, beside=None, group=None):
                whole = r.whole_from < r.nt

                def body(it, next_whole=False):
                    for j in range(BODY):
                        turned(r, it * BODY + j + 1, j + 1, next_whole and j == BODY - 1)
                        if beside is not None:
                            beside(it, j)
                        copied(r, it * BODY + j, j, it * (BODY // 2) + j // 2)

                turned(r, 0, 0)
                products_out(before)
                with act.Fori(0, BODIES - 2) as it:
                    body(it)
                body(BODIES - 2, whole)
                for j in range(BODY):
                    i = r.nt - BODY + j
                    if j < BODY - 1:
                        turned(r, i + 1, j + 1, whole)
                    if j == 1 and group is not None:
                        exponential(group)
                    copied(r, i, j, i // 2, whole)

            def products_out(r):
                for b in range(2):
                    act.wait_ge(phase[r].y_stored[b].sem, phase[r].y_stored[b].landed(r.nt // 2 - 1))

            turned(GATE, 0, 0)
            with act.Fori(0, GATE.nt // 4 - 1) as it:
                for j in range(4):
                    turned(GATE, it * 4 + j + 1, j + 1)
                    copied(GATE, it * 4 + j, j, it * 2 + j // 2)
            for j in range(4):
                i = GATE.nt - 4 + j
                if j < 3:
                    turned(GATE, i + 1, j + 1)
                copied(GATE, i, j, i // 2)

            def inner(t, b, turn):
                act.wait_ge(c_got[b].sem, c_got[b].landed(turn, 64))
                gate_0, up_0 = in4[b][0], in4[b][2]
                act.activation(gate_0, gate_0, ACT.Copy, scale=comb["gate"][:, 0, ds(t, 1)]).then_inc(c_y0.sem, 1)
                act.activation(up_0, up_0, ACT.Copy, scale=comb["up"][:, 0, ds(t, 1)]).then_inc(c_z0.sem, 1)
                act.wait_ge(c_g.sem, c_g.after(t))
                act.activation(gate_0, gate_0, ACT.Silu).then_inc(c_h.sem, 1)

            def inner_turned(t, first):
                act.wait_ge(c_t_mm.sem, c_t_mm.after(t))
                act.wait_ge(c_log_mm.sem, c_log_mm.room(t))
                for h in range(2):
                    ins = act.activation(inter_t[:, h * 512:(h + 1) * 512], bank[first + 2 * h][:, :], ACT.Copy)
                ins.then_inc(c_t_ready.sem, 1)

            def inner_beside(h, first):
                def part(it, j):
                    if j in FIRST_PARTS:
                        k = FIRST_PARTS.index(j)
                        inner(it * 4 + (h * H + k), k % 2, it * 2 + (h * H // 2 + k // 2))
                    if j in SECOND_PARTS:
                        inner_turned(it * 4 + (h * H + SECOND_PARTS.index(j)), first)
                return part

            def output(t, b, turn):
                act.wait_ge(o_got[b].sem, o_got[b].landed(turn, 32))
                act.activation(in2[b][0], in2[b][0], ACT.Copy,
                               scale=comb["down"][:, 0, ds(t, 1)]).then_inc(o_y0.sem, 1)

            def output_beside(it, j):
                if j in SECOND_PARTS:
                    k = SECOND_PARTS.index(j)
                    output(it * 4 + k, k, it)

            sorted_tiles(UP[0], GATE)
            sorted_tiles(UP[1], UP[0], inner_beside(0, 1), 2)
            sorted_tiles(DOWN[0], UP[1], inner_beside(1, 5), 3)
            sorted_tiles(DOWN[1], DOWN[0], output_beside)
            with act.Fori(0, H // 4) as it:
                for b in range(4):
                    output(it * 4 + (H + b), b, it + H // 4)

        @block.tensor
        def _(pe):
            give(pe, v_mm, sim_mm, linkt_mm, kv_mm, mix_mm, proj_mm, x2t_mm, logit_mm, table_mm, c_t_mm, c_log_mm,
                 *(s for r in ROUTES for s in (phase[r].xt_mm, phase[r].y_mm)))
            pe.wait_ge(consts_made.sem, consts_made.after(0))
            pe.wait_ge(consts_loaded.sem, 16 * CONSTS)

            def turn_rows(src, first):
                for k in range(KD):
                    for s in range(SUB):
                        ins = pe.transpose(bank[first + k][:, s * P:(s + 1) * P], src[:, s, k * P:(k + 1) * P],
                                           ident[:, :])
                return ins

            def transposes(m):
                pe.wait_ge(xh_ready.sem, xh_ready.after(m))
                pe.wait_ge(nt_ready.sem, nt_ready.room(m))
                turn_rows(xh, 0).then_inc(xt_mm.sem, 1)

            def projections(m, b):
                pe.wait_ge(nt_ready.sem, nt_ready.after(m))
                pe.wait_ge(sim_read.sem, sim_read.room(m))
                for k in range(KD):
                    ins = pe.matmul(bank[2][:, :], wqk_sb[:, k, :], nt_s[b][:, k, :], start=(k == 0),
                                    stop=(k == KD - 1))
                ins.then_inc(qk_mm.sem, 1)
                for c in range(KH):
                    pe.wait_ge(gate_ready.sem, gate_ready.room(m * KH + c))
                    for k in range(KD):
                        ins = pe.matmul(bank[3 + c % 2][:, :], wh_sb[:, k, HID + c * P:HID + (c + 1) * P],
                                        nt_s[b][:, k, :], start=(k == 0), stop=(k == KD - 1))
                    ins.then_inc(gate_mm.sem, 1)
                for s in range(SUB):
                    pe.wait_ge(v_biased.sem, v_biased.room(m * SUB + s))
                    for k in range(KD):
                        ins = pe.matmul(bank[5 + s % 2][:, :], nt_s[b][:, k, s * P:(s + 1) * P], wh_sb[:, k, 0:HID],
                                        start=(k == 0), stop=(k == KD - 1))
                    ins.then_inc(v_mm.sem, 1)

            def groups(m, b):
                pe.wait_ge(quad_ready.sem, quad_ready.after(m))
                pe.wait_ge(qkt_ready.sem, qkt_ready.after(m))
                for s in range(SUB):
                    c = slice(s * P, (s + 1) * P)
                    ins = pe.matmul(bank[2][:, c], quad_k[:, c], quad_q[:, c], start=True, stop=True)
                ins.then_inc(sim_mm.sem, 1)
                pe.wait_ge(link_ready.sem, link_ready.after(m))
                pe.wait_ge(kv_used.sem, kv_used.room(m))
                for s in range(SUB):
                    c = slice(s * P, (s + 1) * P)
                    ins = pe.transpose(bank[7][:, c], lin_k[:, c], ident[:, :])
                ins.then_inc(linkt_mm.sem, 1)
                pe.wait_ge(linkn_ready.sem, linkn_ready.after(m))
                pe.wait_ge(v_ready.sem, v_ready.after(m * SUB + SUB - 1))
                for s in range(SUB):
                    ins = pe.matmul(bank[7][:, :], link_n[:, s, :], v_st[b][:, s, :], start=(s == 0),
                                    stop=(s == SUB - 1))
                ins.then_inc(kv_mm.sem, 1)

            transposes(0)
            with pe.Fori(0, M // 2 - 1) as it:
                for b in range(2):
                    m = it * 2 + b
                    projections(m, b)
                    transposes(m + 1)
                    groups(m, b)
            for b in range(2):
                m = M - 2 + b
                projections(m, b)
                if b == 0:
                    transposes(m + 1)
                groups(m, b)

            pe.wait_ge(kv_final.sem, kv_final.after(0))
            pe.wait_ge(linq_ready.sem, linq_ready.after(M - 1))
            def mix(m, b, turn):
                pe.wait_ge(v_back[b].sem, v_back[b].landed(turn))
                for c in range(KH):
                    pe.wait_ge(gated_ready.sem, gated_ready.after(m * KH + c - KH))
                    pe.matmul(bank[c][:, :], lin_kv[:, c * P:(c + 1) * P], linq_t[:, ds(m * MT, MT)],
                              start=True, stop=False, skip_group_check=True)
                    for s in range(SUB):
                        ins = pe.matmul(bank[c][:, s * P:(s + 1) * P], v_st[b][:, s, c * P:(c + 1) * P],
                                        attn_t[:, ds(m * SUB + s, 1), :].rearrange("p a b -> p (a b)"),
                                        start=False, stop=(s == SUB - 1), skip_group_check=True)
                    ins.then_inc(mix_mm.sem, 1)

            def project(m):
                pe.wait_ge(gated_ready.sem, gated_ready.after(m * KH + KH - 1))
                for h in range(2):
                    pe.wait_ge(proj_used.sem, proj_used.room(m * 2 + h))
                    for s in (2 * h, 2 * h + 1):
                        for c in range(KH):
                            ins = pe.matmul(bank[4 + h][:, (s % 2) * D:(s % 2 + 1) * D],
                                            gated[c][:, s * P:(s + 1) * P], wo_sb[:, c, :], start=(c == 0),
                                            stop=(c == KH - 1))
                    ins.then_inc(proj_mm.sem, 1)

            def turn_x2(m):
                pe.wait_ge(x2_ready.sem, x2_ready.after(m))
                pe.wait_ge(lg_ready.sem, lg_ready.room(m))
                turn_rows(x2h, 6).then_inc(x2t_mm.sem, 1)

            def logits(m):
                pe.wait_ge(x2t_ready.sem, x2t_ready.after(m))
                for s in range(SUB):
                    for k in range(KD):
                        ins = pe.matmul(bank[6][:, s * 2 * E:(s + 1) * 2 * E], x2t_s[:, k, s * P:(s + 1) * P],
                                        rt_sb[:, k, :], start=(k == 0), stop=(k == KD - 1))
                ins.then_inc(logit_mm.sem, 1)

            mix(0, 0, 0)
            project(0)
            mix(1, 1, 0)
            project(1)
            turn_x2(0)
            with pe.Fori(0, M // 2 - 1) as it:
                for b in range(2):
                    m = it * 2 + b
                    mix(m + 2, b, it + 1)
                    logits(m)
                    project(m + 2)
                    turn_x2(m + 1)
            logits(M - 2)
            turn_x2(M - 1)
            logits(M - 1)

            def ranks(g, first):
                pe.wait_ge(occ_ready.sem, occ_ready.after(g.n))
                o = occ[g.n % 2][:, 0:g.words]
                w = g.words
                pe.matmul(bank[first][:, 0:w], before[:, :], o, start=True, stop=True)
                pe.matmul(bank[first][:, w:2 * w], ones[:, :], o, start=True, stop=True).then_inc(rank_mm.sem, 1)

            def open_table(r, at):
                for part in range(2):
                    pe.matmul(bank[at][:, part * r.nt:(part + 1) * r.nt], zeros[:, :], zeros[:, 0:r.nt], start=True,
                              stop=False, skip_group_check=True)

            def add_to_table(r, batch, b, at):
                pe.wait_ge(onehot_ready.sem, onehot_ready.after(batch + r.batches_before))
                w = 2 * r.nt
                for k in range(2 * B):
                    ins = pe.matmul(bank[at][:, 0:w], one_hots_of[r].row[b][:, k, :],
                                    one_hots_of[r].tile[b][:, k * w:(k + 1) * w], start=False, stop=False,
                                    skip_group_check=True)
                ins.then_inc(table_mm.sem, 1)

            def table(r, at):
                open_table(r, at)
                with pe.Fori(0, r.tiles // B // 2) as it:
                    for b in range(2):
                        add_to_table(r, it * 2 + b, b, at)

            def halved(r, i):
                return not isinstance(i, int) or i < r.whole_from

            def turn(r, i, j, landing):
                n = phase[r]
                pe.wait_ge(n.gathered[j % 4].sem, n.gathered[j % 4].landed(landing))
                pe.wait_ge(n.xt_ready.sem, n.xt_ready.room(i))
                kc, rows = KD, rows_in
                if r.matrix == "down":
                    if halved(r, i - 2):
                        pe.wait_ge(n.half_ready.sem, n.half_ready.room(i))
                    kc, rows = KI, rows_down
                for k in range(kc):
                    ins = pe.transpose(bank[2 * (j % 2) + k // 4][:, (k % 4) * P:(k % 4 + 1) * P],
                                       rows[j % 4][:, k * P:(k + 1) * P], ident[:, :])
                ins.then_inc(n.xt_mm.sem, 1)

            def product(r, i, j, amid=None):
                n = phase[r]
                e = pe.value_load(expert_of[r.group][0:1, ds(i + r.tiles_before, 1)], min_val=0, max_val=E - 1)
                pe.wait_ge(w_ready.sem, w_ready.after(e + r.column * E))
                pe.wait_ge(n.xt_ready.sem, n.xt_ready.after(i))
                kc, width = KD, INNER
                if r.matrix == "down":
                    kc, width = KI, D
                    if halved(r, i):
                        pe.wait_ge(n.half_ready.sem, n.half_ready.after(i))
                pe.wait_ge(n.y0_ready.sem, n.y0_ready.room(i))
                if r.matrix != "down" and halved(r, i - 2):
                    pe.wait_ge(n.half_ready.sem, n.half_ready.room(i))
                w = min(width, 512)
                steps = [(h, k) for h in range(width // w) for k in range(kc)]
                for part in range(2):
                    if part == 1 and amid is not None:
                        amid()
                    for h, k in steps[part * len(steps) // 2:(part + 1) * len(steps) // 2]:
                        ins = pe.matmul(bank[4 + 2 * (j % 2) + h][:, 0:w], rows_t[j % 2][:, k * P:(k + 1) * P],
                                        w_sb[:, ds(e * SLAB + (k * width + h * w), w)],
                                        start=(k == 0), stop=(k == kc - 1))
                ins.then_inc(n.y_mm.sem, 1)

            ranks(GROUPS[0], 0)
            ranks(GROUPS[1], 2)
            table(GATE, 4)
            pe.wait_ge(routed.sem, routed.after(GATE.n))
            open_table(UP[0], 1)
            open_table(UP[1], 3)
            turn(GATE, 0, 0, 0)

            def gate_tiles(it):
                for j in range(4):
                    turn(GATE, it * 4 + j + 1, j + 1, it + (j + 1) // 4)
                    product(GATE, it * 4 + j, j)

            for h in range(2):
                with pe.Fori(0, H // B // 2) as it:
                    for half in range(2):
                        gate_tiles(it * 2 + (h * H // B + half))
                        add_to_table(UP[h], it * 2 + half, half, 1 + 2 * h)
            with pe.Fori(T // B, GATE.nt // 4 - 1) as it:
                gate_tiles(it)
            for j in range(4):
                if j < 3:
                    turn(GATE, GATE.nt - 4 + j + 1, j + 1, GATE.nt // 4 - 1)
                product(GATE, GATE.nt - 4 + j, j)

            def turn_inner(t, b, first):
                pe.wait_ge(c_done.sem, c_done.after(t))
                pe.wait_ge(c_lg.sem, c_lg.room(t))
                for k in range(KI):
                    ins = pe.transpose(bank[first + 2 * (k // 4)][:, (k % 4) * P:(k % 4 + 1) * P],
                                       inter[b][:, k * P:(k + 1) * P], ident[:, :])
                ins.then_inc(c_t_mm.sem, 1)

            def inner_logits(t, first):
                pe.wait_ge(c_t_ready.sem, c_t_ready.after(t))
                for k in range(KI):
                    ins = pe.matmul(bank[first][:, 0:E], inter_t[:, k * P:(k + 1) * P], rd_sb[:, k, :],
                                    start=(k == 0), stop=(k == KI - 1))
                ins.then_inc(c_log_mm.sem, 1)

            def sorted_tiles(r, before, inner_of=None, first=None, after=None):
                def body(it):
                    for j in range(BODY):
                        turn(r, it * BODY + j + 1, j + 1, it * 2 + (j + 1) // 4)
                        beside = j in SECOND_PARTS and inner_of is not None
                        if beside:
                            k = SECOND_PARTS.index(j)
                            t = it * 4 + (inner_of * H + k)
                            product(r, it * BODY + j, j, lambda: turn_inner(t, k % 2, first))
                            inner_logits(t, first)
                        else:
                            product(r, it * BODY + j, j)

                turn(r, 0, 0, 0)
                products_copied(before)
                with pe.Fori(0, BODIES - 2) as it:
                    body(it)
                body(BODIES - 2)
                batches = H // B
                for j in range(BODY):
                    i = r.nt - BODY + j
                    if j < BODY - 1:
                        turn(r, i + 1, j + 1, (i + 1) // 4)
                    product(r, i, j)
                    if j == 0 and after is not None:
                        ranks(after.group, first)
                        open_table(after, first + 2)
                    if j >= BODY - batches and after is not None:
                        batch = j - (BODY - batches)
                        add_to_table(after, batch, batch % 2, first + 2)

            def products_copied(r):
                pe.wait_ge(phase[r].y0_ready.sem, phase[r].y0_ready.after(r.nt - 1))
                if r.matrix != "down":
                    pe.wait_ge(phase[r].half_ready.sem, phase[r].half_ready.after(r.whole_from - 1))

            pe.wait_ge(routed.sem, routed.after(UP[1].n))
            sorted_tiles(UP[0], GATE)
            sorted_tiles(UP[1], UP[0], 0, 1, DOWN[0])
            pe.wait_ge(routed.sem, routed.after(DOWN[0].n))
            sorted_tiles(DOWN[0], UP[1], 1, 5, DOWN[1])
            pe.wait_ge(routed.sem, routed.after(DOWN[1].n))
            sorted_tiles(DOWN[1], DOWN[0])

        @block.vector
        def _(dve):
            give(dve, quad_ready, v_biased, sim_read, kv_used, gated_ready, proj_used, lg_ready, c_done, c_lg,
                 o_ready, *(phase[r].half_ready for r in ROUTES))
            step = Steps()
            for a, n in ((keep, T), (keep_half, H), (restart_e, E)):
                dve.memset(a[:, :], 1.0).then_inc(dve_step.sem, 1)
                dve.wait_ge(dve_step.sem, step.next())
                dve.memset(a[:, :].rearrange("p (e t) -> p e t", t=n)[:, :, 0:1], 0.0).then_inc(dve_step.sem, 1)
                dve.wait_ge(dve_step.sem, step.next())

            def inverse_root(dst, src, n):
                dve.tensor_scalar(root_in[:, :], src, EPS, None, ALU.add).then_inc(root_asked.sem, 1)
                dve.wait_ge(root_asked.sem, root_asked.after(n))
                dve.wait_ge(root_made.sem, root_made.after(n))
                dve.reciprocal(dst[:, :], root[:, :]).then_inc(dve_step.sem, 1)
                dve.wait_ge(dve_step.sem, step.next())
                dve.tensor_tensor(corr[:, :], root_in[:, :], dst[:, :], ALU.mult).then_inc(dve_step.sem, 1)
                dve.wait_ge(dve_step.sem, step.next())
                dve.tensor_tensor(corr[:, :], corr[:, :], dst[:, :], ALU.mult).then_inc(dve_step.sem, 1)
                dve.wait_ge(dve_step.sem, step.next())
                dve.tensor_scalar(corr[:, :], corr[:, :], -0.5, 1.5, ALU.mult, ALU.add).then_inc(dve_step.sem, 1)
                dve.wait_ge(dve_step.sem, step.next())
                dve.tensor_tensor(dst[:, :], dst[:, :], corr[:, :], ALU.mult).then_inc(dve_step.sem, 1)
                dve.wait_ge(dve_step.sem, step.next())

            def tile_of(t):
                return x_sb[:, ds(t, 1), :].rearrange("p a d -> p (a d)")

            def centred(dst, m, scale):
                for s in range(SUB):
                    t = m * SUB + s
                    ins = dve.tensor_scalar(dst[:, s, :], tile_of(t), mean[:, ds(t, 1)], scale[:, ds(t, 1)],
                                            ALU.subtract, ALU.mult)
                return ins

            def chunk_stats(c):
                n = T // 4
                alone(dve)
                for t in range(n):
                    ins = dve.bn_stats(stats[:, t, :], tile_of(c * n + t))
                ins.then_inc(dve_step.sem, 1)
                dve.wait_ge(dve_step.sem, step.next())
                alone(dve)
                for t in range(n):
                    ins = dve.bn_aggr(mv[:, t, :], stats[:, t, :])
                ins.then_inc(dve_step.sem, 1)
                dve.wait_ge(dve_step.sem, step.next())
                alone(dve)
                dve.tensor_copy(mean[:, ds(c * n, n)], mv[:, :, 0])
                inverse_root(rstd8, mv[:, :, 1], c * 2)
                dve.tensor_copy(rstd[:, ds(c * n, n)], rstd8[:, :])
                dve.tensor_tensor(corr[:, :], rstd8[:, :], rstd8[:, :], ALU.mult).then_inc(dve_step.sem, 1)
                dve.wait_ge(dve_step.sem, step.next())
                dve.tensor_tensor(var8[:, :], mv[:, :, 1], corr[:, :], ALU.mult).then_inc(dve_step.sem, 1)
                dve.wait_ge(dve_step.sem, step.next())
                inverse_root(rstd8_2, var8[:, :], c * 2 + 1)
                alone(dve)
                dve.tensor_tensor(rstd12[:, ds(c * n, n)], rstd8_2[:, :], rstd8[:, :], ALU.mult)\
                    .then_inc(dve_step.sem, 1)
                dve.wait_ge(dve_step.sem, step.next())

            dve.wait_ge(x_loaded[0].sem, x_loaded[0].landed(0))
            chunk_stats(0)
            centred(xh, 0, rstd12).then_inc(xh_ready.sem, 1)

            dve.wait_ge(buckets_loaded.sem, buckets_loaded.landed(0))
            dve.wait_ge(consts_made.sem, consts_made.after(0))
            dve.tensor_tensor(bias_oh, buckets.unsqueeze(2).to_broadcast([P, G, BUCKETS]),
                              iota[:, 0:BUCKETS].unsqueeze(1).to_broadcast([P, G, BUCKETS]),
                              ALU.is_equal).then_inc(bucket_oh.sem, 1)
            dve.wait_ge(consts_loaded.sem, 16 * CONSTS)
            dve.wait_ge(emb_chosen.sem, emb_chosen.after(0))
            dve.tensor_reduce(sim_s[:, 0, 0:G], bias_oh, AX.X, ALU.add).then_inc(dve_step.sem, 1)
            dve.wait_ge(dve_step.sem, step.next())
            dve.memset(bias_t, OFF_GROUP).then_inc(dve_step.sem, 1)
            dve.wait_ge(dve_step.sem, step.next())
            dve.memset(lin_kv, 0.0).then_inc(dve_step.sem, 1)
            dve.wait_ge(dve_step.sem, step.next())
            for h in range(2):
                block_h = slice(h * G, (h + 1) * G)
                dve.tensor_scalar(bias_t[block_h, block_h], sim_s[block_h, 0, 0:G], BIAS_SCALE, None,
                                  ALU.mult).then_inc(dve_step.sem, 1)
                dve.wait_ge(dve_step.sem, step.next())

            def first_pass(m, last):
                if not last:
                    dve.wait_ge(xt_mm.sem, xt_mm.after(m))
                    centred(xh, m + 1, rstd12).then_inc(xh_ready.sem, 1)
                dve.wait_ge(qkt_ready.sem, qkt_ready.after(m))
                dve.wait_ge(sim_mm.sem, sim_mm.room(m))
                dve.tensor_scalar(quad_q, qk_t, gamma_col[:, 0:1], beta_col[:, 0:1], ALU.mult, ALU.add)
                dve.tensor_scalar(quad_k, qk_t, gamma_col[:, 2:3], beta_col[:, 2:3], ALU.mult,
                                  ALU.add).then_inc(quad_ready.sem, 1)
                for s in range(SUB):
                    dve.wait_ge(v_mm.sem, v_mm.after(m * SUB + s))
                    dve.wait_ge(v_ready.sem, v_ready.room(m * SUB + s))
                    dve.tensor_tensor(v_tmp[:, s % 2, :], bank[5 + s % 2][:, :], bv_row, ALU.add)\
                        .then_inc(v_biased.sem, 1)
                dve.wait_ge(linkt_mm.sem, linkt_mm.after(m))
                dve.wait_ge(kv_mm.sem, kv_mm.after(m - 1))
                dve.tensor_copy(link_n.rearrange("p s q -> p (s q)"), bank[7][:, :]).then_inc(linkn_ready.sem, 1)
                dve.wait_ge(sim_mm.sem, sim_mm.after(m))
                dve.scalar_tensor_tensor(
                    out=sim_s, in0=bank[2][:, :].rearrange("p (s q) -> p s q", s=SUB), scalar=SIM_SCALE,
                    in1=bias_t.unsqueeze(1).to_broadcast([P, SUB, P]), op0=ALU.mult, op1=ALU.add)\
                    .then_inc(sim_read.sem, 1)
                dve.wait_ge(sim_read.sem, sim_read.after(m))
                dve.scalar_tensor_tensor(out=attn_t[:, ds(m * SUB, SUB), :], in0=sim_s, scalar=0.0, in1=sim_s,
                                         op0=ALU.max, op1=ALU.mult)
                dve.wait_ge(kv_mm.sem, kv_mm.after(m))
                dve.tensor_tensor(lin_kv, lin_kv, bank[7][:, :], ALU.add).then_inc(kv_used.sem, 1)

            for c in range(1, 4):
                dve.wait_ge(x_loaded[c].sem, x_loaded[c].landed(0))
            with dve.Fori(0, M // 2 - 1) as it:
                step.enter(it, 15)
                first_pass(it * 2, False)
                chunk_stats(it + 1)
                first_pass(it * 2 + 1, False)
            step.leave(M // 2 - 1)
            first_pass(M - 2, False)
            first_pass(M - 1, True)
            dve.wait_ge(kv_used.sem, kv_used.after(M - 1))
            dve.tensor_scalar(lin_kv, lin_kv, 1.0 / TOK, None, ALU.mult).then_inc(kv_final.sem, 1)

            def second_pass(m, b, turn, x2_before, top_before):
                dve.wait_ge(x1_ready.sem, x1_ready.room(m))
                centred(xn_s, m, rstd).then_inc(xn_ready.sem, 1)
                dve.wait_ge(gate_back[b].sem, gate_back[b].landed(turn))
                dve.wait_ge(proj_mm.sem, proj_mm.after(m * 2 - 1))
                for c in range(KH):
                    dve.wait_ge(mix_mm.sem, mix_mm.after(m * KH + c))
                    dve.tensor_tensor(gated[c], bank[c][:, :], gate_st[b][:, c, :], ALU.mult)\
                        .then_inc(gated_ready.sem, 1)
                if top_before:
                    take_logits(m - 2)
                if x2_before:
                    normalise(m - 1)
                for h in range(2):
                    dve.wait_ge(proj_mm.sem, proj_mm.after(m * 2 + h))
                    dve.tensor_tensor(proj_s[:, 2 * h:2 * h + 2, :],
                                      bank[4 + h][:, :].rearrange("p (s d) -> p s d", s=2),
                                      bo_row.unsqueeze(1).to_broadcast([P, 2, D]), ALU.add)\
                        .then_inc(proj_used.sem, 1)
                if top_before:
                    top_of_macro(m - 2)

            def normalise(m):
                dve.wait_ge(x1_ready.sem, x1_ready.after(m))
                alone(dve)
                for s in range(SUB):
                    ins = dve.bn_stats(stats[:, s, :], tile_of(m * SUB + s))
                ins.then_inc(dve_step.sem, 1)
                dve.wait_ge(dve_step.sem, step.next())
                alone(dve)
                for s in range(SUB):
                    ins = dve.bn_aggr(mv[:, s, :], stats[:, s, :])
                ins.then_inc(dve_step.sem, 1)
                dve.wait_ge(dve_step.sem, step.next())
                dve.tensor_scalar(root4_in[:, :], mv[:, 0:SUB, 1], EPS, None, ALU.add).then_inc(root4_asked.sem, 1)
                dve.wait_ge(root4_asked.sem, root4_asked.after(m))
                dve.wait_ge(root4_made.sem, root4_made.after(m))
                dve.reciprocal(rstd4[:, :], root4[:, :]).then_inc(dve_step.sem, 1)
                dve.wait_ge(dve_step.sem, step.next())
                dve.tensor_tensor(corr4[:, :], root4_in[:, :], rstd4[:, :], ALU.mult).then_inc(dve_step.sem, 1)
                dve.wait_ge(dve_step.sem, step.next())
                dve.tensor_tensor(corr4[:, :], corr4[:, :], rstd4[:, :], ALU.mult).then_inc(dve_step.sem, 1)
                dve.wait_ge(dve_step.sem, step.next())
                dve.tensor_scalar(corr4[:, :], corr4[:, :], -0.5, 1.5, ALU.mult, ALU.add).then_inc(dve_step.sem, 1)
                dve.wait_ge(dve_step.sem, step.next())
                dve.tensor_tensor(rstd4[:, :], rstd4[:, :], corr4[:, :], ALU.mult).then_inc(dve_step.sem, 1)
                dve.wait_ge(dve_step.sem, step.next())
                dve.wait_ge(x2t_mm.sem, x2t_mm.room(m))
                dve.wait_ge(x2_stored.sem, x2_stored.sent(m))
                for s in range(SUB):
                    ins = dve.tensor_scalar(x2h[:, s, :], tile_of(m * SUB + s), mv[:, s, 0:1], rstd4[:, s:s + 1],
                                            ALU.subtract, ALU.mult)
                ins.then_inc(x2_ready.sem, 1)

            def take_logits(m):
                dve.wait_ge(logit_mm.sem, logit_mm.after(m))
                dve.tensor_copy(lg[:, :, :, :].rearrange("p s j e -> p (s j e)"), bank[6][:, 0:SUB * 2 * E])\
                    .then_inc(lg_ready.sem, 1)

            def top_of_macro(m):
                dve.wait_ge(lg_ready.sem, lg_ready.after(m))
                alone(dve)
                pick_two(SUB, 2, lambda table, got, j: dve.tensor_copy(
                    table[:, j, :, ds(m * SUB, SUB)].rearrange("p k s -> p s k"), got[:, :, j, 0:2]))

            def pick_two(subs, routes, put):
                pairs = [(s, j) for s in range(subs) for j in range(routes)]
                for s, j in pairs:
                    ins = dve.max(mx[:, s, j, :], lg[:, s, j, :])
                ins.then_inc(dve_step.sem, 1)
                dve.wait_ge(dve_step.sem, step.next())
                alone(dve)
                for s, j in pairs:
                    ins = dve.max_index(mi[:, s, j, :], mx[:, s, j, :], lg[:, s, j, :])
                ins.then_inc(dve_step.sem, 1)
                dve.wait_ge(dve_step.sem, step.next())
                alone(dve)
                for table, got in ((top_v, mx), (top_i, mi)):
                    for j in range(routes):
                        ins = put(table, got, j)
                ins.then_inc(dve_step.sem, 1)
                dve.wait_ge(dve_step.sem, step.next())

            second_pass(0, 0, 0, False, False)
            second_pass(1, 1, 0, True, False)
            with dve.Fori(0, M // 2 - 1) as it:
                step.enter(it, 20)
                for b in range(2):
                    second_pass(it * 2 + (b + 2), b, it + 1, True, True)
            step.leave(M // 2 - 1)
            take_logits(M - 2)
            normalise(M - 1)
            top_of_macro(M - 2)
            take_logits(M - 1)
            top_of_macro(M - 1)

            def sized(a, g):
                return a[:, 0:g.words].rearrange("p (g e t) -> p g e t", g=g.count, e=E)

            def by_expert(a, g, n):
                return a[:, 0:g.count * E].rearrange("p (g e) -> p g e", e=E).unsqueeze(3).to_broadcast(
                    [P, g.count, E, n])

            def occupancy(g):
                c, at = comb[g.matrix], g.at
                dve.tensor_tensor(c[:, 0, at], top_v[:, g.column, 1, at], top_v[:, g.column, 0, at], ALU.subtract)\
                    .then_inc(exp_asked.sem, 1)
                o, shape = oh[g.n % 2], [P, g.count, E, g.tiles]
                for k in range(2):
                    ins = dve.tensor_tensor(
                        sized(o[k], g), iota[:, 0:E].unsqueeze(1).unsqueeze(3).to_broadcast(shape),
                        top_i[:, g.column, k, at].rearrange("p (g t) -> p g t", g=g.count).unsqueeze(2)
                        .to_broadcast(shape), ALU.is_equal)
                ins.then_inc(dve_step.sem, 1)
                dve.wait_ge(dve_step.sem, step.next())
                w = g.words
                dve.tensor_tensor(occ[g.n % 2][:, 0:w], o[0][:, 0:w], o[1][:, 0:w], ALU.add)\
                    .then_inc(occ_ready.sem, 1)

            def take_ranks(g, first):
                dve.wait_ge(rank_mm.sem, rank_mm.after(g.n))
                w = g.words
                dve.tensor_copy(within[g.n % 2][:, 0:w], bank[first][:, 0:w])
                dve.tensor_copy(tot[g.n % 2][:, 0:w], bank[first][:, w:2 * w]).then_inc(dve_step.sem, 1)
                dve.wait_ge(dve_step.sem, step.next())

            def places(g):
                def then(ins):
                    ins.then_inc(dve_step.sem, 1)
                    dve.wait_ge(dve_step.sem, step.next())

                c, at, n, w, ge = comb[g.matrix], g.at, g.tiles, g.words, g.count * E
                t_f, in_f, ra_f = tot[g.n % 2][:, 0:w], incl[:, 0:w], rank[:, 0:w]
                restart = (keep if n == T else keep_half)[:, 0:w]
                then(dve.tensor_tensor_scan(in_f, restart, t_f, 0.0, ALU.mult, ALU.add))
                then(dve.tensor_tensor(ra_f, in_f, t_f, ALU.subtract))
                dve.tensor_tensor(ra_f, ra_f, within[g.n % 2][:, 0:w], ALU.add)
                then(dve.tensor_scalar(load_e[:, 0:ge].rearrange("p (g e) -> p g e", e=E),
                                       sized(incl, g)[:, :, :, n - 1], 1.0 / P, None, ALU.mult))
                then(dve.tensor_tensor(sized(full, g), by_expert(load_e, g, n),
                                       iota[:, 0:n].unsqueeze(1).unsqueeze(1).to_broadcast([P, g.count, E, n]),
                                       ALU.is_gt))
                then(dve.tensor_reduce(tiles_e[:, 0:ge], full[:, 0:w].rearrange("p (e t) -> p e t", t=n), AX.X,
                                       ALU.add))
                then(dve.tensor_tensor_scan(end_e[:, 0:ge], restart_e[:, 0:ge], tiles_e[:, 0:ge], 0.0, ALU.mult,
                                            ALU.add))
                then(dve.tensor_tensor(base_e[:, 0:ge], end_e[:, 0:ge], tiles_e[:, 0:ge], ALU.subtract))
                then(dve.tensor_scalar(base_e[:, 0:ge], base_e[:, 0:ge], float(P), None, ALU.mult))
                then(dve.tensor_tensor(sized(rank, g), sized(rank, g), by_expert(base_e, g, n), ALU.add))
                for k in range(2):
                    then(dve.tensor_tensor(full[:, 0:w], oh[g.n % 2][k][:, 0:w], ra_f, ALU.mult))
                    then(dve.tensor_reduce(pos_f[:, at, k].rearrange("p (g t) -> p g t", g=g.count),
                                           sized(full, g).rearrange("p g e t -> p g t e"), AX.X, ALU.add))
                p = pos[g.matrix]
                then(dve.tensor_copy(p[:, at, :], pos_f[:, at, :]))
                dve.tensor_scalar(pa_i[:, at, :], p[:, at, :], 7, None, ALU.logical_shift_right)
                then(dve.tensor_scalar(pb_i[:, at, :], p[:, at, :], P - 1, None, ALU.bitwise_and))
                dve.tensor_copy(pa_h[:, at, :], pa_i[:, at, :])
                then(dve.tensor_copy(pb_h[:, at, :], pb_i[:, at, :]))

            def experts(g):
                def then(ins):
                    ins.then_inc(dve_step.sem, 1)
                    dve.wait_ge(dve_step.sem, step.next())

                c, at, n, ge = comb[g.matrix], g.at, g.count * g.nt, g.count * E
                ends = one_hots_of[g.routes[0]].ends
                e4 = ends[:, 0:n * E].rearrange("p (g i e) -> p g i e", g=g.count, e=E)
                dve.wait_ge(exp_made.sem, exp_made.after(g.n))
                dve.tensor_scalar(c[:, 0, at], c[:, 1, at], 1.0, None, ALU.add)
                then(dve.tensor_tensor(
                    e4, end_e[0:1, 0:ge].rearrange("p (g e) -> p g e", e=E).unsqueeze(2).to_broadcast(
                        [1, g.count, g.nt, E]),
                    iota[0:1, 0:g.nt].unsqueeze(1).unsqueeze(3).to_broadcast([1, g.count, g.nt, E]), ALU.is_le))
                dve.reciprocal(c[:, 0, at], c[:, 0, at])
                then(dve.tensor_reduce(ex_f[:, 0:n], ends[:, 0:n * E].rearrange("p (i e) -> p i e", e=E), AX.X,
                                       ALU.add))
                dve.tensor_tensor(c[:, 1, at], c[:, 1, at], c[:, 0, at], ALU.mult)
                then(dve.tensor_scalar(ex_f[:, 0:n], ex_f[:, 0:n], float(E - 1), None, ALU.min))
                last = g.routes[-1]
                if last in run_counts:
                    credits, base = phase[last].y_mm.credits, last.tiles_before // last.nt * E
                    counts = run_counts[last]
                    dve.memset(counts[:, E - 1:E], last.nt + credits)
                    then(dve.tensor_scalar(load_e[0:1, 0:E], end_e[0:1, base:base + E], float(credits), None,
                                           ALU.add))
                    dve.tensor_copy(counts[:, 0:E - 1], load_e[0:1, 0:E - 1])
                then(dve.tensor_copy(expert_of[g][:, :], ex_f[:, 0:n]))

            def one_hots(r, batch, b):
                dve.wait_ge(table_mm.sem, table_mm.room(batch + r.batches_before))

                def spread(a, width, first=r.first):
                    rows = a[:, ds(batch * B + first, B), :].rearrange("p t k -> p (t k)")
                    return rows.unsqueeze(2).to_broadcast([P, 2 * B, width])

                row_oh = one_hots_of[r].row[b]
                parts = one_hots_of[r].tile[b][:, 0:4 * B * r.nt].rearrange("p (t c i) -> p t c i", c=2, i=r.nt)
                of_part, of_start = parts[:, :, 0, :], parts[:, :, 1, :]
                dve.tensor_tensor(of_start, iota_h[:, 0:r.nt].unsqueeze(1).to_broadcast([P, 2 * B, r.nt]),
                                  spread(pa_h, r.nt), ALU.is_equal).then_inc(dve_step.sem, 1)
                dve.tensor_tensor(row_oh, iota_h[:, :].unsqueeze(1).to_broadcast([P, 2 * B, P]), spread(pb_h, P),
                                  ALU.is_equal)
                dve.wait_ge(dve_step.sem, step.next())
                dve.tensor_scalar(of_part, of_start, part[:, :], None, ALU.mult)
                dve.tensor_tensor(of_start, of_start, spread(start_h, r.nt, 0 if r.matrix == "down" else r.first),
                                  ALU.mult).then_inc(onehot_ready.sem, 1)

            def table(r, at):
                with dve.Fori(0, r.tiles // B // 2) as it:
                    step.enter(it, 2)
                    for b in range(2):
                        one_hots(r, it * 2 + b, b)
                step.leave(r.tiles // B // 2)
                close_table(r, at)

            def close_table(r, at):
                dve.wait_ge(table_mm.sem, table_mm.after(r.tiles // B - 1 + r.batches_before))
                dve.tensor_copy(id_f[:, 0:r.nt], bank[at][:, 0:r.nt]).then_inc(dve_step.sem, 1)
                dve.wait_ge(dve_step.sem, step.next())
                dve.tensor_tensor(ids[r][:, :], id_f[:, 0:r.nt], bank[at][:, r.nt:2 * r.nt], ALU.add)\
                    .then_inc(routed.sem, 1)

            def copied(r, i, j, turn):
                n = phase[r]
                dve.wait_ge(n.y_mm.sem, n.y_mm.after(i))
                dve.wait_ge(n.y_stored[j % 2].sem, n.y_stored[j % 2].sent(turn))
                dve.tensor_copy(y_s[j % 2][:, 512:1024], bank[5 + 2 * (j % 2)][:, :]).then_inc(n.half_ready.sem, 1)

            occupancy(GROUPS[0])
            occupancy(GROUPS[1])
            take_ranks(GROUPS[0], 0)
            places(GROUPS[0])
            take_ranks(GROUPS[1], 2)
            dve.wait_ge(x2_stored.sem, x2_stored.landed(M - 1))
            experts(GROUPS[0])
            table(GATE, 4)
            dve.wait_ge(routed.sem, routed.after(GATE.n))
            places(GROUPS[1])
            experts(GROUPS[1])
            for h in range(2):
                with dve.Fori(0, H // B // 2) as it:
                    step.enter(it, 2)
                    for half in range(2):
                        for j in range(4):
                            i = it * 8 + (h * H + half * 4 + j)
                            copied(GATE, i, j, it * 4 + (h * H // 2 + half * 2 + j // 2))
                            if j == 1:
                                one_hots(UP[h], it * 2 + half, half)
                step.leave(H // B // 2)
            close_table(UP[0], 1)
            dve.wait_ge(routed.sem, routed.after(UP[0].n))
            close_table(UP[1], 3)
            with dve.Fori(T // 2, GATE.nt // 2) as it:
                for j in range(2):
                    copied(GATE, it * 2 + j, j, it)

            def products_out(r):
                for b in range(2):
                    dve.wait_ge(phase[r].y_stored[b].sem, phase[r].y_stored[b].landed(r.nt // 2 - 1))

            products_out(GATE)
            with dve.Fori(0, UP[0].nt // 2) as it:
                for j in range(2):
                    copied(UP[0], it * 2 + j, j, it)
            products_out(UP[0])

            def inner_part(t, b, turn):
                dve.wait_ge(c_y0.sem, c_y0.after(t))
                gate_0, up_0 = in4[b][0], in4[b][2]
                dve.scalar_tensor_tensor(out=gate_0, in0=in4[b][1], scalar=comb["gate"][:, 1, ds(t, 1)], in1=gate_0,
                                         op0=ALU.mult, op1=ALU.add).then_inc(c_g.sem, 1)
                dve.wait_ge(c_z0.sem, c_z0.after(t))
                dve.scalar_tensor_tensor(out=up_0, in0=in4[b][3], scalar=comb["up"][:, 1, ds(t, 1)],
                                         in1=up_0, op0=ALU.mult, op1=ALU.add).then_inc(c_u.sem, 1)
                dve.wait_ge(c_u.sem, c_u.after(t))
                dve.wait_ge(c_h.sem, c_h.after(t))
                dve.wait_ge(c_t_mm.sem, c_t_mm.room(t))
                dve.wait_ge(c_stored[b].sem, c_stored[b].sent(turn))
                dve.tensor_tensor(inter[b], gate_0, up_0, ALU.mult).then_inc(c_done.sem, 1)

            def inner_top(t, first):
                dve.wait_ge(c_log_mm.sem, c_log_mm.after(t))
                dve.tensor_copy(lg[:, 0, 0, :], bank[first][:, 0:E]).then_inc(c_lg.sem, 1)
                dve.wait_ge(c_lg.sem, c_lg.after(t))
                alone(dve)
                pick_two(1, 1, lambda table, got, j: dve.tensor_copy(table[:, 2, :, ds(t, 1)],
                                                                    got[:, 0, 0, 0:2].unsqueeze(2)))

            def turned(r, i, j):
                n = phase[r]
                dve.wait_ge(n.xt_mm.sem, n.xt_mm.after(i))
                dve.wait_ge(n.y_mm.sem, n.y_mm.room(i))
                dve.tensor_copy(rows_t[j % 2][:, 512:1024], bank[2 * (j % 2) + 1][:, :]).then_inc(n.half_ready.sem, 1)

            def output_part(t, b, turn):
                dve.wait_ge(o_y0.sem, o_y0.after(t))
                dve.scalar_tensor_tensor(out=in2[b][0], in0=in2[b][1], scalar=comb["down"][:, 1, ds(t, 1)],
                                         in1=in2[b][0], op0=ALU.mult, op1=ALU.add).then_inc(o_sum.sem, 1)
                dve.wait_ge(o_sum.sem, o_sum.after(t))
                dve.wait_ge(o_stored[b].sem, o_stored[b].sent(turn))
                dve.tensor_tensor(out_s[b], in2[b][0], tile_of(t), ALU.add).then_inc(o_ready.sem, 1)

            def first_part(it, j, h):
                if j in FIRST_PARTS:
                    k = FIRST_PARTS.index(j)
                    inner_part(it * 4 + (h * H + k), k % 2, it * 2 + (h * H // 2 + k // 2))

            def second_part(it, j, h, first):
                if j in SECOND_PARTS:
                    inner_top(it * 4 + (h * H + SECOND_PARTS.index(j)), first)

            with dve.Fori(0, BODIES - 1) as it:
                step.enter(it, 3 * len(SECOND_PARTS))
                for j in range(BODY):
                    first_part(it, j, 0)
                    copied(UP[1], it * BODY + j, j, it * (BODY // 2) + j // 2)
                    second_part(it, j, 0, 1)
            step.leave(BODIES - 1)

            def route(r, first):
                occupancy(r.group)
                take_ranks(r.group, first)
                places(r.group)
                experts(r.group)
                table(r, first + 2)

            route(DOWN[0], 1)

            def down_body(it, tiles):
                for j in range(BODY):
                    if j < tiles:
                        turned(DOWN[0], it * BODY + j + 1, j + 1)
                    first_part(it, j, 1)
                    second_part(it, j, 1, 5)

            turned(DOWN[0], 0, 0)
            with dve.Fori(0, BODIES - 2) as it:
                step.enter(it, 3 * len(SECOND_PARTS))
                down_body(it, BODY)
            step.leave(BODIES - 2)
            down_body(BODIES - 2, BODY - 1)
            route(DOWN[1], 5)
            turned(DOWN[1], 0, 0)
            with dve.Fori(0, BODIES - 1) as it:
                for j in range(BODY):
                    turned(DOWN[1], it * BODY + j + 1, j + 1)
                    if j in SECOND_PARTS:
                        k = SECOND_PARTS.index(j)
                        output_part(it * 4 + k, k, it)
            for j in range(BODY - 1):
                turned(DOWN[1], DOWN[1].nt - BODY + j + 1, j + 1)
            with dve.Fori(0, H // 4) as it:
                for b in range(4):
                    output_part(it * 4 + (H + b), b, it + H // 4)


def buckets_of_pairs():
    n = np.arange(G)[None, :] - np.arange(G)[:, None]
    half = BUCKETS // 2
    exact = half // 2
    size = np.abs(n)
    ratio = np.log(np.maximum(size, 1).astype(np.float32) / np.float32(exact)) / np.float32(np.log(128 / exact))
    large = np.minimum(exact + (ratio * np.float32(half - exact)).astype(np.int32), half - 1)
    bucket = np.where(n < 0, half, 0) + np.where(size < exact, size, large)
    return np.concatenate([bucket, bucket]).astype(np.float32)


def kernel(**inputs):
    import concourse.bacc as bacc
    from concourse.bass_utils import run_bass_kernel_spmd

    a = {k: np.asarray(v) for k, v in inputs.items()}
    c = np.ascontiguousarray

    def columns(v, k):
        return c(v.reshape(k, P).T)

    def experts_in(w, kc):
        n_out = w.shape[1]
        return c(w.transpose(2, 0, 1).reshape(kc, P, E, n_out).transpose(1, 2, 0, 3).reshape(P, -1))

    arrays = {
        "x": a["L0_attn_x"].reshape(TOK, D), "ln_g": columns(a["L0_attn_ln_g"], KD),
        "ln_b": columns(a["L0_attn_ln_b"], KD), "w_h": a["L0_attn_W_h"], "bh_value": a["L0_attn_b_h"][:HID],
        "bh_gate": columns(a["L0_attn_b_h"][HID:], KH), "w_qk": a["L0_attn_W_qk"],
        "b_qk": columns(a["L0_attn_b_qk"], 1), "os_gamma": a["L0_attn_os_gamma"].T,
        "os_beta": a["L0_attn_os_beta"].T, "rel_emb": a["L0_attn_rel_emb"].reshape(-1), "w_out": a["L0_attn_W_out"],
        "b_out": a["L0_attn_b_out"], "r_gate": a["L0_ffn_router_gate"].T,
        "w_gate": experts_in(a["L0_ffn_w_gate"], KD), "r_up": a["L0_ffn_router_up"].T,
        "w_up": experts_in(a["L0_ffn_w_up"], KD), "r_down": a["L0_ffn_router_down"].T,
        "w_down": experts_in(a["L0_ffn_w_down"], KI), "buckets": buckets_of_pairs(),
    }
    arrays = {f"in_{k}": c(v) for k, v in arrays.items()}
    nc = bacc.Bacc("TRN2", target_bir_lowering=False, num_devices=1)
    args = [nc.dram_tensor(k, v.shape, mybir.dt.from_np(v.dtype), kind="ExternalInput").ap()
            for k, v in arrays.items()]
    out = nc.dram_tensor("out", (TOK, D), F32, kind="ExternalOutput").ap()
    block_kernel(nc, *args, out)
    r = run_bass_kernel_spmd(nc, [arrays], core_ids=[0])
    return r.results[0]["out"].reshape(1, TOK, D)
```
